# Optimizing a Trainium2 kernel written in Bass

```python
import numpy as np
import jax
import jax.numpy as jnp

def _softmax(x, axis=-1):
    return jax.nn.softmax(x, axis=axis)

def _gelu(x):
    return jax.nn.gelu(x, approximate=True)

def _silu(x):
    return jax.nn.silu(x)

def _sigmoid(x):
    return jax.nn.sigmoid(x)

def _layernorm(x, axis=-1, eps=1e-05):
    m = jnp.mean(x, axis=axis, keepdims=True)
    v = jnp.var(x, axis=axis, keepdims=True)
    return (x - m) / jnp.sqrt(v + eps)

def _scatter_add(tgt, idx, src, axis=0):
    return tgt.at[idx].add(src)

def _segment_sum(src, seg, n):
    return jax.ops.segment_sum(src, seg, n)
kernel_name = 'mk_adaln_attn_ffn_d2_seqx_r8_2ad019'

def setup_inputs(seed: int=0):
    np.random.seed(seed)
    _w = jnp.asarray

    def _rec_inputs():
        import jax
        import jax.numpy as jnp
        _rk = jax.random.key(seed)
        x = -0.000125 + 0.9999 * jax.random.normal(jax.random.fold_in(_rk, 1), (4, 256, 256), jnp.float32)
        _lenS = 256 - jax.random.randint(jax.random.fold_in(_rk, 7), (4,), 0, max(1, 256 // 4) + 1, jnp.int32)
        _lenS2 = 256 - jax.random.randint(jax.random.fold_in(_rk, 8), (4,), 0, max(1, 256 // 4) + 1, jnp.int32)
        fside_BxSxS_0 = -1.52775e-05 + 0.999936 * jax.random.normal(jax.random.fold_in(_rk, 11), (4, 256, 256), jnp.float32)
        cond_512 = -5.03954e-05 + 1.00559 * jax.random.normal(jax.random.fold_in(_rk, 12), (4, 64), jnp.float32)
        return (x, fside_BxSxS_0, cond_512)
    x, fside_BxSxS_0, cond_512 = _rec_inputs()

    def _L0_cond_setup():
        import jax, jax.numpy as jnp
        from jax import lax
        import numpy as np
        B, T, C, TD = (8, 256, 256, 64)

        def _bi_wkv(r, k, v, w, u, time_emb):
            tf = jax.nn.sigmoid(jnp.sum(time_emb, axis=-1))[:, None, None]
            decay = jnp.exp(-jnp.exp(w.astype(jnp.float32)))[None, :] * (0.5 + 0.5 * tf[:, :, 0])
            kf = k.astype(jnp.float32)
            vf = v.astype(jnp.float32)
            ek = jnp.exp(jnp.minimum(kf, 30.0))
            ekv = ek * vf

            def step(carry, x):
                a, b = carry
                ekv_t, ek_t = x
                a = a * decay + ekv_t
                b = b * decay + ek_t
                return ((a, b), (a, b))
            ekv_t = jnp.swapaxes(ekv, 0, 1)
            ek_t = jnp.swapaxes(ek, 0, 1)
            init = (jnp.zeros_like(decay), jnp.zeros_like(decay))
            _, (nf, df) = lax.scan(step, init, (ekv_t, ek_t))
            _, (nb, db) = lax.scan(step, init, (ekv_t, ek_t), reverse=True)
            nf = jnp.swapaxes(nf, 0, 1)
            df = jnp.swapaxes(df, 0, 1)
            nb = jnp.swapaxes(nb, 0, 1)
            db = jnp.swapaxes(db, 0, 1)
            euk = jnp.exp(jnp.minimum(u.astype(jnp.float32)[None, None, :] + kf, 30.0))
            num = nf + nb - ekv + euk * vf
            den = df + db - ek + euk
            base = jax.nn.sigmoid(r.astype(jnp.float32)) * (num / jnp.maximum(den, 1e-08))
            out = base * (0.8 + 0.2 * tf)
            return out.astype(r.dtype)
        key = jax.random.key(seed)
        ks = jax.random.split(key, 6)
        return {'r': jax.random.normal(ks[0], (B, T, C), dtype=jnp.float32), 'k': jax.random.normal(ks[1], (B, T, C), dtype=jnp.float32), 'v': jax.random.normal(ks[2], (B, T, C), dtype=jnp.float32), 'w': jax.random.normal(ks[3], (C,), dtype=jnp.float32), 'u': jax.random.normal(ks[4], (C,), dtype=jnp.float32), 'time_emb': jax.random.normal(ks[5], (B, TD), dtype=jnp.float32)}
    _L0_cond_all = _L0_cond_setup()
    _L0_cond_in = {k: v for k, v in _L0_cond_all.items() if k in ('w', 'u')}
    del _L0_cond_all

    def _L0_attn_setup():
        import jax, jax.numpy as jnp
        import numpy as np
        B, T, HID = (1, 128, 256)
        H, DK, DV, M, KW = (16, 128, 128, 128, 4)
        SCALE = DK ** (-0.5)
        EPS = 1e-05

        def short_conv(x, w):
            K = w.shape[1]
            xp = jnp.pad(x, ((0, 0), (K - 1, 0), (0, 0)))
            t = x.shape[1]
            y = sum((xp[:, i:i + t] * w[:, i] for i in range(K)))
            return jax.nn.silu(y)

        def l2norm(x):
            return x * jax.lax.rsqrt(jnp.sum(x * x, axis=-1, keepdims=True) + 1e-06)

        def gsa2_scan(q, k, v, w, g, beta):
            b = q.shape[0]
            tm = lambda x: jnp.moveaxis(x, 1, 0)
            Sk0 = jnp.zeros((b, H, DK, M), q.dtype)
            Sv0 = jnp.zeros((b, H, M, DV), q.dtype)

            def step(carry, xs):
                Sk, Sv = carry
                q_t, k_t, v_t, w_t, g_t, b_t = xs
                gt = jnp.exp(g_t)
                bw = b_t[:, :, None] * w_t
                Sk = Sk * gt[:, :, None, :] + k_t[..., :, None] * bw[:, :, None, :]
                Sv = Sv * gt[..., None] + bw[..., None] * v_t[:, :, None, :]
                s = jnp.einsum('bhd,bhdm->bhm', q_t, Sk) * SCALE
                a = jax.nn.softmax(s, axis=-1)
                o_t = jnp.einsum('bhm,bhmd->bhd', a, Sv)
                return ((Sk, Sv), o_t)
            (_, _), o = jax.lax.scan(step, (Sk0, Sv0), (tm(q), tm(k), tm(v), tm(w), tm(g), tm(beta)))
            return jnp.moveaxis(o, 0, 1)
        key = jax.random.key(seed)
        ks = jax.random.split(key, 16)
        s = 0.02
        return {'hidden_states': jax.random.normal(ks[0], (B, T, HID), jnp.float32), 'Wq': jax.random.normal(ks[1], (HID, H * DK), jnp.float32) * s, 'Wk': jax.random.normal(ks[2], (HID, H * DK), jnp.float32) * s, 'Wv': jax.random.normal(ks[3], (HID, H * DV), jnp.float32) * s, 'Ww': jax.random.normal(ks[4], (HID, H * M), jnp.float32) * s, 'cq': jax.random.normal(ks[5], (H * DK, KW), jnp.float32) * 0.2, 'ck': jax.random.normal(ks[6], (H * DK, KW), jnp.float32) * 0.2, 'cv': jax.random.normal(ks[7], (H * DV, KW), jnp.float32) * 0.2, 'Wf1': jax.random.normal(ks[8], (HID, DV), jnp.float32) * s, 'Wf2': jax.random.normal(ks[9], (DV, H * M), jnp.float32) * s, 'Wb': jax.random.normal(ks[10], (HID, H), jnp.float32) * s, 'Wg1': jax.random.normal(ks[11], (HID, DV), jnp.float32) * s, 'Wg2': jax.random.normal(ks[12], (DV, H * DV), jnp.float32) * s, 'bg2': jnp.zeros((H * DV,), jnp.float32), 'norm_w': jnp.ones((DV,), jnp.float32), 'Wo': jax.random.normal(ks[13], (H * DV, HID), jnp.float32) * s}
    _L0_attn_all = _L0_attn_setup()
    _L0_attn_in = {k: v for k, v in _L0_attn_all.items() if k in ('Wq', 'Wk', 'Wv', 'Ww', 'cq', 'ck', 'cv', 'Wf1', 'Wf2', 'Wb', 'Wg1', 'Wg2', 'bg2', 'norm_w', 'Wo')}
    del _L0_attn_all

    def _L0_cond2_setup():
        import jax, jax.numpy as jnp
        from jax import lax
        import numpy as np
        B, T, C, TD = (8, 256, 256, 64)

        def _bi_wkv(r, k, v, w, u, time_emb):
            tf = jax.nn.sigmoid(jnp.sum(time_emb, axis=-1))[:, None, None]
            decay = jnp.exp(-jnp.exp(w.astype(jnp.float32)))[None, :] * (0.5 + 0.5 * tf[:, :, 0])
            kf = k.astype(jnp.float32)
            vf = v.astype(jnp.float32)
            ek = jnp.exp(jnp.minimum(kf, 30.0))
            ekv = ek * vf

            def step(carry, x):
                a, b = carry
                ekv_t, ek_t = x
                a = a * decay + ekv_t
                b = b * decay + ek_t
                return ((a, b), (a, b))
            ekv_t = jnp.swapaxes(ekv, 0, 1)
            ek_t = jnp.swapaxes(ek, 0, 1)
            init = (jnp.zeros_like(decay), jnp.zeros_like(decay))
            _, (nf, df) = lax.scan(step, init, (ekv_t, ek_t))
            _, (nb, db) = lax.scan(step, init, (ekv_t, ek_t), reverse=True)
            nf = jnp.swapaxes(nf, 0, 1)
            df = jnp.swapaxes(df, 0, 1)
            nb = jnp.swapaxes(nb, 0, 1)
            db = jnp.swapaxes(db, 0, 1)
            euk = jnp.exp(jnp.minimum(u.astype(jnp.float32)[None, None, :] + kf, 30.0))
            num = nf + nb - ekv + euk * vf
            den = df + db - ek + euk
            base = jax.nn.sigmoid(r.astype(jnp.float32)) * (num / jnp.maximum(den, 1e-08))
            out = base * (0.8 + 0.2 * tf)
            return out.astype(r.dtype)
        key = jax.random.key(seed)
        ks = jax.random.split(key, 6)
        return {'r': jax.random.normal(ks[0], (B, T, C), dtype=jnp.float32), 'k': jax.random.normal(ks[1], (B, T, C), dtype=jnp.float32), 'v': jax.random.normal(ks[2], (B, T, C), dtype=jnp.float32), 'w': jax.random.normal(ks[3], (C,), dtype=jnp.float32), 'u': jax.random.normal(ks[4], (C,), dtype=jnp.float32), 'time_emb': jax.random.normal(ks[5], (B, TD), dtype=jnp.float32)}
    _L0_cond2_all = _L0_cond2_setup()
    _L0_cond2_in = {k: v for k, v in _L0_cond2_all.items() if k in ('w', 'u')}
    del _L0_cond2_all

    def _L0_ffn_setup():
        import jax, jax.numpy as jnp
        import numpy as np
        B, S, H, I, E = (2, 64, 256, 512, 8)
        JITTER_EPS = 0.01
        NEG_INF = float('-inf')

        def _route(logits):
            max1 = jnp.max(logits, axis=-1, keepdims=True)
            ind1 = jnp.argmax(logits, axis=-1, keepdims=True)
            factor1 = jnp.maximum(jnp.abs(logits), max1)
            mask1 = (max1 - logits) / factor1 > 2.0 * JITTER_EPS
            gates1 = jax.nn.softmax(jnp.where(mask1, NEG_INF, logits), axis=-1)
            mult1 = jnp.take_along_axis(gates1, ind1, axis=-1)
            sel1_onehot = jax.nn.one_hot(ind1[..., 0], E, dtype=jnp.bool_)
            masked_scores = jnp.where(sel1_onehot, NEG_INF, logits)
            max2 = jnp.max(masked_scores, axis=-1, keepdims=True)
            ind2 = jnp.argmax(masked_scores, axis=-1, keepdims=True)
            factor2 = jnp.maximum(jnp.abs(logits), max2)
            mask2 = (max2 - masked_scores) / factor2 > 2.0 * JITTER_EPS
            gates2 = jax.nn.softmax(jnp.where(mask2, NEG_INF, masked_scores), axis=-1)
            mult2 = jnp.take_along_axis(gates2, ind2, axis=-1)
            return (jnp.concatenate([mult1, mult2], axis=-1), jnp.concatenate([ind1, ind2], axis=-1))
        key = jax.random.key(seed)
        ks = jax.random.split(key, 5)
        std = 0.02
        return {'hidden_states': jax.random.normal(ks[0], (B, S, H), jnp.float32), 'gate_w': jax.random.normal(ks[1], (E, H), jnp.float32) * std, 'w1': jax.random.normal(ks[2], (E, I, H), jnp.float32) * std, 'w2': jax.random.normal(ks[3], (E, H, I), jnp.float32) * std, 'w3': jax.random.normal(ks[4], (E, I, H), jnp.float32) * std}
    _L0_ffn_all = _L0_ffn_setup()
    _L0_ffn_in = {k: v for k, v in _L0_ffn_all.items() if k in ('gate_w', 'w1', 'w2', 'w3')}
    del _L0_ffn_all

    def _L1_cond_setup():
        import jax, jax.numpy as jnp
        from jax import lax
        import numpy as np
        B, T, C, TD = (8, 256, 256, 64)

        def _bi_wkv(r, k, v, w, u, time_emb):
            tf = jax.nn.sigmoid(jnp.sum(time_emb, axis=-1))[:, None, None]
            decay = jnp.exp(-jnp.exp(w.astype(jnp.float32)))[None, :] * (0.5 + 0.5 * tf[:, :, 0])
            kf = k.astype(jnp.float32)
            vf = v.astype(jnp.float32)
            ek = jnp.exp(jnp.minimum(kf, 30.0))
            ekv = ek * vf

            def step(carry, x):
                a, b = carry
                ekv_t, ek_t = x
                a = a * decay + ekv_t
                b = b * decay + ek_t
                return ((a, b), (a, b))
            ekv_t = jnp.swapaxes(ekv, 0, 1)
            ek_t = jnp.swapaxes(ek, 0, 1)
            init = (jnp.zeros_like(decay), jnp.zeros_like(decay))
            _, (nf, df) = lax.scan(step, init, (ekv_t, ek_t))
            _, (nb, db) = lax.scan(step, init, (ekv_t, ek_t), reverse=True)
            nf = jnp.swapaxes(nf, 0, 1)
            df = jnp.swapaxes(df, 0, 1)
            nb = jnp.swapaxes(nb, 0, 1)
            db = jnp.swapaxes(db, 0, 1)
            euk = jnp.exp(jnp.minimum(u.astype(jnp.float32)[None, None, :] + kf, 30.0))
            num = nf + nb - ekv + euk * vf
            den = df + db - ek + euk
            base = jax.nn.sigmoid(r.astype(jnp.float32)) * (num / jnp.maximum(den, 1e-08))
            out = base * (0.8 + 0.2 * tf)
            return out.astype(r.dtype)
        key = jax.random.key(seed)
        ks = jax.random.split(key, 6)
        return {'r': jax.random.normal(ks[0], (B, T, C), dtype=jnp.float32), 'k': jax.random.normal(ks[1], (B, T, C), dtype=jnp.float32), 'v': jax.random.normal(ks[2], (B, T, C), dtype=jnp.float32), 'w': jax.random.normal(ks[3], (C,), dtype=jnp.float32), 'u': jax.random.normal(ks[4], (C,), dtype=jnp.float32), 'time_emb': jax.random.normal(ks[5], (B, TD), dtype=jnp.float32)}
    _L1_cond_all = _L1_cond_setup()
    _L1_cond_in = {k: v for k, v in _L1_cond_all.items() if k in ('w', 'u')}
    del _L1_cond_all

    def _L1_attn_setup():
        import jax, jax.numpy as jnp
        import numpy as np
        B, T, D = (2, 256, 256)
        QH, KVH = (16, 4)
        HD = D // QH

        def rotate_half(x):
            d = x.shape[-1] // 2
            return jnp.concatenate([-x[..., d:], x[..., :d]], axis=-1)

        def rope_tables(head_dim, seq_len, theta=10000.0):
            freqs = 1.0 / theta ** (jnp.arange(0, head_dim, 2, dtype=jnp.float32) / head_dim)
            t = jnp.arange(seq_len, dtype=jnp.float32)
            ang = t[:, None] * freqs[None, :]
            cos = jnp.tile(jnp.cos(ang), (1, 2))
            sin = jnp.tile(jnp.sin(ang), (1, 2))
            return (cos, sin)

        def apply_rope(x, cos, sin):
            c = cos[None, None, :, :]
            s = sin[None, None, :, :]
            return x * c + rotate_half(x) * s
        key = jax.random.key(seed)
        kx, kq, kk, kv, ko = jax.random.split(key, 5)
        scale = D ** (-0.5)
        return {'x': jax.random.normal(kx, (B, T, D), dtype=jnp.float32), 'wq': jax.random.normal(kq, (D, D), dtype=jnp.float32) * scale, 'wk': jax.random.normal(kk, (D, KVH * HD), dtype=jnp.float32) * scale, 'wv': jax.random.normal(kv, (D, KVH * HD), dtype=jnp.float32) * scale, 'wo': jax.random.normal(ko, (D, D), dtype=jnp.float32) * scale}
    _L1_attn_all = _L1_attn_setup()
    _L1_attn_in = {k: v for k, v in _L1_attn_all.items() if k in ('wq', 'wk', 'wv', 'wo')}
    del _L1_attn_all

    def _L1_cond2_setup():
        import jax, jax.numpy as jnp
        from jax import lax
        import numpy as np
        B, T, C, TD = (8, 256, 256, 64)

        def _bi_wkv(r, k, v, w, u, time_emb):
            tf = jax.nn.sigmoid(jnp.sum(time_emb, axis=-1))[:, None, None]
            decay = jnp.exp(-jnp.exp(w.astype(jnp.float32)))[None, :] * (0.5 + 0.5 * tf[:, :, 0])
            kf = k.astype(jnp.float32)
            vf = v.astype(jnp.float32)
            ek = jnp.exp(jnp.minimum(kf, 30.0))
            ekv = ek * vf

            def step(carry, x):
                a, b = carry
                ekv_t, ek_t = x
                a = a * decay + ekv_t
                b = b * decay + ek_t
                return ((a, b), (a, b))
            ekv_t = jnp.swapaxes(ekv, 0, 1)
            ek_t = jnp.swapaxes(ek, 0, 1)
            init = (jnp.zeros_like(decay), jnp.zeros_like(decay))
            _, (nf, df) = lax.scan(step, init, (ekv_t, ek_t))
            _, (nb, db) = lax.scan(step, init, (ekv_t, ek_t), reverse=True)
            nf = jnp.swapaxes(nf, 0, 1)
            df = jnp.swapaxes(df, 0, 1)
            nb = jnp.swapaxes(nb, 0, 1)
            db = jnp.swapaxes(db, 0, 1)
            euk = jnp.exp(jnp.minimum(u.astype(jnp.float32)[None, None, :] + kf, 30.0))
            num = nf + nb - ekv + euk * vf
            den = df + db - ek + euk
            base = jax.nn.sigmoid(r.astype(jnp.float32)) * (num / jnp.maximum(den, 1e-08))
            out = base * (0.8 + 0.2 * tf)
            return out.astype(r.dtype)
        key = jax.random.key(seed)
        ks = jax.random.split(key, 6)
        return {'r': jax.random.normal(ks[0], (B, T, C), dtype=jnp.float32), 'k': jax.random.normal(ks[1], (B, T, C), dtype=jnp.float32), 'v': jax.random.normal(ks[2], (B, T, C), dtype=jnp.float32), 'w': jax.random.normal(ks[3], (C,), dtype=jnp.float32), 'u': jax.random.normal(ks[4], (C,), dtype=jnp.float32), 'time_emb': jax.random.normal(ks[5], (B, TD), dtype=jnp.float32)}
    _L1_cond2_all = _L1_cond2_setup()
    _L1_cond2_in = {k: v for k, v in _L1_cond2_all.items() if k in ('w', 'u')}
    del _L1_cond2_all

    def _L1_ffn_setup():
        import jax, jax.numpy as jnp
        import numpy as np
        import math
        B, S, D = (2, 128, 256)
        H, KVH, HD = (16, 4, 128)
        E, K, FF = (8, 2, 896)
        EPS = 1e-05
        ROPE_BASE = 1000000.0

        def rmsnorm(x, w, eps=EPS):
            xf = x.astype(jnp.float32)
            var = jnp.mean(xf * xf, axis=-1, keepdims=True)
            return (xf * jax.lax.rsqrt(var + eps)).astype(x.dtype) * w

        def apply_rope(x, cos, sin):
            x1 = x[..., 0::2]
            x2 = x[..., 1::2]
            r1 = x1 * cos - x2 * sin
            r2 = x1 * sin + x2 * cos
            return jnp.stack([r1, r2], axis=-1).reshape(x.shape)
        key = jax.random.key(seed)
        ks = jax.random.split(key, 12)
        sc = 0.02
        inp = {'x': jax.random.normal(ks[0], (B, S, D), jnp.float32), 'ln_w': jnp.ones((D,), jnp.float32), 'ff_ln_w': jnp.ones((D,), jnp.float32), 'wq': jax.random.normal(ks[1], (D, H * HD), jnp.float32) * sc, 'wk': jax.random.normal(ks[2], (D, KVH * HD), jnp.float32) * sc, 'wv': jax.random.normal(ks[3], (D, KVH * HD), jnp.float32) * sc, 'wo': jax.random.normal(ks[4], (H * HD, D), jnp.float32) * sc, 'gate_w': jax.random.normal(ks[5], (D, E), jnp.float32) * sc, 'w1': jax.random.normal(ks[6], (E, D, FF), jnp.float32) * sc, 'w3': jax.random.normal(ks[7], (E, D, FF), jnp.float32) * sc, 'w2': jax.random.normal(ks[8], (E, FF, D), jnp.float32) * sc}
        return inp
    _L1_ffn_all = _L1_ffn_setup()
    _L1_ffn_in = {k: v for k, v in _L1_ffn_all.items() if k in ('ln_w', 'ff_ln_w', 'wq', 'wk', 'wv', 'wo', 'gate_w', 'w1', 'w3', 'w2')}
    del _L1_ffn_all
    return {'x': x, 'fside_BxSxS_0': fside_BxSxS_0, 'cond_512': cond_512, 'L0_cond_w': _L0_cond_in['w'], 'L0_cond_u': _L0_cond_in['u'], 'L0_attn_Wq': _L0_attn_in['Wq'], 'L0_attn_Wk': _L0_attn_in['Wk'], 'L0_attn_Wv': _L0_attn_in['Wv'], 'L0_attn_Ww': _L0_attn_in['Ww'], 'L0_attn_cq': _L0_attn_in['cq'], 'L0_attn_ck': _L0_attn_in['ck'], 'L0_attn_cv': _L0_attn_in['cv'], 'L0_attn_Wf1': _L0_attn_in['Wf1'], 'L0_attn_Wf2': _L0_attn_in['Wf2'], 'L0_attn_Wb': _L0_attn_in['Wb'], 'L0_attn_Wg1': _L0_attn_in['Wg1'], 'L0_attn_Wg2': _L0_attn_in['Wg2'], 'L0_attn_bg2': _L0_attn_in['bg2'], 'L0_attn_norm_w': _L0_attn_in['norm_w'], 'L0_attn_Wo': _L0_attn_in['Wo'], 'L0_cond2_w': _L0_cond2_in['w'], 'L0_cond2_u': _L0_cond2_in['u'], 'L0_ffn_gate_w': _L0_ffn_in['gate_w'], 'L0_ffn_w1': _L0_ffn_in['w1'], 'L0_ffn_w2': _L0_ffn_in['w2'], 'L0_ffn_w3': _L0_ffn_in['w3'], 'L1_cond_w': _L1_cond_in['w'], 'L1_cond_u': _L1_cond_in['u'], 'L1_attn_wq': _L1_attn_in['wq'], 'L1_attn_wk': _L1_attn_in['wk'], 'L1_attn_wv': _L1_attn_in['wv'], 'L1_attn_wo': _L1_attn_in['wo'], 'L1_cond2_w': _L1_cond2_in['w'], 'L1_cond2_u': _L1_cond2_in['u'], 'L1_ffn_ln_w': _L1_ffn_in['ln_w'], 'L1_ffn_ff_ln_w': _L1_ffn_in['ff_ln_w'], 'L1_ffn_wq': _L1_ffn_in['wq'], 'L1_ffn_wk': _L1_ffn_in['wk'], 'L1_ffn_wv': _L1_ffn_in['wv'], 'L1_ffn_wo': _L1_ffn_in['wo'], 'L1_ffn_gate_w': _L1_ffn_in['gate_w'], 'L1_ffn_w1': _L1_ffn_in['w1'], 'L1_ffn_w3': _L1_ffn_in['w3'], 'L1_ffn_w2': _L1_ffn_in['w2']}

def reference(x, fside_BxSxS_0, cond_512, L0_cond_w, L0_cond_u, L0_attn_Wq, L0_attn_Wk, L0_attn_Wv, L0_attn_Ww, L0_attn_cq, L0_attn_ck, L0_attn_cv, L0_attn_Wf1, L0_attn_Wf2, L0_attn_Wb, L0_attn_Wg1, L0_attn_Wg2, L0_attn_bg2, L0_attn_norm_w, L0_attn_Wo, L0_cond2_w, L0_cond2_u, L0_ffn_gate_w, L0_ffn_w1, L0_ffn_w2, L0_ffn_w3, L1_cond_w, L1_cond_u, L1_attn_wq, L1_attn_wk, L1_attn_wv, L1_attn_wo, L1_cond2_w, L1_cond2_u, L1_ffn_ln_w, L1_ffn_ff_ln_w, L1_ffn_wq, L1_ffn_wk, L1_ffn_wv, L1_ffn_wo, L1_ffn_gate_w, L1_ffn_w1, L1_ffn_w3, L1_ffn_w2):
    import jax
    import jax.numpy as jnp

    def _L0_cond_ref(r, k, v, w, u, time_emb):
        import jax, jax.numpy as jnp
        from jax import lax
        import numpy as np
        B, T, C, TD = (8, 256, 256, 64)

        def _bi_wkv(r, k, v, w, u, time_emb):
            tf = jax.nn.sigmoid(jnp.sum(time_emb, axis=-1))[:, None, None]
            decay = jnp.exp(-jnp.exp(w.astype(jnp.float32)))[None, :] * (0.5 + 0.5 * tf[:, :, 0])
            kf = k.astype(jnp.float32)
            vf = v.astype(jnp.float32)
            ek = jnp.exp(jnp.minimum(kf, 30.0))
            ekv = ek * vf

            def step(carry, x):
                a, b = carry
                ekv_t, ek_t = x
                a = a * decay + ekv_t
                b = b * decay + ek_t
                return ((a, b), (a, b))
            ekv_t = jnp.swapaxes(ekv, 0, 1)
            ek_t = jnp.swapaxes(ek, 0, 1)
            init = (jnp.zeros_like(decay), jnp.zeros_like(decay))
            _, (nf, df) = lax.scan(step, init, (ekv_t, ek_t))
            _, (nb, db) = lax.scan(step, init, (ekv_t, ek_t), reverse=True)
            nf = jnp.swapaxes(nf, 0, 1)
            df = jnp.swapaxes(df, 0, 1)
            nb = jnp.swapaxes(nb, 0, 1)
            db = jnp.swapaxes(db, 0, 1)
            euk = jnp.exp(jnp.minimum(u.astype(jnp.float32)[None, None, :] + kf, 30.0))
            num = nf + nb - ekv + euk * vf
            den = df + db - ek + euk
            base = jax.nn.sigmoid(r.astype(jnp.float32)) * (num / jnp.maximum(den, 1e-08))
            out = base * (0.8 + 0.2 * tf)
            return out.astype(r.dtype)
        return _bi_wkv(r, k, v, w, u, time_emb)

    def _L0_attn_ref(hidden_states, Wq, Wk, Wv, Ww, cq, ck, cv, Wf1, Wf2, Wb, Wg1, Wg2, bg2, norm_w, Wo):
        import jax, jax.numpy as jnp
        import numpy as np
        B, T, HID = (1, 128, 256)
        H, DK, DV, M, KW = (16, 128, 128, 128, 4)
        SCALE = DK ** (-0.5)
        EPS = 1e-05

        def short_conv(x, w):
            K = w.shape[1]
            xp = jnp.pad(x, ((0, 0), (K - 1, 0), (0, 0)))
            t = x.shape[1]
            y = sum((xp[:, i:i + t] * w[:, i] for i in range(K)))
            return jax.nn.silu(y)

        def l2norm(x):
            return x * jax.lax.rsqrt(jnp.sum(x * x, axis=-1, keepdims=True) + 1e-06)

        def gsa2_scan(q, k, v, w, g, beta):
            b = q.shape[0]
            tm = lambda x: jnp.moveaxis(x, 1, 0)
            Sk0 = jnp.zeros((b, H, DK, M), q.dtype)
            Sv0 = jnp.zeros((b, H, M, DV), q.dtype)

            def step(carry, xs):
                Sk, Sv = carry
                q_t, k_t, v_t, w_t, g_t, b_t = xs
                gt = jnp.exp(g_t)
                bw = b_t[:, :, None] * w_t
                Sk = Sk * gt[:, :, None, :] + k_t[..., :, None] * bw[:, :, None, :]
                Sv = Sv * gt[..., None] + bw[..., None] * v_t[:, :, None, :]
                s = jnp.einsum('bhd,bhdm->bhm', q_t, Sk) * SCALE
                a = jax.nn.softmax(s, axis=-1)
                o_t = jnp.einsum('bhm,bhmd->bhd', a, Sv)
                return ((Sk, Sv), o_t)
            (_, _), o = jax.lax.scan(step, (Sk0, Sv0), (tm(q), tm(k), tm(v), tm(w), tm(g), tm(beta)))
            return jnp.moveaxis(o, 0, 1)
        h = hidden_states
        q = short_conv(h @ Wq, cq)
        k = short_conv(h @ Wk, ck)
        v = short_conv(h @ Wv, cv)
        w = short_conv(h @ Ww, cv)
        g = jax.nn.log_sigmoid(h @ Wf1 @ Wf2)
        beta = jax.nn.sigmoid(h @ Wb)
        rs = lambda x, d: x.reshape(x.shape[0], x.shape[1], -1, d)
        q, k = (rs(q, DK), rs(k, DK))
        v = rs(v, DV)
        w = l2norm(rs(w, M))
        g = rs(g, M)
        o = gsa2_scan(q, k, v, w, g, beta)
        gate = rs(h @ Wg1 @ Wg2 + bg2, DV)
        o = o * jax.lax.rsqrt(jnp.mean(o * o, axis=-1, keepdims=True) + EPS)
        o = o * norm_w * jax.nn.sigmoid(gate)
        o = o.reshape(o.shape[0], o.shape[1], -1)
        return o @ Wo

    def _L0_cond2_ref(r, k, v, w, u, time_emb):
        import jax, jax.numpy as jnp
        from jax import lax
        import numpy as np
        B, T, C, TD = (8, 256, 256, 64)

        def _bi_wkv(r, k, v, w, u, time_emb):
            tf = jax.nn.sigmoid(jnp.sum(time_emb, axis=-1))[:, None, None]
            decay = jnp.exp(-jnp.exp(w.astype(jnp.float32)))[None, :] * (0.5 + 0.5 * tf[:, :, 0])
            kf = k.astype(jnp.float32)
            vf = v.astype(jnp.float32)
            ek = jnp.exp(jnp.minimum(kf, 30.0))
            ekv = ek * vf

            def step(carry, x):
                a, b = carry
                ekv_t, ek_t = x
                a = a * decay + ekv_t
                b = b * decay + ek_t
                return ((a, b), (a, b))
            ekv_t = jnp.swapaxes(ekv, 0, 1)
            ek_t = jnp.swapaxes(ek, 0, 1)
            init = (jnp.zeros_like(decay), jnp.zeros_like(decay))
            _, (nf, df) = lax.scan(step, init, (ekv_t, ek_t))
            _, (nb, db) = lax.scan(step, init, (ekv_t, ek_t), reverse=True)
            nf = jnp.swapaxes(nf, 0, 1)
            df = jnp.swapaxes(df, 0, 1)
            nb = jnp.swapaxes(nb, 0, 1)
            db = jnp.swapaxes(db, 0, 1)
            euk = jnp.exp(jnp.minimum(u.astype(jnp.float32)[None, None, :] + kf, 30.0))
            num = nf + nb - ekv + euk * vf
            den = df + db - ek + euk
            base = jax.nn.sigmoid(r.astype(jnp.float32)) * (num / jnp.maximum(den, 1e-08))
            out = base * (0.8 + 0.2 * tf)
            return out.astype(r.dtype)
        return _bi_wkv(r, k, v, w, u, time_emb)

    def _L0_ffn_ref(hidden_states, gate_w, w1, w2, w3):
        import jax, jax.numpy as jnp
        import numpy as np
        B, S, H, I, E = (2, 64, 256, 512, 8)
        JITTER_EPS = 0.01
        NEG_INF = float('-inf')

        def _route(logits):
            max1 = jnp.max(logits, axis=-1, keepdims=True)
            ind1 = jnp.argmax(logits, axis=-1, keepdims=True)
            factor1 = jnp.maximum(jnp.abs(logits), max1)
            mask1 = (max1 - logits) / factor1 > 2.0 * JITTER_EPS
            gates1 = jax.nn.softmax(jnp.where(mask1, NEG_INF, logits), axis=-1)
            mult1 = jnp.take_along_axis(gates1, ind1, axis=-1)
            sel1_onehot = jax.nn.one_hot(ind1[..., 0], E, dtype=jnp.bool_)
            masked_scores = jnp.where(sel1_onehot, NEG_INF, logits)
            max2 = jnp.max(masked_scores, axis=-1, keepdims=True)
            ind2 = jnp.argmax(masked_scores, axis=-1, keepdims=True)
            factor2 = jnp.maximum(jnp.abs(logits), max2)
            mask2 = (max2 - masked_scores) / factor2 > 2.0 * JITTER_EPS
            gates2 = jax.nn.softmax(jnp.where(mask2, NEG_INF, masked_scores), axis=-1)
            mult2 = jnp.take_along_axis(gates2, ind2, axis=-1)
            return (jnp.concatenate([mult1, mult2], axis=-1), jnp.concatenate([ind1, ind2], axis=-1))
        b, s, h = hidden_states.shape
        x = hidden_states.reshape(-1, h)
        logits = x @ gate_w.T
        mult, sel = _route(logits)
        combine = jnp.einsum('tk,tke->te', mult, jax.nn.one_hot(sel, E, dtype=x.dtype))
        h1 = jnp.einsum('th,eih->eti', x, w1)
        h3 = jnp.einsum('th,eih->eti', x, w3)
        act = jax.nn.silu(h1) * h3
        y = jnp.einsum('eti,ehi->eth', act, w2)
        out = jnp.einsum('eth,te->th', y, combine)
        return out.reshape(b, s, h)

    def _L1_cond_ref(r, k, v, w, u, time_emb):
        import jax, jax.numpy as jnp
        from jax import lax
        import numpy as np
        B, T, C, TD = (8, 256, 256, 64)

        def _bi_wkv(r, k, v, w, u, time_emb):
            tf = jax.nn.sigmoid(jnp.sum(time_emb, axis=-1))[:, None, None]
            decay = jnp.exp(-jnp.exp(w.astype(jnp.float32)))[None, :] * (0.5 + 0.5 * tf[:, :, 0])
            kf = k.astype(jnp.float32)
            vf = v.astype(jnp.float32)
            ek = jnp.exp(jnp.minimum(kf, 30.0))
            ekv = ek * vf

            def step(carry, x):
                a, b = carry
                ekv_t, ek_t = x
                a = a * decay + ekv_t
                b = b * decay + ek_t
                return ((a, b), (a, b))
            ekv_t = jnp.swapaxes(ekv, 0, 1)
            ek_t = jnp.swapaxes(ek, 0, 1)
            init = (jnp.zeros_like(decay), jnp.zeros_like(decay))
            _, (nf, df) = lax.scan(step, init, (ekv_t, ek_t))
            _, (nb, db) = lax.scan(step, init, (ekv_t, ek_t), reverse=True)
            nf = jnp.swapaxes(nf, 0, 1)
            df = jnp.swapaxes(df, 0, 1)
            nb = jnp.swapaxes(nb, 0, 1)
            db = jnp.swapaxes(db, 0, 1)
            euk = jnp.exp(jnp.minimum(u.astype(jnp.float32)[None, None, :] + kf, 30.0))
            num = nf + nb - ekv + euk * vf
            den = df + db - ek + euk
            base = jax.nn.sigmoid(r.astype(jnp.float32)) * (num / jnp.maximum(den, 1e-08))
            out = base * (0.8 + 0.2 * tf)
            return out.astype(r.dtype)
        return _bi_wkv(r, k, v, w, u, time_emb)

    def _L1_attn_ref(x, wq, wk, wv, wo):
        import jax, jax.numpy as jnp
        import numpy as np
        B, T, D = (2, 256, 256)
        QH, KVH = (16, 4)
        HD = D // QH

        def rotate_half(x):
            d = x.shape[-1] // 2
            return jnp.concatenate([-x[..., d:], x[..., :d]], axis=-1)

        def rope_tables(head_dim, seq_len, theta=10000.0):
            freqs = 1.0 / theta ** (jnp.arange(0, head_dim, 2, dtype=jnp.float32) / head_dim)
            t = jnp.arange(seq_len, dtype=jnp.float32)
            ang = t[:, None] * freqs[None, :]
            cos = jnp.tile(jnp.cos(ang), (1, 2))
            sin = jnp.tile(jnp.sin(ang), (1, 2))
            return (cos, sin)

        def apply_rope(x, cos, sin):
            c = cos[None, None, :, :]
            s = sin[None, None, :, :]
            return x * c + rotate_half(x) * s
        b, t, d = x.shape
        cos, sin = rope_tables(HD, t)
        q = (x @ wq).reshape(b, t, QH, HD).transpose(0, 2, 1, 3)
        k = (x @ wk).reshape(b, t, KVH, HD).transpose(0, 2, 1, 3)
        v = (x @ wv).reshape(b, t, KVH, HD).transpose(0, 2, 1, 3)
        q = apply_rope(q, cos, sin)
        k = apply_rope(k, cos, sin)
        g = QH // KVH
        k = jnp.repeat(k, g, axis=1)
        v = jnp.repeat(v, g, axis=1)
        attn = jnp.einsum('bhqd,bhkd->bhqk', q, k) / np.sqrt(HD)
        mask = jnp.triu(jnp.ones((t, t), dtype=bool), k=1)
        attn = jnp.where(mask[None, None], -jnp.inf, attn)
        attn = jax.nn.softmax(attn, axis=-1)
        out = jnp.einsum('bhqk,bhkd->bhqd', attn, v)
        out = out.transpose(0, 2, 1, 3).reshape(b, t, d)
        return out @ wo

    def _L1_cond2_ref(r, k, v, w, u, time_emb):
        import jax, jax.numpy as jnp
        from jax import lax
        import numpy as np
        B, T, C, TD = (8, 256, 256, 64)

        def _bi_wkv(r, k, v, w, u, time_emb):
            tf = jax.nn.sigmoid(jnp.sum(time_emb, axis=-1))[:, None, None]
            decay = jnp.exp(-jnp.exp(w.astype(jnp.float32)))[None, :] * (0.5 + 0.5 * tf[:, :, 0])
            kf = k.astype(jnp.float32)
            vf = v.astype(jnp.float32)
            ek = jnp.exp(jnp.minimum(kf, 30.0))
            ekv = ek * vf

            def step(carry, x):
                a, b = carry
                ekv_t, ek_t = x
                a = a * decay + ekv_t
                b = b * decay + ek_t
                return ((a, b), (a, b))
            ekv_t = jnp.swapaxes(ekv, 0, 1)
            ek_t = jnp.swapaxes(ek, 0, 1)
            init = (jnp.zeros_like(decay), jnp.zeros_like(decay))
            _, (nf, df) = lax.scan(step, init, (ekv_t, ek_t))
            _, (nb, db) = lax.scan(step, init, (ekv_t, ek_t), reverse=True)
            nf = jnp.swapaxes(nf, 0, 1)
            df = jnp.swapaxes(df, 0, 1)
            nb = jnp.swapaxes(nb, 0, 1)
            db = jnp.swapaxes(db, 0, 1)
            euk = jnp.exp(jnp.minimum(u.astype(jnp.float32)[None, None, :] + kf, 30.0))
            num = nf + nb - ekv + euk * vf
            den = df + db - ek + euk
            base = jax.nn.sigmoid(r.astype(jnp.float32)) * (num / jnp.maximum(den, 1e-08))
            out = base * (0.8 + 0.2 * tf)
            return out.astype(r.dtype)
        return _bi_wkv(r, k, v, w, u, time_emb)

    def _L1_ffn_ref(x, ln_w, ff_ln_w, wq, wk, wv, wo, gate_w, w1, w3, w2):
        import jax, jax.numpy as jnp
        import numpy as np
        import math
        B, S, D = (2, 128, 256)
        H, KVH, HD = (16, 4, 128)
        E, K, FF = (8, 2, 896)
        EPS = 1e-05
        ROPE_BASE = 1000000.0

        def rmsnorm(x, w, eps=EPS):
            xf = x.astype(jnp.float32)
            var = jnp.mean(xf * xf, axis=-1, keepdims=True)
            return (xf * jax.lax.rsqrt(var + eps)).astype(x.dtype) * w

        def apply_rope(x, cos, sin):
            x1 = x[..., 0::2]
            x2 = x[..., 1::2]
            r1 = x1 * cos - x2 * sin
            r2 = x1 * sin + x2 * cos
            return jnp.stack([r1, r2], axis=-1).reshape(x.shape)
        Bx, Sx, Dx = x.shape
        residual = x
        h = rmsnorm(x, ln_w)
        q = (h @ wq).reshape(Bx, Sx, H, HD)
        k = (h @ wk).reshape(Bx, Sx, KVH, HD)
        v = (h @ wv).reshape(Bx, Sx, KVH, HD)
        pos = jnp.arange(Sx, dtype=jnp.float32)
        inv_freq = ROPE_BASE ** (-jnp.arange(0, HD, 2, dtype=jnp.float32) / HD)
        ang = pos[:, None] * inv_freq[None, :]
        cos = jnp.cos(ang)[None, :, None, :]
        sin = jnp.sin(ang)[None, :, None, :]
        q = apply_rope(q, cos, sin)
        k = apply_rope(k, cos, sin)
        rep = H // KVH
        k = jnp.repeat(k, rep, axis=2)
        v = jnp.repeat(v, rep, axis=2)
        scores = jnp.einsum('bqhd,bkhd->bhqk', q, k) / math.sqrt(HD)
        causal = jnp.tril(jnp.ones((Sx, Sx), dtype=bool))
        scores = jnp.where(causal[None, None], scores, jnp.finfo(scores.dtype).min)
        attn = jax.nn.softmax(scores, axis=-1)
        o = jnp.einsum('bhqk,bkhd->bqhd', attn, v).reshape(Bx, Sx, H * HD)
        x = o @ wo + residual
        residual = x
        h = rmsnorm(x, ff_ln_w)
        ht = h.reshape(-1, Dx)
        logits = ht @ gate_w
        top_vals, top_idx = jax.lax.top_k(logits, K)
        gates = jax.nn.softmax(top_vals, axis=-1)
        out = jnp.zeros_like(ht)
        for e in range(E):
            we = jnp.sum(gates * (top_idx == e), axis=-1)
            ye = jax.nn.silu(ht @ w1[e]) * (ht @ w3[e]) @ w2[e]
            out = out + we[:, None] * ye
        return out.reshape(Bx, Sx, Dx) + residual
    x = x + _L0_attn_ref(_L0_cond_ref(x, fside_BxSxS_0, fside_BxSxS_0, L0_cond_w, L0_cond_u, cond_512), L0_attn_Wq, L0_attn_Wk, L0_attn_Wv, L0_attn_Ww, L0_attn_cq, L0_attn_ck, L0_attn_cv, L0_attn_Wf1, L0_attn_Wf2, L0_attn_Wb, L0_attn_Wg1, L0_attn_Wg2, L0_attn_bg2, L0_attn_norm_w, L0_attn_Wo)
    x = x + _L0_ffn_ref(_L0_cond2_ref(x, fside_BxSxS_0, fside_BxSxS_0, L0_cond2_w, L0_cond2_u, cond_512), L0_ffn_gate_w, L0_ffn_w1, L0_ffn_w2, L0_ffn_w3)
    x = x + _L1_attn_ref(_L1_cond_ref(x, fside_BxSxS_0, fside_BxSxS_0, L1_cond_w, L1_cond_u, cond_512), L1_attn_wq, L1_attn_wk, L1_attn_wv, L1_attn_wo)
    x = x + _L1_ffn_ref(_L1_cond2_ref(x, fside_BxSxS_0, fside_BxSxS_0, L1_cond2_w, L1_cond2_u, cond_512), L1_ffn_ln_w, L1_ffn_ff_ln_w, L1_ffn_wq, L1_ffn_wk, L1_ffn_wv, L1_ffn_wo, L1_ffn_gate_w, L1_ffn_w1, L1_ffn_w3, L1_ffn_w2)
    return x

_drawn_inputs = setup_inputs


def setup_inputs(seed=0):
    import zlib

    import numpy as np

    out = dict(_drawn_inputs(seed))
    spreads = {'L0_attn_bg2': (0.0, 0.8),
     'L0_attn_norm_w': (1.0, 0.6),
     'L1_ffn_ln_w': (1.0, 0.2),
     'L1_ffn_ff_ln_w': (1.0, 0.6)}
    factors = {'L0_cond_w': 4.524,
     'L0_cond_u': 8.0,
     'L0_attn_Wq': 8.0,
     'L0_attn_Wk': 8.0,
     'L0_attn_Ww': 2.702,
     'L0_attn_cq': 8.0,
     'L0_attn_ck': 8.0,
     'L0_attn_Wf1': 8.0,
     'L0_attn_Wf2': 8.0,
     'L0_attn_Wb': 8.0,
     'L0_attn_Wg1': 8.0,
     'L0_attn_Wg2': 8.0,
     'L0_cond2_w': 8.0,
     'L0_cond2_u': 8.0,
     'L0_ffn_gate_w': 8.0,
     'L0_ffn_w1': 8.0,
     'L0_ffn_w2': 8.0,
     'L0_ffn_w3': 8.0,
     'L1_attn_wq': 5.974,
     'L1_attn_wk': 5.966,
     'L1_ffn_wq': 8.0,
     'L1_ffn_wk': 8.0,
     'L1_ffn_gate_w': 3.347,
     'L1_ffn_w1': 2.905,
     'L1_ffn_w3': 2.849,
     'L1_ffn_w2': 2.863}
    for name, (base, spread) in spreads.items():
        noise = np.random.default_rng([zlib.crc32(name.encode()), seed]).standard_normal(out[name].shape)
        drawn = base * np.exp(spread * noise) if base else spread * noise
        out[name] = jnp.asarray(drawn.astype(out[name].dtype))
    for name, factor in factors.items():
        out[name] = (out[name] * factor).astype(out[name].dtype)
    return out
```

```python
from contextlib import ExitStack

import numpy as np

import concourse.bass as bass
from concourse import mybir

F32 = mybir.dt.float32
ALU = mybir.AluOpType
ACT = mybir.ActivationFunctionType
AX = mybir.AxisListType.X

P = 128
B, T, C, TD = 4, 256, 256, 64
N = B * T
CT = C // P
NT = N // P
HN = N // 2
NCOND = 4

GH, GK, LEVELS, KW = 16, 2, 8, 4
G_W = dict(q=0, k=256, v=512, w=768, f=1024, g=1152, o=1280, conv=1536, bg=1548, beta=1549)
G_COLS = 1552
BIG = 1e30

K_ID, K_MASK, K_CAUSAL = 0, 128, 128 + LEVELS * 128
K_COS1 = K_CAUSAL + 384
K_SIN1, K_COS2, K_SIN2 = K_COS1 + T, K_COS1 + 2 * T, K_COS1 + 3 * T
K_ROT1 = K_COS1 + 4 * T
K_ROT2 = K_ROT1 + P
K_RANK = K_ROT2 + P
K_COLS = K_RANK + 8

V_W, V_U, V_NORM, V_LN, V_FFLN = 0, 8, 16, 17, 19
V_GATE0, V_GATE1 = 21, 37
V_COLS = 53

A_Q, A_K, A_V, A_O = 0, 1024, 1280, 1408
A_COLS = A_O + 4 * C
F_K, F_V, F_COLS = 0, 1024, 2048


class Signals:

    def __init__(self, nc, ctx, env, stage):
        self.nc, self.ctx, self.stage, self.known = nc, ctx, stage, {}
        env["signals"].append(self)

    def __call__(self, name):
        if name not in self.known:
            self.known[name] = self.ctx.enter_context(self.nc.semaphore(f"{self.stage}_{name}"))
        return self.known[name]


def clear_signals(nc, env):
    with nc.Block() as block:
        @block.gpsimd
        def _(pool):
            for signals in env["signals"]:
                for semaphore in signals.known.values():
                    nc.gpsimd.sem_clear(semaphore)
    env["signals"].clear()


def halves(ap, level):
    h = 1 << level
    v = ap.rearrange("p (n two h) -> p n two h", two=2, h=h)
    return v[:, :, 0, :], v[:, :, 1, :]


def packed(ap, level):
    return ap.rearrange("p (n h) -> p n h", h=1 << level)


def over_batches(ap, n=B):
    return ap.unsqueeze(1).broadcast_to([ap.shape[0], n, ap.shape[1]])


def build(nc, a):
    with ExitStack() as ctx:
        keep = lambda name, cols: ctx.enter_context(nc.sbuf_tensor(name, [P, cols], F32))
        xT = keep("xT", CT * N)
        const = keep("const", K_COLS)
        vec = keep("vec", V_COLS)
        ratio = keep("ratio", NCOND * CT * N)
        hT = keep("hT", CT * N)
        ones = keep("ones", P)
        eps = keep("eps", 4)
        ps = ctx.enter_context(nc.psum_tensor("ps", [P, 8, 512], F32))
        env = dict(xT=xT, const=const, vec=vec, ratio=ratio, hT=hT, ones=ones, eps=eps, ps=ps, signals=[])
        conditioning(nc, a, env)
        condition(nc, env, 0)
        slot_attention(nc, a, env)
        clear_signals(nc, env)
        condition(nc, env, 1)
        moe(nc, a, env, 0)
        condition(nc, env, 2)
        attention1(nc, a, env)
        condition(nc, env, 3)
        attention2(nc, a, env)
        moe(nc, a, env, 1)


def conditioning(nc, a, env):
    xT, const, vec, ratio, ones, eps = (env[k] for k in ("xT", "const", "vec", "ratio", "ones", "eps"))
    with ExitStack() as ctx:
        s = Signals(nc, ctx, env, "cond")
        sb = lambda name, cols: ctx.enter_context(nc.sbuf_tensor(name, [P, cols], F32))
        fT = sb("fT", CT * N)
        emb = sb("emb", B * TD)
        ek = sb("ek", CT * N)
        ekv = sb("ekv", CT * N)
        kmin = sb("kmin", CT * N)
        tf = sb("tf", 3 * B)
        dw = sb("dw", 2 * 8)
        dec = sb("dec", 8 * B)
        sc = sb("sc", 4 * N)
        euk = sb("euk", 2 * N)
        block = ctx.enter_context(nc.Block())
        JOBS = [(i, ct) for i in range(NCOND) for ct in range(CT)]

        @block.sync
        def _(sp):
            sp.dma_start(fT[:, :], a["fT"]).then_inc(s("f_loaded"), 16)
            sp.dma_start(vec[:, :], a["vec"]).then_inc(s("vec_loaded"), 16)
            sp.dma_start(emb[:, :], a["emb"].partition_broadcast(P)).then_inc(s("vec_loaded"), 16)
            sp.dma_start(xT[:, :], a["xT"]).then_inc(s("rest_loaded"), 16)
            sp.dma_start(const[:, :], a["const"]).then_inc(s("rest_loaded"), 16)
            sp.wait_ge(s("rest_loaded"), 32)

        @block.scalar
        def _(act):
            act.wait_ge(s("emb_sum"), 1)
            nc.scalar.activation(tf[:, 0:B], tf[:, 0:B], ACT.Sigmoid).then_inc(s("tf"), 1)
            act.wait_ge(s("vec_loaded"), 32)
            nc.scalar.activation(dw[:, 0:8], vec[:, V_W:V_W + 8], ACT.Exp).then_inc(s("exp_w"), 1)
            act.wait_ge(s("exp_w"), 1)
            nc.scalar.activation(dw[:, 8:16], dw[:, 0:8], ACT.Exp, scale=-1.0).then_inc(s("decay_w"), 1)
            act.wait_ge(s("k_min"), 1)
            nc.scalar.activation(ek[:, :], kmin[:, :], ACT.Exp).then_inc(s("ek"), 1)
            for j in range(len(JOBS)):
                act.wait_ge(s("uk_min"), j + 1)
                e = euk[:, (j % 2) * N:(j % 2 + 1) * N]
                nc.scalar.activation(e, e, ACT.Exp).then_inc(s("euk"), 1)

        @block.gpsimd
        def _(pool):
            nc.gpsimd.memset(ones[:, :], 1.0).then_inc(s("ones"), 1)
            nc.gpsimd.memset(eps[:, 0:1], 1e-6).then_inc(s("ones"), 1)
            nc.gpsimd.memset(eps[:, 1:2], 1e-5).then_inc(s("ones"), 1)
            nc.gpsimd.memset(eps[:, 2:3], 0.0).then_inc(s("ones"), 1)
            pool.wait_ge(s("ones"), 4)

        @block.vector
        def _(dve):
            steps = [0]

            def step(ins):
                steps[0] += 1
                ins.then_inc(s("dve_step"), 1)
                dve.wait_ge(s("dve_step"), steps[0])

            v = nc.vector
            dve.wait_ge(s("f_loaded"), 16)
            v.tensor_scalar(kmin[:, :], fT[:, :], 30.0, None, ALU.min).then_inc(s("k_min"), 1)
            dve.wait_ge(s("vec_loaded"), 32)
            v.tensor_reduce(tf[:, 0:B], emb[:, :].rearrange("p (b d) -> p b d", b=B), AX, ALU.add).then_inc(s("emb_sum"), 1)

            def uk(j):
                i, ct = JOBS[j]
                u = vec[:, V_U + 2 * i + ct:V_U + 2 * i + ct + 1]
                v.tensor_scalar(euk[:, (j % 2) * N:(j % 2 + 1) * N], fT[:, ct * N:(ct + 1) * N], u, 30.0,
                                ALU.add, ALU.min).then_inc(s("uk_min"), 1)

            uk(0)
            uk(1)
            dve.wait_ge(s("ek"), 1)
            v.tensor_tensor(ekv[:, :], ek[:, :], fT[:, :], ALU.mult).then_inc(s("ekv"), 1)
            for j in range(2, len(JOBS)):
                if j == 2:
                    dve.wait_ge(s("ekv"), 1)
                scan_job(nc, dve, s, step, v, JOBS, j - 2, a, env, fT, ek, ekv, tf, dw, dec, sc, euk)
                uk(j)
            for j in range(len(JOBS) - 2, len(JOBS)):
                scan_job(nc, dve, s, step, v, JOBS, j, a, env, fT, ek, ekv, tf, dw, dec, sc, euk)
            for j in range(len(JOBS)):
                r = ratio[:, j * N:(j + 1) * N].rearrange("p (b t) -> p b t", b=B)
                w = tf[:, 2 * B:3 * B].unsqueeze(2).broadcast_to([P, B, T])
                v.tensor_tensor(r, r, w, ALU.mult)
            v.tensor_copy(tf[:, 0:1], tf[:, 1:2]).then_inc(s("done"), 1)
            dve.wait_ge(s("done"), 1)


def scan_job(nc, dve, s, step, v, JOBS, j, a, env, fT, ek, ekv, tf, dw, dec, sc, euk):
    ratio = env["ratio"]
    i, ct = JOBS[j]
    if j == 0:
        dve.wait_ge(s("tf"), 1)
        step(v.tensor_scalar(tf[:, B:2 * B], tf[:, 0:B], 0.5, 0.5, ALU.mult, ALU.add))
        step(v.tensor_scalar(tf[:, 2 * B:3 * B], tf[:, 0:B], 0.2, 0.8, ALU.mult, ALU.add))
        dve.wait_ge(s("decay_w"), 1)
        for b in range(B):
            v.tensor_scalar(dec[:, b * 8:(b + 1) * 8], dw[:, 8:16], tf[:, B + b:B + b + 1], None, ALU.mult)
        step(v.tensor_copy(sc[:, 0:1], tf[:, 0:1]))
    for b in range(B):
        lo, hi = ct * N + b * T, ct * N + (b + 1) * T
        d = dec[:, b * 8 + 2 * i + ct:b * 8 + 2 * i + ct + 1].broadcast_to([P, T])
        for n, src in ((0, ekv), (2, ek)):
            fwd = src[:, lo:hi]
            v.tensor_tensor_scan(sc[:, n * N + b * T:n * N + (b + 1) * T], d, fwd, 0.0, ALU.mult, ALU.add)
            bwd = fwd[:, ::-1]
            last = v.tensor_tensor_scan(sc[:, (n + 1) * N + b * T:(n + 1) * N + (b + 1) * T][:, ::-1],
                                        d, bwd, 0.0, ALU.mult, ALU.add)
    step(last)
    nf, nb, df, db = (sc[:, n * N:(n + 1) * N] for n in range(4))
    k, kv = ek[:, ct * N:(ct + 1) * N], ekv[:, ct * N:(ct + 1) * N]
    e = euk[:, (j % 2) * N:(j % 2 + 1) * N]
    f = fT[:, ct * N:(ct + 1) * N]
    v.tensor_tensor(nf, nf, nb, ALU.add).then_inc(s("nf"), 1)
    v.tensor_tensor(df, df, db, ALU.add).then_inc(s("df"), 1)
    dve.wait_ge(s("nf"), j + 1)
    step(v.tensor_tensor(nf, nf, kv, ALU.subtract))
    dve.wait_ge(s("df"), j + 1)
    step(v.tensor_tensor(df, df, k, ALU.subtract))
    dve.wait_ge(s("euk"), j + 1)
    step(v.tensor_tensor(df, df, e, ALU.add))
    step(v.tensor_tensor(nb, e, f, ALU.mult))
    step(v.tensor_tensor(nf, nf, nb, ALU.add))
    step(v.tensor_scalar(df, df, 1e-8, None, ALU.max))
    step(v.reciprocal(df, df))
    step(v.tensor_tensor(ratio[:, j * N:(j + 1) * N], nf, df, ALU.mult))


def condition(nc, env, i):
    xT, hT, ratio = env["xT"], env["hT"], env["ratio"]
    with ExitStack() as ctx:
        s = Signals(nc, ctx, env, f"apply{i}")
        block = ctx.enter_context(nc.Block())

        @block.scalar
        def _(act):
            for ct in range(CT):
                c = slice(ct * N, (ct + 1) * N)
                nc.scalar.activation(hT[:, c], xT[:, c], ACT.Sigmoid).then_inc(s("sigmoid"), 1)

        @block.vector
        def _(dve):
            for ct in range(CT):
                c = slice(ct * N, (ct + 1) * N)
                r = slice((i * CT + ct) * N, (i * CT + ct + 1) * N)
                dve.wait_ge(s("sigmoid"), ct + 1)
                nc.vector.tensor_tensor(hT[:, c], hT[:, c], ratio[:, r], ALU.mult).then_inc(s("h"), 1)
            dve.wait_ge(s("h"), CT)


def slot_attention(nc, a, env):
    xT, const, vec, hT, ones, eps, ps = (env[k] for k in ("xT", "const", "vec", "hT", "ones", "eps", "ps"))
    SCALE = float(P) ** -0.5
    ident = const[:, K_ID:K_ID + P]
    PROJ = ("f", "w", "beta", "k", "q", "v", "g")
    CONV = ("w", "k", "q", "v")
    TAPS = dict(q=0, k=4, v=8, w=8)
    NPROJ, NCONV = len(PROJ), len(CONV)
    with ExitStack() as ctx:
        s = Signals(nc, ctx, env, "gsa")
        sb = lambda name, cols, dt=F32: ctx.enter_context(nc.sbuf_tensor(name, [P, cols], dt))
        wt = sb("wt", G_W["o"])
        wo = sb("wo", C)
        small = sb("small", G_COLS - G_W["conv"])
        f1g1 = sb("f1g1", 2 * CT * P)
        low = sb("low", 2 * N)
        y = sb("y", NCONV * N)
        prefix = sb("prefix", N)
        suffix = sb("suffix", N)
        beta = sb("beta", N)
        gate = sb("gate", N)
        rnorm = sb("rnorm", N)
        writes = sb("writes", LEVELS * N)
        raw = writes[:, 0:NCONV * B * (T + KW - 1)]
        pre = sb("pre", LEVELS * HN)
        qk = sb("qk", N + HN)
        pairs = sb("pairs", 2 * HN)
        wt_t = sb("wt_t", 2 * N)
        v_t = sb("v_t", N)
        score = sb("score", N)
        slots = sb("slots", N)
        sm = sb("sm", N)
        tmp = sb("tmp", N)
        stat = sb("stat", 3 * NT)
        zero = sb("zero", P + 512, mybir.dt.bfloat16)
        block = ctx.enter_context(nc.Block())

        yv = {name: y[:, i * N:(i + 1) * N] for i, name in enumerate(CONV)}
        rv = {name: raw.rearrange("p (j b t) -> p j b t", j=NCONV, b=B)[:, i] for i, name in enumerate(CONV)}
        pair = lambda j: ps[:, 2 * j:2 * j + 2, :]
        flat = lambda ap: ap.rearrange("p a b -> p (a b)")
        by_batch = lambda ap: ap.rearrange("p (b t) -> p b t", b=B)
        packs = a["gsa"]

        @block.sync
        def _(sp):
            sp.dma_start(f1g1[:, :], a["f1g1"]).then_inc(s("low_weights"), 16)
            sp.dma_start(wt[:, :], packs[0, :, 0:G_W["o"]]).then_inc(s("proj_weights"), 16)
            sp.dma_start(small[:, :], packs[0, :, G_W["conv"]:G_COLS]).then_inc(s("small_weights"), 16)
            sp.dma_start(wo[:, :], packs[0, :, G_W["o"]:G_W["conv"]]).then_inc(s("out_weights"), 16)
            with sp.Fori(0, GH - 1) as h:
                nxt = packs[bass.ds(h + 1, 1)].rearrange("o p n -> p (o n)")
                sp.wait_ge(s("proj"), NPROJ * h + NPROJ)
                sp.dma_start(wt[:, :], nxt[:, 0:G_W["o"]]).then_inc(s("proj_weights"), 16)
                sp.wait_ge(s("conv"), NCONV * h + NCONV)
                sp.wait_ge(s("proj_out"), NPROJ * h + NPROJ)
                sp.dma_start(small[:, :], nxt[:, G_W["conv"]:G_COLS]).then_inc(s("small_weights"), 16)
                sp.wait_ge(s("y_out"), h + 1)
                sp.dma_start(wo[:, :], nxt[:, G_W["o"]:G_W["conv"]]).then_inc(s("out_weights"), 16)

        @block.tensor
        def _(pe):
            mm = nc.tensor.matmul
            pe.wait_ge(s("low_weights"), 16)
            for j in range(2):
                for half in range(2):
                    for kt in range(CT):
                        last = mm(ps[:, 2 * j + half, :], f1g1[:, (j * CT + kt) * P:(j * CT + kt + 1) * P],
                                  hT[:, kt * N + half * HN:kt * N + (half + 1) * HN], start=kt == 0, stop=kt == CT - 1)
                last.then_inc(s("low_ps"), 1)
            pe.wait_ge(s("low"), 2)
            pe.wait_ge(s("zero"), 1)

            def ones_sum(banks, src):
                for half in range(2):
                    last = mm(ps[:, banks + half, :], ones[:, :], src[:, half * HN:(half + 1) * HN], start=True, stop=True)
                return last

            with pe.Fori(0, GH) as h:
                pe.wait_ge(s("proj_weights"), 16 * h + 16)
                pe.wait_ge(s("small_weights"), 16 * h + 16)
                pe.wait_ge(s("x_added"), h + 1)
                for j, name in enumerate(PROJ):
                    if j >= 2:
                        pe.wait_ge(s("proj_out"), NPROJ * h + j - 1)
                    for half in range(2):
                        cols = slice(half * HN, (half + 1) * HN)
                        out = ps[:, 2 * (j % 2) + half, :]
                        if name in "fg":
                            last = mm(out, wt[:, G_W[name]:G_W[name] + P],
                                      low[:, (name == "g") * N + half * HN:(name == "g") * N + (half + 1) * HN],
                                      start=True, stop=True)
                            continue
                        for kt in range(CT):
                            if name == "beta":
                                c = G_W["beta"] - G_W["conv"] + kt
                                w = small[:, c:c + 1].broadcast_to([P, P])
                            else:
                                w = wt[:, G_W[name] + kt * P:G_W[name] + (kt + 1) * P]
                            last = mm(out, w, hT[:, kt * N + half * HN:kt * N + (half + 1) * HN], start=kt == 0, stop=kt == CT - 1)
                    last.then_inc(s("proj"), 1)
                pe.wait_ge(s("w_squared"), h + 1)
                ones_sum(4, tmp).then_inc(s("w_norm_ps"), 1)
                pe.wait_ge(s("qk"), h + 1)
                ones_sum(6, sm).then_inc(s("qk_ps"), 1)

                pe.wait_ge(s("proj_out"), NPROJ * h + NPROJ)
                for n in range(NT):
                    mm(ps[:, n // 4, (n % 4) * P:(n % 4 + 1) * P], yv["k"][:, n * P:(n + 1) * P],
                       yv["q"][:, n * P:(n + 1) * P], start=True, stop=True)
                for b in range(B):
                    last = mm(ps[:, 2, b * P:(b + 1) * P], yv["k"][:, b * T:b * T + P],
                              yv["q"][:, b * T + P:(b + 1) * T], start=True, stop=True)
                last.then_inc(s("kq_ps"), 1)
                pe.wait_ge(s("w_rnorm"), h + 1)
                for n in range(NT):
                    last = nc.tensor.transpose(ps[:, 4 + n // 4, (n % 4) * P:(n % 4 + 1) * P], yv["v"][:, n * P:(n + 1) * P], ident)
                last.then_inc(s("v_t_ps"), 1)

                def turn(l):
                    n = LEVELS * h + l
                    pe.wait_ge(s("writes"), n + 1)
                    if l >= 2:
                        pe.wait_ge(s("writes_t"), n - 1)
                    else:
                        pe.wait_ge(s("kq"), h + 1)
                    for i, tile in enumerate(range(NT) if l < LEVELS - 1 else range(0, NT, 2)):
                        c = l * N + tile * P
                        last = nc.tensor.transpose(ps[:, 2 * (l % 2) + i // 4, (i % 4) * P:(i % 4 + 1) * P], writes[:, c:c + P], ident)
                    last.then_inc(s("writes_t_ps"), 1)

                def read(l):
                    n = LEVELS * h + l
                    pe.wait_ge(s("writes_t"), n + 1)
                    if l < 2:
                        pe.wait_ge(s("v_t"), h + 1)
                    else:
                        pe.wait_ge(s("score_level"), n - 1)
                    wt_l = wt_t[:, (l % 2) * N:(l % 2 + 1) * N]
                    if l < LEVELS - 1:
                        pe.wait_ge(s("kq_pairs"), (LEVELS - 1) * h + l + 1)
                        for i in range(NT):
                            c = (l % 2) * HN + i * (P // 2)
                            last = mm(ps[:, 4 + l % 2, i * (P // 2):(i + 1) * (P // 2)], wt_l[:, i * P:(i + 1) * P],
                                      pairs[:, c:c + P // 2], start=True, stop=True)
                    else:
                        for b in range(B):
                            last = mm(ps[:, 4 + l % 2, b * P:(b + 1) * P], wt_l[:, b * P:(b + 1) * P],
                                      qk[:, N + b * P:N + (b + 1) * P], start=True, stop=True)
                    last.then_inc(s("level_ps"), 1)

                for l in range(LEVELS + 1):
                    if l < LEVELS:
                        turn(l)
                    if l >= 1:
                        read(l - 1)

                pe.wait_ge(s("score_level"), LEVELS * h + LEVELS)
                for n in range(NT):
                    last = nc.tensor.transpose(ps[:, 6 + n // 4, (n % 4) * P:(n % 4 + 1) * P], score[:, n * P:(n + 1) * P], ident)
                last.then_inc(s("score_t"), 1)
                pe.wait_ge(s("softmax"), h + 1)
                for n in range(NT):
                    last = nc.tensor.transpose(ps[:, 4 + n // 4, (n % 4) * P:(n % 4 + 1) * P], sm[:, n * P:(n + 1) * P], ident)
                last.then_inc(s("slots_ps"), 1)
                pe.wait_ge(s("slot_write"), h + 1)
                ones_sum(4, tmp).then_inc(s("slot_write_ps"), 1)

                for half in range(2):
                    mm(ps[:, 6 + half, :], zero[0:1, 0:P], zero[0:1, P:P + 512], start=True, stop=False, skip_group_check=True)

                def products(l):
                    n = LEVELS * h + l
                    pe.wait_ge(s("reads"), n + 1)
                    if l >= 2:
                        pe.wait_ge(s("aw_pairs"), n - 1)
                    w = P // 2 if l < LEVELS - 1 else P
                    for i, tile in enumerate(range(NT) if l < LEVELS - 1 else range(0, NT, 2)):
                        last = mm(ps[:, l % 2, i * w:(i + 1) * w], writes[:, l * N + tile * P:l * N + (tile + 1) * P],
                                  sm[:, (l % 2) * HN + i * w:(l % 2) * HN + (i + 1) * w], start=True, stop=True)
                    last.then_inc(s("aw_pairs_ps"), 1)

                def collect(l):
                    pe.wait_ge(s("aw_pairs"), LEVELS * h + l + 1)
                    c = (l % 2) * HN
                    if l < LEVELS - 1:
                        for i in range(NT):
                            out = halves(ps[:, 6 + i // 4, (i % 4) * P:(i % 4 + 1) * P], l)[1]
                            last = mm(out, v_t[:, i * P:(i + 1) * P], packed(pairs[:, c + i * (P // 2):c + (i + 1) * (P // 2)], l),
                                      start=False, stop=False, skip_group_check=True)
                    else:
                        for b in range(B):
                            i = 2 * b + 1
                            last = mm(ps[:, 6 + i // 4, (i % 4) * P:(i % 4 + 1) * P], v_t[:, 2 * b * P:(2 * b + 1) * P],
                                      pairs[:, c + b * P:c + (b + 1) * P], start=False, stop=True, skip_group_check=True)
                    last.then_inc(s("level_out"), 1)

                for l in range(LEVELS + 1):
                    if l < LEVELS:
                        products(l)
                    if l >= 1:
                        collect(l - 1)
                pe.wait_ge(s("o_squared"), h + 1)
                ones_sum(4, tmp).then_inc(s("o_norm_ps"), 1)
                pe.wait_ge(s("o_gated"), h + 1)
                pe.wait_ge(s("out_weights"), 16 * h + 16)
                for ct in range(CT):
                    for half in range(2):
                        last = mm(ps[:, 2 * ct + half, :], wo[:, ct * P:(ct + 1) * P], score[:, half * HN:(half + 1) * HN],
                                  start=True, stop=True)
                last.then_inc(s("y_out"), 1)

        @block.scalar
        def _(act):
            A = nc.scalar.activation
            for j in range(2):
                act.wait_ge(s("low_ps"), j + 1)
                A(low[:, j * N:(j + 1) * N], flat(pair(j)), ACT.Copy).then_inc(s("low"), 1)
            act.wait_ge(s("zero"), 1)
            with act.Fori(0, GH) as h:
                act.wait_ge(s("small_weights"), 16 * h + 16)

                def sigmoid_y(name):
                    act.wait_ge(s("conv"), NCONV * h + CONV.index(name) + 1)
                    A(rv[name][:, :, KW - 1:], by_batch(yv[name]), ACT.Sigmoid).then_inc(s("y_sigmoid"), 1)

                for j, name in enumerate(PROJ):
                    act.wait_ge(s("proj"), NPROJ * h + j + 1)
                    src = flat(pair(j % 2))
                    if name == "f":
                        A(prefix[:, :], src, ACT.Sigmoid).then_inc(s("proj_out"), 1)
                    elif name == "beta":
                        A(beta[:, :], src, ACT.Sigmoid).then_inc(s("proj_out"), 1)
                    elif name == "g":
                        c = G_W["bg"] - G_W["conv"]
                        A(gate[:, :], src, ACT.Sigmoid, bias=small[:, c:c + 1]).then_inc(s("proj_out"), 1)
                    else:
                        A(rv[name][:, :, KW - 1:], by_batch(src), ACT.Copy)
                        c = TAPS[name] + KW - 1
                        A(yv[name], src, ACT.Copy, scale=small[:, c:c + 1]).then_inc(s("proj_out"), 1)
                    if j >= 3 and PROJ[j] in "kqv":
                        sigmoid_y(CONV[CONV.index(name) - 1])
                sigmoid_y("v")
                act.wait_ge(s("w"), h + 1)
                A(tmp[:, :], yv["w"], ACT.Square).then_inc(s("w_squared"), 1)
                act.wait_ge(s("w_norm_ps"), h + 1)
                A(rnorm[:, :], flat(pair(2)), ACT.Ln, bias=eps[:, 0:1]).then_inc(s("log"), 1)
                act.wait_ge(s("log"), 2 * h + 1)
                A(rnorm[:, :], rnorm[:, :], ACT.Exp, scale=-0.5).then_inc(s("w_rnorm"), 1)
                act.wait_ge(s("kq_ps"), h + 1)
                A(qk[:, 0:N], flat(pair(0)), ACT.Copy, scale=SCALE)
                A(qk[:, N:], ps[:, 2, :], ACT.Copy, scale=SCALE).then_inc(s("kq"), 1)
                act.wait_ge(s("v_t_ps"), h + 1)
                A(v_t[:, :], flat(pair(2)), ACT.Copy).then_inc(s("v_t"), 1)
                for l in range(LEVELS):
                    n = LEVELS * h + l
                    if l:
                        act.wait_ge(s("prefix"), (LEVELS - 1) * h + l)
                    A(packed(pre[:, l * HN:(l + 1) * HN], l), halves(prefix[:, :], l)[1], ACT.Copy).then_inc(s("pre"), 1)
                    act.wait_ge(s("writes_t_ps"), n + 1)
                    if l >= 2:
                        act.wait_ge(s("level_ps"), n - 1)
                    w = N if l < LEVELS - 1 else HN
                    A(wt_t[:, (l % 2) * N:(l % 2) * N + w], flat(pair(l % 2))[:, 0:w], ACT.Copy).then_inc(s("writes_t"), 1)
                act.wait_ge(s("centred"), h + 1)
                A(sm[:, :], sm[:, :], ACT.Exp).then_inc(s("exp"), 1)
                act.wait_ge(s("slots_ps"), h + 1)
                A(slots[:, :], flat(pair(2)), ACT.Copy).then_inc(s("slots"), 1)
                act.wait_ge(s("o"), h + 1)
                A(tmp[:, :], score[:, :], ACT.Square).then_inc(s("o_squared"), 1)
                act.wait_ge(s("o_norm_ps"), h + 1)
                A(rnorm[:, :], flat(pair(2)), ACT.Ln, bias=eps[:, 1:2], scale=1.0 / P).then_inc(s("log"), 1)
                act.wait_ge(s("log"), 2 * h + 2)
                A(rnorm[:, :], rnorm[:, :], ACT.Exp, scale=-0.5).then_inc(s("o_rnorm"), 1)

        @block.gpsimd
        def _(pool):
            g = nc.gpsimd
            g.memset(zero[:, :], 0.0)
            g.memset(writes[:, :], 0.0).then_inc(s("zero"), 1)
            pool.wait_ge(s("zero"), 1)
            with pool.Fori(0, GH) as h:
                pool.wait_ge(s("bw"), h + 1)
                pool.wait_ge(s("kqv"), 3 * h + 3)
                for l in range(LEVELS):
                    left, right = halves(prefix[:, :], l)
                    half = [P, N >> (l + 1), 1 << l]
                    sl = halves(suffix[:, :], l)[0]
                    pool.wait_ge(s("suffix"), LEVELS * h + l + 1)
                    g.tensor_tensor(halves(writes[:, l * N:(l + 1) * N], l)[0], halves(yv["w"], l)[0], sl,
                                    ALU.mult).then_inc(s("writes"), 1)
                    if l == LEVELS - 1:
                        break
                    if l:
                        pool.wait_ge(s("prefix"), (LEVELS - 1) * h + l)
                    end = right[:, :, (1 << l) - 1:1 << l].broadcast_to(half)
                    g.tensor_tensor(sl, sl, end, ALU.mult).then_inc(s("suffix"), 1)
                    pool.wait_ge(s("suffix"), LEVELS * h + l + 2)
                    pool.wait_ge(s("pre"), LEVELS * h + l + 1)
                    end = left[:, :, (1 << l) - 1:1 << l].broadcast_to(half)
                    g.tensor_tensor(right, right, end, ALU.mult).then_inc(s("prefix"), 1)
                pool.wait_ge(s("slots"), h + 1)
                for l in range(LEVELS):
                    if l >= 2:
                        pool.wait_ge(s("aw_pairs_ps"), LEVELS * h + l - 1)
                    g.tensor_tensor(packed(sm[:, (l % 2) * HN:(l % 2 + 1) * HN], l), halves(slots[:, :], l)[1],
                                    packed(pre[:, l * HN:(l + 1) * HN], l), ALU.mult).then_inc(s("reads"), 1)

        @block.vector
        def _(dve):
            v = nc.vector
            dve.wait_ge(s("zero"), 1)
            dve.sem_inc(s("x_added"), 1)
            pads = raw.rearrange("p (j t) -> p j t", j=NCONV * B)[:, :, 0:KW - 1]
            with dve.Fori(0, GH) as h:
                dve.wait_ge(s("small_weights"), 16 * h + 16)
                v.memset(suffix[:, :], 1.0).then_inc(s("suffix"), 1)
                v.memset(pads, 0.0).then_inc(s("pads"), 1)
                dve.wait_ge(s("pads"), h + 1)

                def silu(name):
                    dve.wait_ge(s("y_sigmoid"), NCONV * h + CONV.index(name) + 1)
                    return v.tensor_tensor(by_batch(yv[name]), by_batch(yv[name]), rv[name][:, :, KW - 1:], ALU.mult)

                for i, name in enumerate(CONV):
                    dve.wait_ge(s("proj_out"), NPROJ * h + PROJ.index(name) + 1)
                    for tap in range(KW - 1):
                        c = TAPS[name] + tap
                        ins = v.scalar_tensor_tensor(by_batch(yv[name]), rv[name][:, :, tap:tap + T], small[:, c:c + 1],
                                                     by_batch(yv[name]), ALU.mult, ALU.add)
                        if tap < KW - 2:
                            ins.then_inc(s("tap"), 1)
                            dve.wait_ge(s("tap"), (KW - 2) * (NCONV * h + i) + tap + 1)
                    ins.then_inc(s("conv"), 1)
                    if i:
                        done = silu(CONV[i - 1])
                        done.then_inc(s("w" if i == 1 else "kqv"), 1)
                silu("v").then_inc(s("kqv"), 1)
                dve.wait_ge(s("kqv"), 3 * h + 3)
                v.tensor_tensor(sm[:, :], yv["q"], yv["k"], ALU.mult).then_inc(s("qk"), 1)
                dve.wait_ge(s("w_squared"), h + 1)
                v.tensor_tensor(yv["w"], yv["w"], beta[:, :], ALU.mult).then_inc(s("w_beta"), 1)
                dve.wait_ge(s("w_beta"), h + 1)
                dve.wait_ge(s("w_rnorm"), h + 1)
                v.tensor_tensor(yv["w"], yv["w"], rnorm[:, :], ALU.mult).then_inc(s("bw"), 1)
                dve.wait_ge(s("bw"), h + 1)
                dve.wait_ge(s("qk_ps"), h + 1)
                v.scalar_tensor_tensor(score[:, :], flat(pair(3)), SCALE, yv["w"], ALU.mult, ALU.mult).then_inc(s("score_diag"), 1)

                def masked(l, products):
                    m = halves(const[:, K_MASK + l * P:K_MASK + (l + 1) * P], l)[1]
                    m = m.unsqueeze(1).broadcast_to([P, NT, m.shape[1], m.shape[2]])
                    split = dict(i=NT, h=1 << l)
                    return v.tensor_tensor(pairs[:, (l % 2) * HN:(l % 2 + 1) * HN].rearrange("p (i n h) -> p i n h", **split),
                                           products, m, ALU.mult)

                dve.wait_ge(s("kq"), h + 1)
                for l in range(LEVELS + 1):
                    if l < LEVELS - 1:
                        if l >= 2:
                            dve.wait_ge(s("level_ps"), LEVELS * h + l - 1)
                        kq = qk[:, 0:N].rearrange("p (i n two h) -> p i n two h", i=NT, two=2, h=1 << l)[:, :, :, 1, :]
                        masked(l, kq).then_inc(s("kq_pairs"), 1)
                    if l >= 1:
                        k = l - 1
                        n = LEVELS * h + k
                        dve.wait_ge(s("level_ps"), n + 1)
                        dve.wait_ge(s("pre"), n + 1)
                        t = tmp[:, (k % 2) * HN:(k % 2 + 1) * HN]
                        v.tensor_tensor(t, ps[:, 4 + k % 2, :], pre[:, k * HN:(k + 1) * HN], ALU.mult).then_inc(s("level_read"), 1)
                        dve.wait_ge(s("level_read"), n + 1)
                        if k:
                            dve.wait_ge(s("score_level"), n)
                        else:
                            dve.wait_ge(s("score_diag"), h + 1)
                        right = halves(score[:, :], k)[1]
                        v.tensor_tensor(right, right, packed(t, k), ALU.add).then_inc(s("score_level"), 1)

                sv = sm[:, :].rearrange("p (n m) -> p n m", n=NT)
                across = lambda ap: ap.unsqueeze(2).broadcast_to([P, NT, P])
                pv = flat(pair(3)).rearrange("p (n m) -> p n m", n=NT)
                dve.wait_ge(s("score_t"), h + 1)
                v.tensor_reduce(stat[:, 0:NT], pv, AX, ALU.max).then_inc(s("max"), 1)
                dve.wait_ge(s("max"), h + 1)
                v.tensor_tensor(sv, pv, across(stat[:, 0:NT]), ALU.subtract).then_inc(s("centred"), 1)
                dve.wait_ge(s("exp"), h + 1)
                v.tensor_reduce(stat[:, NT:2 * NT], sv, AX, ALU.add).then_inc(s("sum"), 1)
                dve.wait_ge(s("sum"), h + 1)
                v.reciprocal(stat[:, 2 * NT:3 * NT], stat[:, NT:2 * NT]).then_inc(s("inverse"), 1)
                dve.wait_ge(s("inverse"), h + 1)
                v.tensor_tensor(sv, sv, across(stat[:, 2 * NT:3 * NT]), ALU.mult).then_inc(s("softmax"), 1)

                dve.wait_ge(s("slots"), h + 1)
                v.tensor_tensor(tmp[:, :], slots[:, :], yv["w"], ALU.mult).then_inc(s("slot_write"), 1)
                dve.wait_ge(s("slot_write_ps"), h + 1)
                v.tensor_tensor(score[:, :], flat(pair(2)), yv["v"], ALU.mult).then_inc(s("own"), 1)
                for l in range(LEVELS):
                    dve.wait_ge(s("aw_pairs_ps"), LEVELS * h + l + 1)
                    if l >= 2:
                        dve.wait_ge(s("level_out"), LEVELS * h + l - 1)
                    if l < LEVELS - 1:
                        aw = ps[:, l % 2, :].rearrange("p (i n h) -> p i n h", i=NT, h=1 << l)
                        masked(l, aw).then_inc(s("aw_pairs"), 1)
                    else:
                        v.tensor_copy(pairs[:, (l % 2) * HN:(l % 2 + 1) * HN], ps[:, l % 2, :]).then_inc(s("aw_pairs"), 1)
                dve.wait_ge(s("own"), h + 1)
                dve.wait_ge(s("level_out"), LEVELS * h + LEVELS)
                v.tensor_tensor(score[:, :], flat(pair(3)), score[:, :], ALU.add).then_inc(s("o"), 1)
                dve.wait_ge(s("o_squared"), h + 1)
                dve.wait_ge(s("o_rnorm"), h + 1)
                v.tensor_tensor(score[:, :], score[:, :], rnorm[:, :], ALU.mult).then_inc(s("o_normed"), 1)
                dve.wait_ge(s("o_normed"), h + 1)
                v.scalar_tensor_tensor(score[:, :], score[:, :], vec[:, V_NORM:V_NORM + 1], gate[:, :],
                                       ALU.mult, ALU.mult).then_inc(s("o_gated"), 1)
                dve.wait_ge(s("y_out"), h + 1)
                v.tensor_tensor(xT[:, :], xT[:, :], ps[:, 0:4, :].rearrange("p a b -> p (a b)"), ALU.add).then_inc(s("x_added"), 1)
                dve.wait_ge(s("x_added"), h + 2)

def rmsnorm(nc, env, dst, col):
    vec, hT, ones, eps, ps = (env[k] for k in ("vec", "hT", "ones", "eps", "ps"))
    with ExitStack() as ctx:
        s = Signals(nc, ctx, env, f"rms{col}")
        square = ctx.enter_context(nc.sbuf_tensor(f"square{col}", [P, CT * N], F32))
        rnorm = ctx.enter_context(nc.sbuf_tensor(f"rms_rnorm{col}", [P, N], F32))
        block = ctx.enter_context(nc.Block())

        @block.scalar
        def _(act):
            nc.scalar.activation(square[:, :], hT[:, :], ACT.Square).then_inc(s("square"), 1)
            act.wait_ge(s("sum"), 1)
            nc.scalar.activation(rnorm[:, :], ps[:, 0:2, :].rearrange("p a b -> p (a b)"), ACT.Ln, bias=eps[:, 1:2],
                                 scale=1.0 / C).then_inc(s("log"), 1)
            act.wait_ge(s("log"), 1)
            nc.scalar.activation(rnorm[:, :], rnorm[:, :], ACT.Exp, scale=-0.5).then_inc(s("rnorm"), 1)

        @block.tensor
        def _(pe):
            pe.wait_ge(s("square"), 1)
            for half in range(2):
                for kt in range(CT):
                    last = nc.tensor.matmul(ps[:, half, :], ones[:, :], square[:, kt * N + half * HN:kt * N + (half + 1) * HN],
                                            start=kt == 0, stop=kt == CT - 1)
            last.then_inc(s("sum"), 1)

        @block.vector
        def _(dve):
            dve.wait_ge(s("rnorm"), 1)
            for ct in range(CT):
                c = slice(ct * N, (ct + 1) * N)
                nc.vector.scalar_tensor_tensor(dst[:, c], hT[:, c], vec[:, col + ct:col + ct + 1], rnorm[:, :],
                                               ALU.mult, ALU.mult).then_inc(s("out"), 1)
            dve.wait_ge(s("out"), CT)


def moe(nc, a, env, layer):
    xT, const, vec, hT, ps = (env[k] for k in ("xT", "const", "vec", "hT", "ps"))
    packs = a[f"moe{layer}"]
    NE = packs.shape[0]
    NI = packs.shape[2] // (3 * C)
    W1, W3, W2 = 0, CT * NI * P, 2 * CT * NI * P
    UNITS = 2 * NI
    TH = NT // 2
    assert UNITS % 2 == 0 and NE % 2 == 0
    with ExitStack() as ctx:
        sb = lambda name, cols: ctx.enter_context(nc.sbuf_tensor(f"{name}_moe{layer}", [P, cols], F32))
        if layer:
            src = sb("normed", CT * N)
            rmsnorm(nc, env, src, V_FFLN)
        else:
            src = hT
        s = Signals(nc, ctx, env, f"moe{layer}")
        weights = sb("weights", 2 * packs.shape[2])
        hidden = sb("hidden", NI * N)
        silu = sb("silu", 2 * HN)
        acc = sb("acc", NT * C)
        comb = sb("comb", NE * NT)
        mine = sb("mine", 2 * NT)
        rt = {k: sb("rt_" + k, NT * NE) for k in ("logits", "abs", "hot1", "hot2", "a", "b", "c")}
        st = {k: sb("st_" + k, NT) for k in ("max1", "max2", "index", "gate1", "gate2", "sum")}
        block = ctx.enter_context(nc.Block())
        gate_col = V_GATE1 if layer else V_GATE0

        @block.sync
        def _(sp):
            W = packs.shape[2]
            for slot in range(2):
                sp.dma_start(weights[:, slot * W:(slot + 1) * W], packs[slot]).then_inc(s(f"weights{slot}"), 16)
            with sp.Fori(0, NE // 2 - 1) as i:
                for slot in range(2):
                    sp.wait_ge(s("y_ps"), (2 * i + slot + 1) * NT + 1)
                    nxt = packs[bass.ds(2 * i + slot + 2, 1)].rearrange("o p n -> p (o n)")
                    sp.dma_start(weights[:, slot * W:(slot + 1) * W], nxt).then_inc(s(f"weights{slot}"), 16)
            if layer:
                out = a["out"].rearrange("(n p) c -> p n c", p=P)
                sp.wait_ge(s("final"), 1)
                sp.dma_start(out, acc[:, :].rearrange("p (n c) -> p n c", n=NT)).then_inc(s("stored"), 16)
                sp.wait_ge(s("stored"), 16)

        @block.tensor
        def _(pe):
            mm = nc.tensor.matmul
            for n in range(NT):
                for kt in range(CT):
                    last = mm(ps[:, 7, n * NE:(n + 1) * NE], src[:, kt * N + n * P:kt * N + (n + 1) * P],
                              vec[:, gate_col + kt * NE:gate_col + (kt + 1) * NE], start=kt == 0, stop=kt == CT - 1)
            last.then_inc(s("logits_ps"), 1)
            pe.sem_inc(s("y_ps"), 1)
            with pe.Fori(0, NE // 2) as i:
                for slot in range(2):
                    e = 2 * i + slot
                    w = weights[:, slot * packs.shape[2]:(slot + 1) * packs.shape[2]]
                    pe.wait_ge(s(f"weights{slot}"), 16 * i + 16)
                    for u in range(UNITS):
                        half, it = divmod(u, NI)
                        pe.wait_ge(s("up_free"), UNITS * e + u + 1)
                        for bank, base in ((u % 2, W1), (2 + u % 2, W3)):
                            for kt in range(CT):
                                c = base + kt * NI * P + it * P
                                last = mm(ps[:, bank, :], w[:, c:c + P], src[:, kt * N + half * HN:kt * N + (half + 1) * HN],
                                          start=kt == 0, stop=kt == CT - 1)
                            if base == W1:
                                last.then_inc(s("up1_ps"), 1)
                        last.then_inc(s("up3_ps"), 1)
                    for n in range(NT):
                        half = n // TH
                        pe.wait_ge(s("up_free"), UNITS * e + NI * (half + 1) + 2)
                        pe.wait_ge(s("y_free"), NT * e + n + 1)
                        for it in range(NI):
                            last = mm(ps[:, 4 + n % 4, 0:C], hidden[:, it * N + n * P:it * N + (n + 1) * P],
                                      w[:, W2 + it * C:W2 + (it + 1) * C], start=it == 0, stop=it == NI - 1)
                        last.then_inc(s("y_ps"), 1)
            ident = const[:, K_ID:K_ID + P]
            if layer:
                pe.wait_ge(s("streams"), 1)
                for n in range(NT):
                    for ct in range(CT):
                        last = nc.tensor.transpose(ps[:, n // 2, (n % 2) * C + ct * P:(n % 2) * C + (ct + 1) * P],
                                                   src[:, ct * N + n * P:ct * N + (n + 1) * P], ident)
            else:
                pe.wait_ge(s("y_free"), NT * NE + 4)
                for n in range(NT):
                    for ct in range(CT):
                        last = nc.tensor.transpose(ps[:, 2 * ct + n // 4, (n % 4) * P:(n % 4 + 1) * P],
                                                   acc[:, n * C + ct * P:n * C + (ct + 1) * P], ident)
            last.then_inc(s("turned"), 1)

        @block.scalar
        def _(act):
            act.wait_ge(s("exp_in"), 1)
            if layer:
                nc.scalar.activation(st["gate2"][:, :], st["gate2"][:, :], ACT.Exp).then_inc(s("exp"), 1)
            else:
                nc.scalar.activation(rt["b"][:, :], rt["b"][:, :], ACT.Exp).then_inc(s("exp"), 1)
                act.wait_ge(s("exp_in"), 2)
                nc.scalar.activation(rt["b"][:, :], rt["b"][:, :], ACT.Exp).then_inc(s("exp"), 1)
            with act.Fori(0, NE // 2) as i:
                for slot in range(2):
                    e = 2 * i + slot
                    for u in range(UNITS):
                        act.wait_ge(s("up1_ps"), UNITS * e + u + 1)
                        act.wait_ge(s("up_free"), UNITS * e + u + 1)
                        nc.scalar.activation(silu[:, (u % 2) * HN:(u % 2 + 1) * HN], ps[:, u % 2, :],
                                             ACT.Silu).then_inc(s("silu"), 1)

        @block.vector
        def _(dve):
            v = nc.vector
            steps = [0]

            def step(ins):
                steps[0] += 1
                ins.then_inc(s("dve_step"), 1)
                dve.wait_ge(s("dve_step"), steps[0])

            by_tile = lambda t: t[:, :].rearrange("p (n e) -> p n e", e=NE)
            each = lambda t: t[:, :].unsqueeze(2).broadcast_to([P, NT, NE])
            rank = const[:, K_RANK:K_RANK + NE].unsqueeze(1).broadcast_to([P, NT, NE])
            L, AB, H1, H2, TA, TB, TC = (by_tile(rt[k]) for k in ("logits", "abs", "hot1", "hot2", "a", "b", "c"))
            v.memset(acc[:, :], 0.0).then_inc(s("y_free"), 4)
            dve.wait_ge(s("y_free"), 4)
            v.memset(silu[:, 0:1], 0.0).then_inc(s("up_free"), 2)
            dve.wait_ge(s("up_free"), 2)
            dve.wait_ge(s("logits_ps"), 1)
            step(v.tensor_copy(rt["logits"][:, :], ps[:, 7, 0:NT * NE]))

            def first_max(scores, top, hot):
                step(v.tensor_reduce(st[top][:, :], scores, AX, ALU.max))
                step(v.tensor_tensor(TA, scores, each(st[top]), ALU.is_equal))
                step(v.tensor_tensor(TA, TA, rank, ALU.mult))
                step(v.tensor_reduce(st["index"][:, :], TA, AX, ALU.max))
                step(v.tensor_tensor(hot, rank, each(st["index"]), ALU.is_equal))

            def sparse_gate(scores, top, gate, n):
                step(v.tensor_tensor(TA, AB, each(st[top]), ALU.max))
                step(v.tensor_scalar(rt["a"][:, :], rt["a"][:, :], 0.02, None, ALU.mult))
                step(v.tensor_tensor(TB, scores, each(st[top]), ALU.subtract))
                step(v.tensor_scalar(rt["c"][:, :], rt["b"][:, :], -1.0, None, ALU.mult))
                step(v.tensor_tensor(TA, TC, TA, ALU.is_le))
                v.tensor_copy(st["index"][:, :], st[top][:, :]).then_inc(s("exp_in"), 1)
                dve.wait_ge(s("exp"), n)
                step(v.tensor_tensor(TB, TB, TA, ALU.mult))
                step(v.tensor_reduce(st["sum"][:, :], TB, AX, ALU.add))
                step(v.reciprocal(st[gate][:, :], st["sum"][:, :]))

            first_max(L, "max1", H1)
            if layer:
                step(v.scalar_tensor_tensor(TC, H1, -BIG, L, ALU.mult, ALU.add))
                first_max(TC, "max2", H2)
                v.tensor_tensor(st["gate2"][:, :], st["max2"][:, :], st["max1"][:, :], ALU.subtract).then_inc(s("exp_in"), 1)
                dve.wait_ge(s("exp"), 1)
                step(v.tensor_scalar(st["sum"][:, :], st["gate2"][:, :], 1.0, None, ALU.add))
                step(v.reciprocal(st["gate1"][:, :], st["sum"][:, :]))
                step(v.tensor_tensor(st["gate2"][:, :], st["gate2"][:, :], st["gate1"][:, :], ALU.mult))
            else:
                step(v.scalar_tensor_tensor(rt["abs"][:, :], rt["logits"][:, :], -1.0, rt["logits"][:, :], ALU.mult, ALU.max))
                sparse_gate(L, "max1", "gate1", 1)
                step(v.scalar_tensor_tensor(TC, H1, -BIG, L, ALU.mult, ALU.add))
                step(v.tensor_copy(rt["logits"][:, :], rt["c"][:, :]))
                first_max(L, "max2", H2)
                sparse_gate(L, "max2", "gate2", 2)
            step(v.tensor_tensor(H1, H1, each(st["gate1"]), ALU.mult))
            step(v.tensor_tensor(H2, H2, each(st["gate2"]), ALU.mult))
            step(v.tensor_tensor(comb[:, :].rearrange("p (e n) -> p n e", e=NE), H1, H2, ALU.add))
            with dve.Fori(0, NE // 2) as i:
                for slot in range(2):
                    e = 2 * i + slot
                    v.tensor_copy(mine[:, slot * NT:(slot + 1) * NT], comb[:, bass.ds(e * NT, NT)]).then_inc(s("mine"), 1)
                    for u in range(UNITS):
                        half, it = divmod(u, NI)
                        dve.wait_ge(s("silu"), UNITS * e + u + 1)
                        dve.wait_ge(s("up3_ps"), UNITS * e + u + 1)
                        c = it * N + half * HN
                        dve.wait_ge(s("y_ps"), NT * e + 1)
                        v.tensor_tensor(hidden[:, c:c + HN], silu[:, (u % 2) * HN:(u % 2 + 1) * HN], ps[:, 2 + u % 2, :],
                                        ALU.mult).then_inc(s("up_free"), 1)
                    dve.wait_ge(s("mine"), e + 1)
                    for n in range(NT):
                        dve.wait_ge(s("y_ps"), NT * e + n + 2)
                        dve.wait_ge(s("y_free"), NT * e + n + 4)
                        tile = acc[:, n * C:(n + 1) * C]
                        c = slot * NT + n
                        v.scalar_tensor_tensor(tile, ps[:, 4 + n % 4, 0:C], mine[:, c:c + 1], tile, ALU.mult,
                                               ALU.add).then_inc(s("y_free"), 1)
            if layer:
                dve.wait_ge(s("y_ps"), NT * NE + 1)
                v.tensor_tensor(src[:, :], xT[:, :], hT[:, :], ALU.add).then_inc(s("streams"), 1)
                dve.wait_ge(s("turned"), 1)
                dve.wait_ge(s("y_free"), NT * NE + 4)
                v.tensor_tensor(acc[:, :], acc[:, :], ps[:, 0:4, :].rearrange("p a b -> p (a b)"), ALU.add).then_inc(s("final"), 1)
                dve.wait_ge(s("final"), 1)
            else:
                dve.wait_ge(s("turned"), 1)
                v.tensor_tensor(xT[:, :], xT[:, :], ps[:, 0:4, :].rearrange("p a b -> p (a b)"), ALU.add).then_inc(s("final"), 1)
                dve.wait_ge(s("final"), 1)


SEG = 3 * P


def softmax_group(nc, dve, s, g, buf, env, probs, stat, scale):
    const, ps = env["const"], env["ps"]
    v = nc.vector
    p = probs[:, buf * 4 * SEG:(buf + 1) * 4 * SEG].rearrange("p (u k) -> p u k", u=4)
    first, second = p[:, :, 0:P], p[:, :, P:SEG]
    top, total, inverse = (stat[:, (buf * 3 + i) * 8:(buf * 3 + i + 1) * 8] for i in range(3))
    each = lambda ap, part: ap[:, 4 * part:4 * part + 4].unsqueeze(2).broadcast_to([P, 4, P * (part + 1)])
    mask = const[:, K_CAUSAL:K_CAUSAL + SEG].unsqueeze(1).broadcast_to([P, 4, SEG])
    dve.wait_ge(s("scores_ps"), g + 1)
    v.scalar_tensor_tensor(p, ps[:, 0:4, 0:SEG], scale, mask, ALU.mult, ALU.add).then_inc(s("masked"), 1)
    dve.wait_ge(s("masked"), g + 2)
    v.tensor_reduce(top[:, 0:4], first, AX, ALU.max)
    v.tensor_reduce(top[:, 4:8], second, AX, ALU.max).then_inc(s("max"), 1)
    dve.wait_ge(s("max"), g + 1)
    v.tensor_tensor(first, first, each(top, 0), ALU.subtract)
    v.tensor_tensor(second, second, each(top, 1), ALU.subtract).then_inc(s("centred"), 1)
    dve.wait_ge(s("exp"), g + 1)
    v.tensor_reduce(total[:, 0:4], first, AX, ALU.add)
    v.tensor_reduce(total[:, 4:8], second, AX, ALU.add).then_inc(s("sum"), 1)
    dve.wait_ge(s("sum"), g + 1)
    v.reciprocal(inverse, total).then_inc(s("inverse"), 1)
    dve.wait_ge(s("inverse"), g + 1)
    v.tensor_tensor(first, first, each(inverse, 0), ALU.mult)
    v.tensor_tensor(second, second, each(inverse, 1), ALU.mult).then_inc(s("probs"), 1)


def turn_probs(nc, pe, s, g, buf, env, probs):
    ps, ident = env["ps"], env["const"][:, K_ID:K_ID + P]
    pe.wait_ge(s("probs"), g + 1)
    for piece in range(3):
        for u in range(4):
            c = (buf * 4 + u) * SEG + piece * P
            last = nc.tensor.transpose(ps[:, 4 + piece, u * P:(u + 1) * P], probs[:, c:c + P], ident)
    last.then_inc(s("turned"), 1)


def attention1(nc, a, env):
    xT, const, hT, ps = (env[k] for k in ("xT", "const", "hT", "ps"))
    HD = 16
    with ExitStack() as ctx:
        s = Signals(nc, ctx, env, "a1")
        sb = lambda name, cols: ctx.enter_context(nc.sbuf_tensor(name, [P, cols], F32))
        wkv = sb("wkv", 4 * P)
        wq = sb("wq", 2 * P)
        wo = sb("wo1", C)
        kT = sb("kT", N)
        qT = sb("qT", N)
        plain = sb("plain", N)
        spin = sb("spin", N)
        values = sb("values", N)
        probs = sb("probs", 2 * 4 * SEG)
        probs_t = sb("probs_t", 2 * 4 * SEG)
        stat = sb("stat1", 48)
        oT = sb("oT", N)
        block = ctx.enter_context(nc.Block())
        flat = lambda ap: ap.rearrange("p a b -> p (a b)")
        by_batch = lambda ap: ap.rearrange("p (b t) -> p b t", b=B)
        packs = a["att1"]

        @block.sync
        def _(sp):
            sp.dma_start(wkv[:, :], a["att1_kv"]).then_inc(s("kv_weights"), 16)
            sp.dma_start(wq[:, :], packs[0, :, 0:2 * P]).then_inc(s("q_weights"), 16)
            sp.dma_start(wo[:, :], packs[0, :, 2 * P:2 * P + C]).then_inc(s("o_weights"), 16)
            with sp.Fori(0, 3) as t:
                nxt = packs[bass.ds(t + 1, 1)].rearrange("o p n -> p (o n)")
                sp.wait_ge(s("plain_ps"), t + 2)
                sp.dma_start(wq[:, :], nxt[:, 0:2 * P]).then_inc(s("q_weights"), 16)
                sp.wait_ge(s("y_ps"), t + 1)
                sp.dma_start(wo[:, :], nxt[:, 2 * P:2 * P + C]).then_inc(s("o_weights"), 16)

        @block.tensor
        def _(pe):
            mm = nc.tensor.matmul

            def rope(w, n):
                for half in range(2):
                    for kt in range(CT):
                        last = mm(ps[:, half, :], w[:, kt * P:(kt + 1) * P], hT[:, kt * N + half * HN:kt * N + (half + 1) * HN],
                                  start=kt == 0, stop=kt == CT - 1)
                last.then_inc(s("plain_ps"), 1)
                pe.wait_ge(s("plain"), n + 1)
                for half in range(2):
                    last = mm(ps[:, 2 + half, :], const[:, K_ROT1:K_ROT1 + P], plain[:, half * HN:(half + 1) * HN], start=True, stop=True)
                last.then_inc(s("rotated_ps"), 1)

            pe.wait_ge(s("kv_weights"), 16)
            for n in range(NT):
                for kt in range(CT):
                    last = mm(ps[:, 4 + n // 4, (n % 4) * P:(n % 4 + 1) * P], hT[:, kt * N + n * P:kt * N + (n + 1) * P],
                              wkv[:, (2 + kt) * P:(3 + kt) * P], start=kt == 0, stop=kt == CT - 1)
            last.then_inc(s("values_ps"), 1)
            rope(wkv, 0)
            pe.wait_ge(s("roped"), 1)
            pe.wait_ge(s("values"), 1)

            def scores(t, b):
                g = B * t + b
                pe.wait_ge(s("masked"), g + 1)
                if b == 0:
                    pe.wait_ge(s("roped"), t + 2)
                for u in range(4):
                    rows = slice(32 * u, 32 * u + HD)
                    for q, (c, k) in enumerate(((0, P), (P, 2 * P))):
                        last = mm(ps[:, u, c:c + k], qT[rows, b * T + q * P:b * T + (q + 1) * P], kT[rows, b * T:b * T + k],
                                  start=True, stop=True)
                last.then_inc(s("scores_ps"), 1)

            def weigh(t, b):
                g = B * t + b
                pe.wait_ge(s("probs_t"), g + 1)
                pe.wait_ge(s("o"), g + 1)
                for u in range(4):
                    rows = slice(32 * u, 32 * (u + 1))
                    for piece, (tile, q) in enumerate(((0, 0), (0, 1), (1, 1))):
                        c = (b % 2) * 4 * SEG + (piece * 4 + u) * P
                        last = mm(ps[rows, 7, q * P:(q + 1) * P], values[:, (2 * b + tile) * P + 32 * u:(2 * b + tile) * P + 32 * (u + 1)],
                                  probs_t[:, c:c + P], start=piece < 2, stop=piece != 1, skip_group_check=True)
                last.then_inc(s("o_ps"), 1)

            with pe.Fori(0, 4) as t:
                pe.wait_ge(s("q_weights"), 16 * t + 16)
                rope(wq, t + 1)
                for b in range(B + 1):
                    if b < B:
                        scores(t, b)
                    if b:
                        if b == 1:
                            pe.wait_ge(s("x_added"), t + 1)
                        turn_probs(nc, pe, s, B * t + b - 1, (b - 1) % 2, env, probs)
                        weigh(t, b - 1)
                pe.wait_ge(s("o"), B * t + B + 1)
                pe.wait_ge(s("o_weights"), 16 * t + 16)
                for ct in range(CT):
                    for half in range(2):
                        last = mm(ps[:, 4 + 2 * ct + half, :], wo[:, ct * P:(ct + 1) * P], oT[:, half * HN:(half + 1) * HN],
                                  start=True, stop=True)
                last.then_inc(s("y_ps"), 1)

        @block.scalar
        def _(act):
            A = nc.scalar.activation
            act.sem_inc(s("o"), 1)
            act.wait_ge(s("values_ps"), 1)
            A(values[:, :], flat(ps[:, 4:6, :]), ACT.Copy).then_inc(s("values"), 1)
            act.wait_ge(s("plain_ps"), 1)
            A(plain[:, :], flat(ps[:, 0:2, :]), ACT.Copy).then_inc(s("plain"), 1)
            with act.Fori(0, 4) as t:
                act.wait_ge(s("plain_ps"), t + 2)
                act.wait_ge(s("roped"), t + 1)
                A(plain[:, :], flat(ps[:, 0:2, :]), ACT.Copy).then_inc(s("plain"), 1)
                for b in range(B + 1):
                    if b < B:
                        act.wait_ge(s("centred"), B * t + b + 1)
                        p = probs[:, (b % 2) * 4 * SEG:(b % 2 + 1) * 4 * SEG]
                        A(p, p, ACT.Exp).then_inc(s("exp"), 1)
                    if b:
                        g = B * t + b - 1
                        act.wait_ge(s("turned"), g + 1)
                        p = probs_t[:, ((b - 1) % 2) * 4 * SEG:((b - 1) % 2 + 1) * 4 * SEG]
                        A(p, flat(ps[:, 4:7, :]), ACT.Copy).then_inc(s("probs_t"), 1)
                        act.wait_ge(s("o_ps"), g + 1)
                        A(oT[:, (b - 1) * T:b * T], ps[:, 7, 0:T], ACT.Copy).then_inc(s("o"), 1)

        @block.vector
        def _(dve):
            v = nc.vector

            def rope(dst, n):
                cos, sin = (over_batches(const[:, k:k + T]) for k in (K_COS1, K_SIN1))
                dve.wait_ge(s("plain"), n + 1)
                v.tensor_tensor(by_batch(dst[:, :]), by_batch(plain[:, :]), cos, ALU.mult).then_inc(s("cos"), 1)
                dve.wait_ge(s("rotated_ps"), n + 1)
                v.tensor_tensor(by_batch(spin[:, :]), by_batch(flat(ps[:, 2:4, :])), sin, ALU.mult).then_inc(s("sin"), 1)
                dve.wait_ge(s("cos"), n + 1)
                dve.wait_ge(s("sin"), n + 1)
                v.tensor_tensor(dst[:, :], dst[:, :], spin[:, :], ALU.add).then_inc(s("roped"), 1)

            rope(kT, 0)
            dve.sem_inc(s("masked"), 1)
            dve.sem_inc(s("x_added"), 1)
            with dve.Fori(0, 4) as t:
                rope(qT, t + 1)
                for b in range(B):
                    softmax_group(nc, dve, s, B * t + b, b % 2, env, probs, stat, float(HD) ** -0.5)
                dve.wait_ge(s("y_ps"), t + 1)
                v.tensor_tensor(xT[:, :], xT[:, :], flat(ps[:, 4:8, :]), ALU.add).then_inc(s("x_added"), 1)
                dve.wait_ge(s("x_added"), t + 2)


def attention2(nc, a, env):
    const, hT, ps = (env[k] for k in ("const", "hT", "ps"))
    KV, REP = 4, 4
    with ExitStack() as ctx:
        sb = lambda name, cols: ctx.enter_context(nc.sbuf_tensor(name, [P, cols], F32))
        nT = sb("nT", CT * N)
        rmsnorm(nc, env, nT, V_LN)
        s = Signals(nc, ctx, env, "a2")
        wp = sb("wp", (2 + REP) * C)
        wo = sb("wo2", REP * C)
        kT = sb("kT2", N)
        qT = sb("qT2", REP * N)
        plain = sb("plain2", N)
        spin = sb("spin2", N)
        values = sb("values2", N)
        probs = sb("probs2", 2 * 4 * SEG)
        probs_t = sb("probs_t2", 4 * SEG)
        stat = sb("stat2", 48)
        oT = sb("oT2", REP * N)
        block = ctx.enter_context(nc.Block())
        flat = lambda ap: ap.rearrange("p a b -> p (a b)")
        by_batch = lambda ap: ap.rearrange("p (b t) -> p b t", b=B)
        packs = a["att2"]
        WP = (2 + REP) * C
        ROPES = 1 + REP

        @block.sync
        def _(sp):
            sp.dma_start(wp[:, :], packs[0, :, 0:WP]).then_inc(s("p_weights"), 16)
            sp.dma_start(wo[:, :], packs[0, :, WP:WP + REP * C]).then_inc(s("o_weights"), 16)
            with sp.Fori(0, KV - 1) as kv:
                nxt = packs[bass.ds(kv + 1, 1)].rearrange("o p n -> p (o n)")
                sp.wait_ge(s("plain_ps"), ROPES * kv + ROPES)
                sp.dma_start(wp[:, :], nxt[:, 0:WP]).then_inc(s("p_weights"), 16)
                sp.wait_ge(s("y_ps"), 2 * kv + 2)
                sp.dma_start(wo[:, :], nxt[:, WP:WP + REP * C]).then_inc(s("o_weights"), 16)

        @block.tensor
        def _(pe):
            mm = nc.tensor.matmul
            with pe.Fori(0, KV) as kv:
                pe.wait_ge(s("p_weights"), 16 * kv + 16)
                pe.wait_ge(s("h_added"), 2 * kv + 1)
                for n in range(NT):
                    for kt in range(CT):
                        last = mm(ps[:, 6 + n // 4, (n % 4) * P:(n % 4 + 1) * P], nT[:, kt * N + n * P:kt * N + (n + 1) * P],
                                  wp[:, C + kt * P:C + (kt + 1) * P], start=kt == 0, stop=kt == CT - 1)
                last.then_inc(s("values_ps"), 1)
                for r in range(ROPES):
                    n = ROPES * kv + r
                    w = wp[:, (0 if r == 0 else (1 + r) * C):]
                    for half in range(2):
                        for kt in range(CT):
                            last = mm(ps[:, half, :], w[:, kt * P:(kt + 1) * P], nT[:, kt * N + half * HN:kt * N + (half + 1) * HN],
                                      start=kt == 0, stop=kt == CT - 1)
                    last.then_inc(s("plain_ps"), 1)
                    pe.wait_ge(s("plain"), n + 1)
                    pe.wait_ge(s("roped"), n + 1)
                    for half in range(2):
                        last = mm(ps[:, 2 + half, :], const[:, K_ROT2:K_ROT2 + P], plain[:, half * HN:(half + 1) * HN],
                                  start=True, stop=True)
                    last.then_inc(s("rotated_ps"), 1)
                pe.wait_ge(s("values"), kv + 1)

                def scores(j):
                    pe.wait_ge(s("masked"), REP * kv + j + 1)
                    if j == 0:
                        pe.wait_ge(s("roped"), ROPES * kv + ROPES + 1)
                    for u in range(B):
                        for q, (c, k) in enumerate(((0, P), (P, 2 * P))):
                            last = mm(ps[:, u, c:c + k], qT[:, j * N + u * T + q * P:j * N + u * T + (q + 1) * P],
                                      kT[:, u * T:u * T + k], start=True, stop=True)
                    last.then_inc(s("scores_ps"), 1)

                def weigh(j):
                    g = REP * kv + j
                    pe.wait_ge(s("probs_t"), g + 1)
                    for u in range(B):
                        for piece, (tile, q) in enumerate(((0, 0), (0, 1), (1, 1))):
                            c = (piece * 4 + u) * P
                            col = (u % 2) * T + q * P
                            last = mm(ps[:, 4 + u // 2, col:col + P], values[:, (2 * u + tile) * P:(2 * u + tile + 1) * P],
                                      probs_t[:, c:c + P], start=piece < 2, stop=piece != 1, skip_group_check=True)
                    last.then_inc(s("o_ps"), 1)

                for j in range(REP + 1):
                    if j < REP:
                        scores(j)
                    if j:
                        g = REP * kv + j - 1
                        pe.wait_ge(s("o"), g + 1)
                        turn_probs(nc, pe, s, g, (j - 1) % 2, env, probs)
                        weigh(j - 1)
                pe.wait_ge(s("o"), REP * kv + REP + 1)
                pe.wait_ge(s("o_weights"), 16 * kv + 16)
                for ct in range(CT):
                    pe.wait_ge(s("h_added"), 2 * kv + ct + 1)
                    for half in range(2):
                        for j in range(REP):
                            last = mm(ps[:, 6 + half, :], wo[:, j * C + ct * P:j * C + (ct + 1) * P],
                                      oT[:, j * N + half * HN:j * N + (half + 1) * HN], start=j == 0, stop=j == REP - 1)
                    last.then_inc(s("y_ps"), 1)

        @block.scalar
        def _(act):
            A = nc.scalar.activation
            act.sem_inc(s("o"), 1)
            with act.Fori(0, KV) as kv:
                act.wait_ge(s("values_ps"), kv + 1)
                A(values[:, :], flat(ps[:, 6:8, :]), ACT.Copy).then_inc(s("values"), 1)
                for r in range(ROPES):
                    n = ROPES * kv + r
                    act.wait_ge(s("plain_ps"), n + 1)
                    act.wait_ge(s("roped"), n + 1)
                    A(plain[:, :], flat(ps[:, 0:2, :]), ACT.Copy).then_inc(s("plain"), 1)
                for j in range(REP + 1):
                    if j < REP:
                        act.wait_ge(s("centred"), REP * kv + j + 1)
                        p = probs[:, (j % 2) * 4 * SEG:(j % 2 + 1) * 4 * SEG]
                        A(p, p, ACT.Exp).then_inc(s("exp"), 1)
                    if j:
                        g = REP * kv + j - 1
                        act.wait_ge(s("turned"), g + 1)
                        A(probs_t[:, :], flat(ps[:, 4:7, :]), ACT.Copy).then_inc(s("probs_t"), 1)
                        act.wait_ge(s("o_ps"), g + 1)
                        A(oT[:, (j - 1) * N:j * N], flat(ps[:, 4:6, :]), ACT.Copy).then_inc(s("o"), 1)

        @block.vector
        def _(dve):
            v = nc.vector
            cos, sin = (over_batches(const[:, k:k + T]) for k in (K_COS2, K_SIN2))
            for free in ("masked", "roped", "h_added"):
                dve.sem_inc(s(free), 1)
            with dve.Fori(0, KV) as kv:
                for r in range(ROPES):
                    n = ROPES * kv + r
                    dst = kT[:, :] if r == 0 else qT[:, (r - 1) * N:r * N]
                    dve.wait_ge(s("plain"), n + 1)
                    v.tensor_tensor(by_batch(dst), by_batch(plain[:, :]), cos, ALU.mult).then_inc(s("cos"), 1)
                    dve.wait_ge(s("rotated_ps"), n + 1)
                    v.tensor_tensor(by_batch(spin[:, :]), by_batch(flat(ps[:, 2:4, :])), sin, ALU.mult).then_inc(s("sin"), 1)
                    dve.wait_ge(s("cos"), n + 1)
                    dve.wait_ge(s("sin"), n + 1)
                    v.tensor_tensor(dst, dst, spin[:, :], ALU.add).then_inc(s("roped"), 1)
                for j in range(REP):
                    softmax_group(nc, dve, s, REP * kv + j, j % 2, env, probs, stat, float(P) ** -0.5)
                for ct in range(CT):
                    dve.wait_ge(s("y_ps"), 2 * kv + ct + 1)
                    c = slice(ct * N, (ct + 1) * N)
                    v.tensor_tensor(hT[:, c], hT[:, c], flat(ps[:, 6:8, :]), ALU.add).then_inc(s("h_added"), 1)
                dve.wait_ge(s("h_added"), 2 * kv + 3)



def constants():
    k = np.zeros((P, K_COLS), np.float32)
    k[:, K_ID:K_ID + P] = np.eye(P)
    i = np.arange(P)
    for l in range(LEVELS):
        k[:, K_MASK + l * P:K_MASK + (l + 1) * P] = ((i[:, None] >> (l + 1)) == (i[None] >> (l + 1))) & ((i[:, None] >> l) % 2 == 0) & ((i[None] >> l) % 2 == 1)
    k[:, K_RANK:K_RANK + 8] = np.arange(8, 0, -1)
    later = (i[None] > i[:, None]) * -BIG
    k[:, K_CAUSAL:K_CAUSAL + P] = later
    k[:, K_CAUSAL + 2 * P:K_CAUSAL + 3 * P] = later
    t = np.arange(T, dtype=np.float32)
    hd = 16
    f = (np.float32(1.0) / np.float32(10000.0) ** (np.arange(0, hd, 2, dtype=np.float32) / np.float32(hd))).astype(np.float32)
    ang = np.tile((t[:, None] * f[None]).astype(np.float32), (1, 2)).T
    for g in range(4):
        k[32 * g:32 * g + hd, K_COS1:K_COS1 + T] = np.cos(ang)
        k[32 * g:32 * g + hd, K_SIN1:K_SIN1 + T] = np.sin(ang)
        for d in range(hd):
            src, sign = (d + 8, -1) if d < 8 else (d - 8, 1)
            k[32 * g + src, K_ROT1 + 32 * g + d] = sign
    f = (np.float32(1000000.0) ** (-np.arange(0, P, 2, dtype=np.float32) / np.float32(P))).astype(np.float32)
    ang = np.repeat((t[:, None] * f[None]).astype(np.float32), 2, axis=1).T
    k[:, K_COS2:K_COS2 + T] = np.cos(ang)
    k[:, K_SIN2:K_SIN2 + T] = np.sin(ang)
    for d in range(0, P, 2):
        k[d + 1, K_ROT2 + d] = -1
        k[d, K_ROT2 + d + 1] = 1
    return k


def rows(w):
    return w.reshape(-1, P, w.shape[-1]).transpose(1, 0, 2)


def flat_rows(w):
    return rows(w).reshape(P, -1)


def layout(inp):
    g = lambda name: np.asarray(inp[name])
    out = {}
    out["xT"] = flat_rows(g("x").reshape(N, C).T)
    out["fT"] = flat_rows(g("fside_BxSxS_0").reshape(N, C).T)
    out["emb"] = g("cond_512").reshape(-1)
    out["const"] = constants()
    vec = np.zeros((P, V_COLS), np.float32)
    for i, name in enumerate(("L0_cond", "L0_cond2", "L1_cond", "L1_cond2")):
        vec[:, V_W + 2 * i:V_W + 2 * i + 2] = g(name + "_w").reshape(CT, P).T
        vec[:, V_U + 2 * i:V_U + 2 * i + 2] = g(name + "_u").reshape(CT, P).T
    vec[:, V_NORM] = g("L0_attn_norm_w")
    vec[:, V_LN:V_LN + 2] = g("L1_ffn_ln_w").reshape(CT, P).T
    vec[:, V_FFLN:V_FFLN + 2] = g("L1_ffn_ff_ln_w").reshape(CT, P).T
    vec[:, V_GATE0:V_GATE0 + 16] = flat_rows(g("L0_ffn_gate_w").T)
    vec[:, V_GATE1:V_GATE1 + 16] = flat_rows(g("L1_ffn_gate_w"))
    out["vec"] = vec
    out["f1g1"] = np.concatenate([flat_rows(g("L0_attn_Wf1")), flat_rows(g("L0_attn_Wg1"))], axis=1)
    gsa = np.zeros((GH, P, G_COLS), np.float32)
    for h in range(GH):
        c = slice(h * P, (h + 1) * P)
        for key, name in (("q", "Wq"), ("k", "Wk"), ("v", "Wv"), ("w", "Ww")):
            gsa[h, :, G_W[key]:G_W[key] + 2 * P] = flat_rows(g("L0_attn_" + name)[:, c])
        gsa[h, :, G_W["f"]:G_W["f"] + P] = g("L0_attn_Wf2")[:, c]
        gsa[h, :, G_W["g"]:G_W["g"] + P] = g("L0_attn_Wg2")[:, c]
        gsa[h, :, G_W["o"]:G_W["o"] + C] = g("L0_attn_Wo")[c]
        for j, name in enumerate(("cq", "ck", "cv")):
            gsa[h, :, G_W["conv"] + 4 * j:G_W["conv"] + 4 * j + 4] = g("L0_attn_" + name)[c]
        gsa[h, :, G_W["bg"]] = g("L0_attn_bg2")[c]
        gsa[h, :, G_W["beta"]:G_W["beta"] + 2] = g("L0_attn_Wb")[:, h].reshape(CT, P).T
    out["gsa"] = gsa
    layout_rest(g, out)
    return out

def layout_rest(g, out):
    kv = np.zeros((P, 4 * P), np.float32)
    for kt in range(CT):
        for h in range(4):
            c = kt * P + 32 * h
            kv[:, c:c + 16] = g("L1_attn_wk")[kt * P:(kt + 1) * P, 16 * h:16 * h + 16]
            kv[:, 2 * P + c:2 * P + c + 16] = g("L1_attn_wv")[kt * P:(kt + 1) * P, 16 * h:16 * h + 16]
    out["att1_kv"] = kv
    att1 = np.zeros((4, P, 2 * P + C), np.float32)
    for t in range(4):
        for u in range(4):
            h = 4 * u + t
            for kt in range(CT):
                att1[t, :, kt * P + 32 * u:kt * P + 32 * u + 16] = g("L1_attn_wq")[kt * P:(kt + 1) * P, 16 * h:16 * h + 16]
            att1[t, 32 * u:32 * u + 16, 2 * P:] = g("L1_attn_wo")[16 * h:16 * h + 16]
    out["att1"] = att1
    att2 = []
    for kv in range(4):
        c = slice(kv * P, (kv + 1) * P)
        heads = [slice(h * P, (h + 1) * P) for h in range(4 * kv, 4 * kv + 4)]
        att2.append(np.concatenate([flat_rows(g("L1_ffn_wk")[:, c]), flat_rows(g("L1_ffn_wv")[:, c])]
                                   + [flat_rows(g("L1_ffn_wq")[:, h]) for h in heads]
                                   + [g("L1_ffn_wo")[h] for h in heads], axis=1))
    out["att2"] = np.stack(att2)
    out["moe0"] = np.stack([np.concatenate([flat_rows(w1.T), flat_rows(w3.T), flat_rows(w2.T)], axis=1)
                            for w1, w3, w2 in zip(g("L0_ffn_w1"), g("L0_ffn_w3"), g("L0_ffn_w2"))])
    out["moe1"] = np.stack([np.concatenate([flat_rows(w1), flat_rows(w3), flat_rows(w2)], axis=1)
                            for w1, w3, w2 in zip(g("L1_ffn_w1"), g("L1_ffn_w3"), g("L1_ffn_w2"))])



def kernel(**inputs):
    import concourse.bacc as bacc
    from concourse.bass_utils import run_bass_kernel_spmd

    nc = bacc.Bacc("TRN2", target_bir_lowering=False, num_devices=1)
    arrays = {f"in_{n}": np.ascontiguousarray(v) for n, v in layout(inputs).items()}
    args = {n[3:]: nc.dram_tensor(n, v.shape, mybir.dt.from_np(v.dtype), kind="ExternalInput").ap() for n, v in arrays.items()}
    args["out"] = nc.dram_tensor("out", (N, C), F32, kind="ExternalOutput").ap()
    build(nc, args)
    r = run_bass_kernel_spmd(nc, [arrays], core_ids=[0])
    return r.results[0]["out"].reshape(B, T, C)
```

```python
from contextlib import ExitStack

import numpy as np

import concourse.bass as bass
from concourse import mybir

F32 = mybir.dt.float32
F32R = mybir.dt.float32r
ALU = mybir.AluOpType
ACT = mybir.ActivationFunctionType
AX = mybir.AxisListType.X

P = 128
B, T, C, TD = 4, 256, 256, 64
N = B * T
CT = C // P
NT = N // P
HN = N // 2
NCOND = 4

GH, GK, LEVELS, KW = 16, 2, 8, 4
G_W = dict(q=0, k=256, v=512, w=768, f=1024, g=1152, o=1280, conv=1536, bg=1548)
G_COLS = 1552
BIG = 1e30

K_ID, K_MASK, K_CAUSAL = 0, 128, 128 + LEVELS * 128
K_COS1 = K_CAUSAL + 384
K_SIN1, K_COS2, K_SIN2 = K_COS1 + T, K_COS1 + 2 * T, K_COS1 + 3 * T
K_ROT1 = K_COS1 + 4 * T
K_ROT2 = K_ROT1 + P
K_RANK = K_ROT2 + P
K_COLS = K_RANK + 8

V_W, V_U, V_NORM, V_LN, V_FFLN = 0, 8, 16, 17, 19
V_GATE0, V_GATE1 = 21, 37
V_COLS = 53

A_Q, A_K, A_V, A_O = 0, 1024, 1280, 1408
A_COLS = A_O + 4 * C
F_K, F_V, F_COLS = 0, 1024, 2048


class Signals:

    def __init__(self, nc, ctx, env, stage):
        self.nc, self.ctx, self.stage, self.known = nc, ctx, stage, {}
        env["signals"].append(self)

    def __call__(self, name):
        if name not in self.known:
            self.known[name] = self.ctx.enter_context(self.nc.semaphore(f"{self.stage}_{name}"))
        return self.known[name]


def clear_signals(nc, env):
    with nc.Block() as block:
        @block.gpsimd
        def _(pool):
            for signals in env["signals"]:
                for semaphore in signals.known.values():
                    nc.gpsimd.sem_clear(semaphore)
    env["signals"].clear()


def halves(ap, level):
    h = 1 << level
    v = ap.rearrange("p (n two h) -> p n two h", two=2, h=h)
    return v[:, :, 0, :], v[:, :, 1, :]


def packed(ap, level):
    return ap.rearrange("p (n h) -> p n h", h=1 << level)


def over_batches(ap, n=B):
    return ap.unsqueeze(1).broadcast_to([ap.shape[0], n, ap.shape[1]])


def build(nc, a):
    with ExitStack() as ctx:
        env = shared(nc, ctx)
        condition(nc, a, env, 0)
        slot_attention(nc, a, env)
        clear_signals(nc, env)
        condition(nc, a, env, 1)
        moe(nc, a, env, 0)
        condition(nc, a, env, 2)
        attention1(nc, a, env)
        clear_signals(nc, env)
        condition(nc, a, env, 3)
        attention2(nc, a, env)
        moe(nc, a, env, 1)


def shared(nc, ctx):
    keep = lambda name, cols: ctx.enter_context(nc.sbuf_tensor(name, [P, cols], F32))
    return dict(
        xT=keep("xT", CT * N),
        hT=keep("hT", CT * N),
        const=keep("const", K_COLS),
        vec=keep("vec", V_COLS),
        tf=keep("tf", 3 * B),
        dec=keep("dec", 8 * B),
        ones=keep("ones", P),
        eps=keep("eps", 4),
        ps=ctx.enter_context(nc.psum_tensor("ps", [P, 8, 512], F32)),
        signals=[],
    )


def condition(nc, a, env, i):
    xT, const, vec, hT, ones, eps, tf, dec = (env[k] for k in ("xT", "const", "vec", "hT", "ones", "eps", "tf", "dec"))
    with ExitStack() as ctx:
        s = Signals(nc, ctx, env, f"cond{i}")
        sb = lambda name, cols: ctx.enter_context(nc.sbuf_tensor(f"{name}_c{i}", [P, cols], F32))
        fT = sb("fT", CT * N)
        emb = sb("emb", B * TD)
        dw = sb("dw", 2 * 8)
        ek = sb("ek", CT * N)
        ekv = sb("ekv", CT * N)
        bonus = sb("bonus", CT * N)
        bonus_v = sb("bonus_v", CT * N)
        gate = sb("r_gate", CT * N)
        sc = sb("sc", CT * 4 * N)
        block = ctx.enter_context(nc.Block())
        tile = lambda t, ct: t[:, ct * N:(ct + 1) * N]
        scan = lambda ct, n: sc[:, (ct * 4 + n) * N:(ct * 4 + n + 1) * N]
        by_batch = lambda ap: ap.rearrange("p (c b t) -> p c b t", c=CT, b=B)
        first = i == 0

        @block.sync
        def _(sp):
            sp.dma_start(fT[:, :], a["fT"]).then_inc(s("f_loaded"), 16)
            if first:
                sp.dma_start(vec[:, :], a["vec"]).then_inc(s("vec_loaded"), 16)
                sp.dma_start(emb[:, :], a["emb"].partition_broadcast(P)).then_inc(s("vec_loaded"), 16)
                sp.dma_start(xT[:, :], a["xT"]).then_inc(s("x_loaded"), 16)
                sp.dma_start(const[:, :], a["const"]).then_inc(s("const_loaded"), 16)
                sp.wait_ge(s("const_loaded"), 16)

        @block.scalar
        def _(act):
            A = nc.scalar.activation
            if first:
                act.wait_ge(s("emb_sum"), 1)
                A(tf[:, 0:B], tf[:, 0:B], ACT.Sigmoid).then_inc(s("tf"), 1)
                act.wait_ge(s("x_loaded"), 16)
            A(gate[:, :], xT[:, :], ACT.Sigmoid).then_inc(s("r_sigmoid"), 1)
            if first:
                act.wait_ge(s("vec_loaded"), 32)
                A(dw[:, 0:8], vec[:, V_W:V_W + 8], ACT.Exp).then_inc(s("exp_w"), 1)
                act.wait_ge(s("exp_w"), 1)
                A(dw[:, 8:16], dw[:, 0:8], ACT.Exp, scale=-1.0).then_inc(s("decay_w"), 1)
            act.wait_ge(s("k_min"), 1)
            A(ek[:, :], ek[:, :], ACT.Exp).then_inc(s("ek"), 1)
            act.wait_ge(s("uk_min"), CT)
            A(bonus[:, :], bonus[:, :], ACT.Exp).then_inc(s("euk"), 1)
            for ct in range(CT):
                act.wait_ge(s("den"), ct + 1)
                A(scan(ct, 3), scan(ct, 2), ACT.Ln).then_inc(s("log"), 1)
                act.wait_ge(s("log"), ct + 1)
                A(scan(ct, 3), scan(ct, 3), ACT.Exp, scale=-1.0).then_inc(s("near"), 1)

        @block.gpsimd
        def _(pool):
            g = nc.gpsimd
            if first:
                g.memset(ones[:, :], 1.0).then_inc(s("ones"), 1)
                g.memset(eps[:, 0:1], 1e-6).then_inc(s("ones"), 1)
                g.memset(eps[:, 1:2], 1e-5).then_inc(s("ones"), 1)
                pool.wait_ge(s("ones"), 3)
            pool.wait_ge(s("f_loaded"), 16)
            pool.wait_ge(s("ek"), 1)
            pool.wait_ge(s("euk"), 1)
            g.tensor_tensor(bonus[:, :], bonus[:, :], ek[:, :], ALU.subtract).then_inc(s("bonus"), 1)
            pool.wait_ge(s("bonus"), 1)
            g.tensor_tensor(bonus_v[:, :], bonus[:, :], fT[:, :], ALU.mult).then_inc(s("bonus_v"), 1)
            pool.wait_ge(s("r_sigmoid"), 1)
            if first:
                pool.wait_ge(s("tf_parts"), 2)
            w = tf[:, 2 * B:3 * B].unsqueeze(1).unsqueeze(3).broadcast_to([P, CT, B, T])
            g.tensor_tensor(by_batch(gate[:, :]), by_batch(gate[:, :]), w, ALU.mult).then_inc(s("r_gate"), 1)
            for ct in range(CT):
                pool.wait_ge(s("den_scans"), ct + 1)
                g.tensor_tensor(scan(ct, 2), scan(ct, 2), scan(ct, 3), ALU.add).then_inc(s("den_step"), 1)
                pool.wait_ge(s("den_step"), 2 * ct + 1)
                g.tensor_tensor(scan(ct, 2), scan(ct, 2), tile(bonus, ct), ALU.add).then_inc(s("den_step"), 1)
                pool.wait_ge(s("den_step"), 2 * ct + 2)
                g.tensor_scalar(scan(ct, 2), scan(ct, 2), 1e-8, 1.0, ALU.max, ALU.mult).then_inc(s("den"), 1)

        @block.vector
        def _(dve):
            v = nc.vector
            if first:
                dve.wait_ge(s("vec_loaded"), 32)
                v.tensor_reduce(tf[:, 0:B], emb[:, :].rearrange("p (b d) -> p b d", b=B), AX, ALU.add).then_inc(s("emb_sum"), 1)
            dve.wait_ge(s("f_loaded"), 16)
            v.tensor_scalar(ek[:, :], fT[:, :], 30.0, None, ALU.min).then_inc(s("k_min"), 1)
            for ct in range(CT):
                u = vec[:, V_U + 2 * i + ct:V_U + 2 * i + ct + 1]
                v.tensor_scalar(tile(bonus, ct), tile(fT, ct), u, 30.0, ALU.add, ALU.min).then_inc(s("uk_min"), 1)
            if first:
                dve.wait_ge(s("tf"), 1)
                v.tensor_scalar(tf[:, B:2 * B], tf[:, 0:B], 0.5, 0.5, ALU.mult, ALU.add).then_inc(s("tf_parts"), 1)
                v.tensor_scalar(tf[:, 2 * B:3 * B], tf[:, 0:B], 0.2, 0.8, ALU.mult, ALU.add).then_inc(s("tf_parts"), 1)
                dve.wait_ge(s("tf_parts"), 2)
                dve.wait_ge(s("decay_w"), 1)
                for b in range(B):
                    v.tensor_scalar(dec[:, b * 8:(b + 1) * 8], dw[:, 8:16], tf[:, B + b:B + b + 1], None,
                                    ALU.mult).then_inc(s("decay"), 1)
                dve.wait_ge(s("decay"), B)
            dve.wait_ge(s("ek"), 1)
            v.tensor_tensor(ekv[:, :], ek[:, :], fT[:, :], ALU.mult).then_inc(s("ekv"), 1)
            for ct in range(CT):
                for n, src in ((2, ek), (0, ekv)):
                    if src is ekv:
                        dve.wait_ge(s("ekv"), 1)
                    for b in range(B):
                        d = dec[:, b * 8 + 2 * i + ct:b * 8 + 2 * i + ct + 1].broadcast_to([P, T])
                        k = tile(src, ct)[:, b * T:(b + 1) * T]
                        fwd, bwd = (scan(ct, n + m)[:, b * T:(b + 1) * T] for m in range(2))
                        v.tensor_tensor_scan(fwd, d, k, 0.0, ALU.mult, ALU.add)
                        last = v.tensor_tensor_scan(bwd[:, ::-1], d, k[:, ::-1], 0.0, ALU.mult, ALU.add)
                    last.then_inc(s("den_scans" if n else "num_scans"), 1)
                dve.wait_ge(s("num_scans"), ct + 1)
                v.tensor_tensor(scan(ct, 0), scan(ct, 0), scan(ct, 1), ALU.add).then_inc(s("num_step"), 1)
                dve.wait_ge(s("num_step"), 2 * ct + 1)
                dve.wait_ge(s("bonus_v"), 1)
                v.tensor_tensor(scan(ct, 0), scan(ct, 0), tile(bonus_v, ct), ALU.add).then_inc(s("num_step"), 1)
                dve.wait_ge(s("num_step"), 2 * ct + 2)
                if ct == 0:
                    dve.wait_ge(s("r_gate"), 1)
                v.tensor_tensor(scan(ct, 0), scan(ct, 0), tile(gate, ct), ALU.mult).then_inc(s("num"), 1)
            for ct in range(CT):
                dve.wait_ge(s("near"), ct + 1)
                v.tensor_tensor(scan(ct, 2), scan(ct, 2), scan(ct, 3), ALU.mult).then_inc(s("newton"), 1)
                dve.wait_ge(s("newton"), 2 * ct + 1)
                v.scalar_tensor_tensor(scan(ct, 2), scan(ct, 2), 2.0, scan(ct, 3), ALU.subtract, ALU.mult).then_inc(s("newton"), 1)
                dve.wait_ge(s("newton"), 2 * ct + 2)
                dve.wait_ge(s("num"), ct + 1)
                v.scalar_tensor_tensor(tile(hT, ct), scan(ct, 0), -1.0, scan(ct, 2), ALU.mult, ALU.mult).then_inc(s("h"), 1)
            dve.wait_ge(s("h"), CT)


def slot_attention(nc, a, env):
    xT, const, vec, hT, ones, eps, ps = (env[k] for k in ("xT", "const", "vec", "hT", "ones", "eps", "ps"))
    SCALE = float(P) ** -0.5
    ident = const[:, K_ID:K_ID + P]
    PROJ = ("w", "k", "q", "v", "f", "g")
    CONV = ("w", "k", "q", "v")
    TAPS = dict(q=0, k=4, v=8, w=8)
    NPROJ, NCONV = len(PROJ), len(CONV)
    with ExitStack() as ctx:
        s = Signals(nc, ctx, env, "gsa")
        sb = lambda name, cols, dt=F32: ctx.enter_context(nc.sbuf_tensor(name, [P, cols], dt))
        wt = sb("wt", G_W["o"])
        wo = sb("wo", C)
        small = sb("small", G_COLS - G_W["conv"])
        low_w = sb("low_w", 2 * CT * P + CT * GH)
        low = sb("low", 2 * N)
        raw = sb("raw", 2 * B * (T + KW - 1))
        y = sb("y", 2 * NCONV * N)
        prefix = sb("prefix", 2 * N)
        gate = sb("gate", 2 * N)
        beta = sb("beta", N)
        front_sum = sb("front_sum", N)
        suffix = sb("suffix", N)
        rnorm = sb("rnorm", N)
        writes = sb("writes", LEVELS * N)
        pre = sb("pre", LEVELS * HN)
        kq = sb("kq", N + HN)
        pairs = sb("pairs", 2 * HN)
        wt_t = sb("wt_t", 2 * N)
        v_t = sb("v_t", N)
        score = sb("score", N)
        sm = sb("sm", N)
        tmp = sb("tmp", N)
        stat = sb("stat", 3 * NT)
        zero = sb("zero", P + 512, mybir.dt.bfloat16)
        beta_dram = nc.dram_tensor("beta_all", (GH, N), F32).ap()
        block = ctx.enter_context(nc.Block())

        own = kq[:, 0:N]
        Y = lambda p, name: y[:, (p * NCONV + CONV.index(name)) * N:(p * NCONV + CONV.index(name) + 1) * N]
        raws = raw[:, :].rearrange("p (j b t) -> p j b t", j=2, b=B)
        of = lambda buf, p: buf[:, p * N:(p + 1) * N]
        pair = lambda j: ps[:, 2 * j:2 * j + 2, :].rearrange("p a b -> p (a b)")
        by_batch = lambda ap: ap.rearrange("p (b t) -> p b t", b=B)
        packs = a["gsa"]

        def heads(engine, body):
            with engine.Fori(0, GH // 2 - 1) as i:
                body(2 * i, 0, True)
                body(2 * i + 1, 1, True)
            body(GH - 2, 0, True)
            body(GH - 1, 1, False)

        @block.sync
        def _(sp):
            sp.dma_start(low_w[:, :], a["low_w"]).then_inc(s("low_weights"), 16)
            sp.dma_start(wt[:, :], packs[0, :, 0:G_W["o"]]).then_inc(s("proj_weights"), 16)
            sp.dma_start(small[:, :], packs[0, :, G_W["conv"]:G_COLS]).then_inc(s("small_weights"), 16)
            sp.dma_start(wo[:, :], packs[0, :, G_W["o"]:G_W["conv"]]).then_inc(s("out_weights"), 16)
            sp.wait_ge(s("beta_all"), 1)
            sp.dma_start(beta_dram, tmp[0:GH, :]).then_inc(s("beta_stored"), 16)
            sp.wait_ge(s("beta_stored"), 16)
            sp.dma_start(beta[:, :], beta_dram[0].partition_broadcast(P)).then_inc(s("beta"), 16)

            def load(f):
                nxt = packs[bass.ds(f + 1, 1)].rearrange("o p n -> p (o n)")
                sp.wait_ge(s("proj"), NPROJ * f + NPROJ)
                sp.dma_start(wt[:, :], nxt[:, 0:G_W["o"]]).then_inc(s("proj_weights"), 16)
                sp.wait_ge(s("conv"), NCONV * f + NCONV)
                sp.wait_ge(s("proj_out"), NPROJ * f + NPROJ)
                sp.dma_start(small[:, :], nxt[:, G_W["conv"]:G_COLS]).then_inc(s("small_weights"), 16)
                sp.wait_ge(s("w_beta"), f + 1)
                row = beta_dram[bass.ds(f + 1, 1)].rearrange("o n -> (o n)")
                sp.dma_start(beta[:, :], row.partition_broadcast(P)).then_inc(s("beta"), 16)

            def load_out(h):
                own_out = packs[bass.ds(h, 1)].rearrange("o p n -> p (o n)")
                sp.wait_ge(s("y_out"), h)
                sp.dma_start(wo[:, :], own_out[:, G_W["o"]:G_W["conv"]]).then_inc(s("out_weights"), 16)

            load(0)
            with sp.Fori(1, GH - 1) as f:
                load(f)
                load_out(f)
            load_out(GH - 1)

        @block.tensor
        def _(pe):
            mm = nc.tensor.matmul

            def ones_sum(banks, src):
                for half in range(2):
                    last = mm(ps[:, banks + half, :], ones[:, :], src[:, half * HN:(half + 1) * HN], start=True, stop=True)
                return last

            def project(f, j):
                name = PROJ[j]
                if j == 0:
                    pe.wait_ge(s("proj_weights"), 16 * f + 16)
                else:
                    pe.wait_ge(s("proj_out"), NPROJ * f + j)
                for half in range(2):
                    cols = slice(half * HN, (half + 1) * HN)
                    if name in "fg":
                        base = (name == "g") * N
                        last = mm(ps[:, 6 + half, :], wt[:, G_W[name]:G_W[name] + P],
                                  low[:, base + half * HN:base + (half + 1) * HN], start=True, stop=True)
                    else:
                        for kt in range(CT):
                            last = mm(ps[:, 6 + half, :], wt[:, G_W[name] + kt * P:G_W[name] + (kt + 1) * P],
                                      hT[:, kt * N + half * HN:kt * N + (half + 1) * HN], start=kt == 0, stop=kt == CT - 1)
                last.then_inc(s("proj"), 1)

            def w_norm(f):
                pe.wait_ge(s("w_squared"), f + 1)
                ones_sum(4, front_sum).then_inc(s("w_norm_ps"), 1)

            pe.wait_ge(s("low_weights"), 16)
            for half in range(2):
                for kt in range(CT):
                    last = mm(ps[0:GH, 4 + half, :], low_w[:, 2 * CT * P + kt * GH:2 * CT * P + (kt + 1) * GH],
                              hT[:, kt * N + half * HN:kt * N + (half + 1) * HN], start=kt == 0, stop=kt == CT - 1)
            last.then_inc(s("beta_ps"), 1)
            for j in range(2):
                for half in range(2):
                    for kt in range(CT):
                        last = mm(ps[:, 2 * j + half, :], low_w[:, (j * CT + kt) * P:(j * CT + kt + 1) * P],
                                  hT[:, kt * N + half * HN:kt * N + (half + 1) * HN], start=kt == 0, stop=kt == CT - 1)
                last.then_inc(s("low_ps"), 1)
            pe.wait_ge(s("low"), 2)
            pe.wait_ge(s("zero"), 1)
            for j in range(NPROJ):
                project(0, j)
            w_norm(0)

            def head(h, p, more):
                pe.wait_ge(s("qk"), h + 1)
                ones_sum(6, front_sum).then_inc(s("qk_ps"), 1)
                pe.wait_ge(s("x_added"), h + 1)
                for n in range(NT):
                    mm(ps[:, n // 4, (n % 4) * P:(n % 4 + 1) * P], Y(p, "k")[:, n * P:(n + 1) * P],
                       Y(p, "q")[:, n * P:(n + 1) * P], start=True, stop=True)
                for b in range(B):
                    last = mm(ps[:, 2, b * P:(b + 1) * P], Y(p, "k")[:, b * T:b * T + P],
                              Y(p, "q")[:, b * T + P:(b + 1) * T], start=True, stop=True)
                last.then_inc(s("kq_ps"), 1)
                pe.wait_ge(s("w_log"), h + 1)
                for n in range(NT):
                    last = nc.tensor.transpose(ps[:, 4 + n // 4, (n % 4) * P:(n % 4 + 1) * P], Y(p, "v")[:, n * P:(n + 1) * P], ident)
                last.then_inc(s("v_t_ps"), 1)

                def turn(l):
                    n = LEVELS * h + l
                    pe.wait_ge(s("writes"), n + 1)
                    if l >= 2:
                        pe.wait_ge(s("writes_t"), n - 1)
                    else:
                        pe.wait_ge(s("kq"), h + 1)
                    for i, tile in enumerate(range(NT) if l < LEVELS - 1 else range(0, NT, 2)):
                        c = l * N + tile * P
                        last = nc.tensor.transpose(ps[:, 2 * (l % 2) + i // 4, (i % 4) * P:(i % 4 + 1) * P], writes[:, c:c + P], ident)
                    last.then_inc(s("writes_t_ps"), 1)

                def read(l):
                    n = LEVELS * h + l
                    pe.wait_ge(s("writes_t"), n + 1)
                    if l < 2:
                        pe.wait_ge(s("v_t"), h + 1)
                    else:
                        pe.wait_ge(s("score_level"), n - 1)
                    wt_l = wt_t[:, (l % 2) * N:(l % 2 + 1) * N]
                    if l < LEVELS - 1:
                        pe.wait_ge(s("kq_pairs"), (LEVELS - 1) * h + l + 1)
                        for i in range(NT):
                            c = (l % 2) * HN + i * (P // 2)
                            last = mm(ps[:, 4 + l % 2, i * (P // 2):(i + 1) * (P // 2)], wt_l[:, i * P:(i + 1) * P],
                                      pairs[:, c:c + P // 2], start=True, stop=True)
                    else:
                        for b in range(B):
                            last = mm(ps[:, 4 + l % 2, b * P:(b + 1) * P], wt_l[:, b * P:(b + 1) * P],
                                      kq[:, N + b * P:N + (b + 1) * P], start=True, stop=True)
                    last.then_inc(s("level_ps"), 1)

                for l in range(LEVELS + 1):
                    if l < LEVELS:
                        turn(l)
                    if l >= 1:
                        read(l - 1)
                    if more and 1 <= l <= NPROJ:
                        if l == 1:
                            pe.wait_ge(s("score_diag"), h + 1)
                        project(h + 1, l - 1)

                pe.wait_ge(s("score_level"), LEVELS * h + LEVELS)
                if more:
                    pe.wait_ge(s("proj_out"), NPROJ * h + 2 * NPROJ)
                for n in range(NT):
                    last = nc.tensor.transpose(ps[:, 6 + n // 4, (n % 4) * P:(n % 4 + 1) * P], score[:, n * P:(n + 1) * P], ident)
                last.then_inc(s("score_t"), 1)
                if more:
                    w_norm(h + 1)
                    pe.wait_ge(s("w_log"), h + 2)
                pe.wait_ge(s("softmax"), h + 1)
                for n in range(NT):
                    last = nc.tensor.transpose(ps[:, 4 + n // 4, (n % 4) * P:(n % 4 + 1) * P], sm[:, n * P:(n + 1) * P], ident)
                last.then_inc(s("slots_ps"), 1)
                for half in range(2):
                    mm(ps[:, 6 + half, :], zero[0:1, 0:P], zero[0:1, P:P + 512], start=True, stop=False, skip_group_check=True)

                def products(l):
                    n = LEVELS * h + l
                    pe.wait_ge(s("reads"), n + 1)
                    if l >= 2:
                        pe.wait_ge(s("aw_pairs"), n - 1)
                    w = P // 2 if l < LEVELS - 1 else P
                    for i, tile in enumerate(range(NT) if l < LEVELS - 1 else range(0, NT, 2)):
                        last = mm(ps[:, l % 2, i * w:(i + 1) * w], writes[:, l * N + tile * P:l * N + (tile + 1) * P],
                                  sm[:, (l % 2) * HN + i * w:(l % 2) * HN + (i + 1) * w], start=True, stop=True)
                    last.then_inc(s("aw_pairs_ps"), 1)

                def collect(l):
                    pe.wait_ge(s("aw_pairs"), LEVELS * h + l + 1)
                    c = (l % 2) * HN
                    if l < LEVELS - 1:
                        for i in range(NT):
                            out = halves(ps[:, 6 + i // 4, (i % 4) * P:(i % 4 + 1) * P], l)[1]
                            last = mm(out, v_t[:, i * P:(i + 1) * P], packed(pairs[:, c + i * (P // 2):c + (i + 1) * (P // 2)], l),
                                      start=False, stop=False, skip_group_check=True)
                    else:
                        for b in range(B):
                            i = 2 * b + 1
                            last = mm(ps[:, 6 + i // 4, (i % 4) * P:(i % 4 + 1) * P], v_t[:, 2 * b * P:(2 * b + 1) * P],
                                      pairs[:, c + b * P:c + (b + 1) * P], start=False, stop=True, skip_group_check=True)
                    last.then_inc(s("level_out"), 1)

                for l in range(LEVELS + 1):
                    if l < LEVELS:
                        products(l)
                    if l == 1:
                        pe.wait_ge(s("slot_write"), h + 1)
                        ones_sum(4, tmp).then_inc(s("slot_write_ps"), 1)
                    if l >= 1:
                        collect(l - 1)
                pe.wait_ge(s("o_squared"), h + 1)
                ones_sum(4, tmp).then_inc(s("o_norm_ps"), 1)
                pe.wait_ge(s("o_gated"), h + 1)
                pe.wait_ge(s("out_weights"), 16 * h + 16)
                for ct in range(CT):
                    for half in range(2):
                        last = mm(ps[:, 2 * ct + half, :], wo[:, ct * P:(ct + 1) * P], score[:, half * HN:(half + 1) * HN],
                                  start=True, stop=True)
                last.then_inc(s("y_out"), 1)

            heads(pe, head)

        @block.scalar
        def _(act):
            A = nc.scalar.activation
            act.wait_ge(s("beta_ps"), 1)
            A(tmp[0:GH, :], ps[0:GH, 4:6, :].rearrange("p a b -> p (a b)"), ACT.Sigmoid).then_inc(s("beta_all"), 1)
            for j in range(2):
                act.wait_ge(s("low_ps"), j + 1)
                A(low[:, j * N:(j + 1) * N], pair(j), ACT.Copy).then_inc(s("low"), 1)
            act.wait_ge(s("zero"), 1)

            def take(f, p, j):
                name = PROJ[j]
                if j == 0:
                    act.wait_ge(s("small_weights"), 16 * f + 16)
                act.wait_ge(s("proj"), NPROJ * f + j + 1)
                if name == "f":
                    A(of(prefix, p), pair(3), ACT.Sigmoid).then_inc(s("proj_out"), 1)
                elif name == "g":
                    c = G_W["bg"] - G_W["conv"]
                    A(of(gate, p), pair(3), ACT.Sigmoid, bias=small[:, c:c + 1]).then_inc(s("proj_out"), 1)
                else:
                    if j >= 2:
                        act.wait_ge(s("conv"), NCONV * f + j - 1)
                    A(raws[:, j % 2, :, KW - 1:], by_batch(pair(3)), ACT.Copy)
                    c = TAPS[name] + KW - 1
                    A(Y(p, name), pair(3), ACT.Copy, scale=small[:, c:c + 1]).then_inc(s("proj_out"), 1)

            def finish(f, p):
                for i, name in enumerate(CONV):
                    act.wait_ge(s("conv"), NCONV * f + i + 1)
                    A(Y(p, name), Y(p, name), ACT.Silu).then_inc(s("silu"), 1)
                act.wait_ge(s("silu"), NCONV * f + 1)
                if not isinstance(f, int) or f:
                    act.wait_ge(s("qk_ps"), f)
                A(front_sum[:, :], Y(p, "w"), ACT.Square).then_inc(s("w_squared"), 1)

            def w_log(f):
                act.wait_ge(s("w_norm_ps"), f + 1)
                if not isinstance(f, int) or f > 1:
                    act.wait_ge(s("o_normed"), f - 1)
                A(rnorm[:, :], pair(2), ACT.Ln, bias=eps[:, 0:1]).then_inc(s("w_log"), 1)

            def w_exp(f):
                act.wait_ge(s("w_log"), f + 1)
                A(rnorm[:, :], rnorm[:, :], ACT.Exp, scale=-0.5).then_inc(s("w_rnorm"), 1)

            for j in range(NPROJ):
                take(0, 0, j)
            finish(0, 0)
            w_log(0)
            w_exp(0)

            def head(h, p, more):
                act.wait_ge(s("kq_ps"), h + 1)
                A(kq[:, 0:N], pair(0), ACT.Copy, scale=SCALE)
                A(kq[:, N:], ps[:, 2, :], ACT.Copy, scale=SCALE).then_inc(s("kq"), 1)
                act.wait_ge(s("v_t_ps"), h + 1)
                A(v_t[:, :], pair(2), ACT.Copy).then_inc(s("v_t"), 1)
                for l in range(LEVELS):
                    n = LEVELS * h + l
                    if l:
                        act.wait_ge(s("prefix"), (LEVELS - 1) * h + l)
                    A(packed(pre[:, l * HN:(l + 1) * HN], l), halves(of(prefix, p), l)[1], ACT.Copy).then_inc(s("pre"), 1)
                    act.wait_ge(s("writes_t_ps"), n + 1)
                    if l >= 2:
                        act.wait_ge(s("level_ps"), n - 1)
                    w = N if l < LEVELS - 1 else HN
                    A(wt_t[:, (l % 2) * N:(l % 2) * N + w], pair(l % 2)[:, 0:w], ACT.Copy).then_inc(s("writes_t"), 1)
                    if more and 1 <= l <= NPROJ:
                        take(h + 1, 1 - p, l - 1)
                if more:
                    finish(h + 1, 1 - p)
                act.wait_ge(s("centred"), h + 1)
                A(sm[:, :], sm[:, :], ACT.Exp).then_inc(s("exp"), 1)
                if more:
                    w_log(h + 1)
                act.wait_ge(s("slots_ps"), h + 1)
                A(score[:, :], pair(2), ACT.Copy).then_inc(s("slots"), 1)
                if more:
                    w_exp(h + 1)
                act.wait_ge(s("o"), h + 1)
                A(tmp[:, :], score[:, :], ACT.Square).then_inc(s("o_squared"), 1)
                act.wait_ge(s("o_norm_ps"), h + 1)
                if more:
                    act.wait_ge(s("bw"), h + 2)
                A(rnorm[:, :], pair(2), ACT.Ln, bias=eps[:, 1:2], scale=1.0 / P).then_inc(s("o_log"), 1)
                act.wait_ge(s("o_log"), h + 1)
                A(rnorm[:, :], rnorm[:, :], ACT.Exp, scale=-0.5).then_inc(s("o_rnorm"), 1)

            heads(act, head)

        @block.gpsimd
        def _(pool):
            g = nc.gpsimd
            g.memset(zero[:, :], 0.0)
            g.memset(raw[:, :], 0.0)
            g.memset(writes[:, :], 0.0).then_inc(s("zero"), 1)
            pool.wait_ge(s("zero"), 1)

            def head(h, p, more):
                pool.wait_ge(s("bw"), h + 1)
                for l in range(LEVELS):
                    left, right = halves(of(prefix, p), l)
                    half = [P, N >> (l + 1), 1 << l]
                    sl = halves(suffix[:, :], l)[0]
                    pool.wait_ge(s("suffix"), LEVELS * h + l + 1)
                    g.tensor_tensor(halves(writes[:, l * N:(l + 1) * N], l)[0], halves(Y(p, "w"), l)[0], sl,
                                    ALU.mult).then_inc(s("writes"), 1)
                    if l == LEVELS - 1:
                        break
                    if l:
                        pool.wait_ge(s("prefix"), (LEVELS - 1) * h + l)
                    else:
                        pool.wait_ge(s("proj_out"), NPROJ * h + NPROJ)
                    end = right[:, :, (1 << l) - 1:1 << l].broadcast_to(half)
                    g.tensor_tensor(sl, sl, end, ALU.mult).then_inc(s("suffix"), 1)
                    pool.wait_ge(s("suffix"), LEVELS * h + l + 2)
                    pool.wait_ge(s("pre"), LEVELS * h + l + 1)
                    end = left[:, :, (1 << l) - 1:1 << l].broadcast_to(half)
                    g.tensor_tensor(right, right, end, ALU.mult).then_inc(s("prefix"), 1)
                pool.wait_ge(s("slots"), h + 1)
                for l in range(LEVELS):
                    if l >= 2:
                        pool.wait_ge(s("aw_pairs_ps"), LEVELS * h + l - 1)
                    g.tensor_tensor(packed(sm[:, (l % 2) * HN:(l % 2 + 1) * HN], l), halves(score[:, :], l)[1],
                                    packed(pre[:, l * HN:(l + 1) * HN], l), ALU.mult).then_inc(s("reads"), 1)

            heads(pool, head)

        @block.vector
        def _(dve):
            v = nc.vector
            dve.wait_ge(s("zero"), 1)
            dve.sem_inc(s("x_added"), 1)

            def conv(f, p, j):
                name = CONV[j]
                dve.wait_ge(s("proj_out"), NPROJ * f + j + 1)
                for tap in range(KW - 1):
                    c = TAPS[name] + tap
                    ins = v.scalar_tensor_tensor(by_batch(Y(p, name)), raws[:, j % 2, :, tap:tap + T], small[:, c:c + 1],
                                                 by_batch(Y(p, name)), ALU.mult, ALU.add)
                    if tap < KW - 2:
                        ins.then_inc(s("tap"), 1)
                        dve.wait_ge(s("tap"), (KW - 2) * (NCONV * f + j) + tap + 1)
                ins.then_inc(s("conv"), 1)

            def times_beta(f, p):
                dve.wait_ge(s("w_squared"), f + 1)
                dve.wait_ge(s("beta"), 16 * f + 16)
                v.tensor_tensor(Y(p, "w"), Y(p, "w"), beta[:, :], ALU.mult).then_inc(s("w_beta"), 1)

            def times_norm(f, p):
                dve.wait_ge(s("w_beta"), f + 1)
                dve.wait_ge(s("w_rnorm"), f + 1)
                v.tensor_tensor(Y(p, "w"), Y(p, "w"), rnorm[:, :], ALU.mult).then_inc(s("bw"), 1)

            def q_times_k(f, p):
                dve.wait_ge(s("silu"), NCONV * f + NCONV)
                dve.wait_ge(s("w_norm_ps"), f + 1)
                v.tensor_tensor(front_sum[:, :], Y(p, "q"), Y(p, "k"), ALU.mult).then_inc(s("qk"), 1)

            dve.wait_ge(s("small_weights"), 16)
            for j in range(NCONV):
                conv(0, 0, j)
            times_beta(0, 0)
            times_norm(0, 0)
            q_times_k(0, 0)

            def head(h, p, more):
                v.memset(suffix[:, :], 1.0).then_inc(s("suffix"), 1)
                dve.wait_ge(s("bw"), h + 1)
                dve.wait_ge(s("qk_ps"), h + 1)
                v.scalar_tensor_tensor(score[:, :], pair(3), SCALE, Y(p, "w"), ALU.mult, ALU.mult).then_inc(s("score_diag"), 1)

                def masked(l, products):
                    m = halves(const[:, K_MASK + l * P:K_MASK + (l + 1) * P], l)[1]
                    m = m.unsqueeze(1).broadcast_to([P, NT, m.shape[1], m.shape[2]])
                    split = dict(i=NT, h=1 << l)
                    return v.tensor_tensor(pairs[:, (l % 2) * HN:(l % 2 + 1) * HN].rearrange("p (i n h) -> p i n h", **split),
                                           products, m, ALU.mult)

                dve.wait_ge(s("kq"), h + 1)
                for l in range(LEVELS + 1):
                    if l < LEVELS - 1:
                        if l >= 2:
                            dve.wait_ge(s("level_ps"), LEVELS * h + l - 1)
                        kq_l = kq[:, 0:N].rearrange("p (i n two h) -> p i n two h", i=NT, two=2, h=1 << l)[:, :, :, 1, :]
                        masked(l, kq_l).then_inc(s("kq_pairs"), 1)
                    if l >= 1:
                        k = l - 1
                        n = LEVELS * h + k
                        dve.wait_ge(s("level_ps"), n + 1)
                        dve.wait_ge(s("pre"), n + 1)
                        t = tmp[:, (k % 2) * HN:(k % 2 + 1) * HN]
                        v.tensor_tensor(t, ps[:, 4 + k % 2, :], pre[:, k * HN:(k + 1) * HN], ALU.mult).then_inc(s("level_read"), 1)
                        dve.wait_ge(s("level_read"), n + 1)
                        if k:
                            dve.wait_ge(s("score_level"), n)
                        else:
                            dve.wait_ge(s("score_diag"), h + 1)
                        right = halves(score[:, :], k)[1]
                        v.tensor_tensor(right, right, packed(t, k), ALU.add).then_inc(s("score_level"), 1)
                    if more and 2 <= l < 2 + NCONV:
                        conv(h + 1, 1 - p, l - 2)

                sv = sm[:, :].rearrange("p (n m) -> p n m", n=NT)
                across = lambda ap: ap.unsqueeze(2).broadcast_to([P, NT, P])
                pv = pair(3).rearrange("p (n m) -> p n m", n=NT)
                dve.wait_ge(s("score_t"), h + 1)
                v.tensor_reduce(stat[:, 0:NT], pv, AX, ALU.max).then_inc(s("max"), 1)
                dve.wait_ge(s("max"), h + 1)
                v.tensor_tensor(sv, pv, across(stat[:, 0:NT]), ALU.subtract).then_inc(s("centred"), 1)
                dve.wait_ge(s("exp"), h + 1)
                v.tensor_reduce(stat[:, NT:2 * NT], sv, AX, ALU.add).then_inc(s("sum"), 1)
                dve.wait_ge(s("sum"), h + 1)
                v.reciprocal(stat[:, 2 * NT:3 * NT], stat[:, NT:2 * NT]).then_inc(s("inverse"), 1)
                dve.wait_ge(s("inverse"), h + 1)
                v.tensor_tensor(sv, sv, across(stat[:, 2 * NT:3 * NT]), ALU.mult).then_inc(s("softmax"), 1)

                dve.wait_ge(s("slots"), h + 1)
                v.tensor_tensor(tmp[:, :], score[:, :], Y(p, "w"), ALU.mult).then_inc(s("slot_write"), 1)
                for l in range(LEVELS):
                    dve.wait_ge(s("aw_pairs_ps"), LEVELS * h + l + 1)
                    if l >= 2:
                        dve.wait_ge(s("level_out"), LEVELS * h + l - 1)
                    if l < LEVELS - 1:
                        aw = ps[:, l % 2, :].rearrange("p (i n h) -> p i n h", i=NT, h=1 << l)
                        masked(l, aw).then_inc(s("aw_pairs"), 1)
                    else:
                        v.tensor_copy(pairs[:, (l % 2) * HN:(l % 2 + 1) * HN], ps[:, l % 2, :]).then_inc(s("aw_pairs"), 1)
                    if l == 2:
                        dve.wait_ge(s("slot_write_ps"), h + 1)
                        v.tensor_tensor(own, pair(2), Y(p, "v"), ALU.mult).then_inc(s("own"), 1)
                    if more and l == 1:
                        times_beta(h + 1, 1 - p)
                    if more and l == 3:
                        times_norm(h + 1, 1 - p)
                    if more and l == 4:
                        q_times_k(h + 1, 1 - p)
                dve.wait_ge(s("own"), h + 1)
                dve.wait_ge(s("level_out"), LEVELS * h + LEVELS)
                v.tensor_tensor(score[:, :], pair(3), own, ALU.add).then_inc(s("o"), 1)
                dve.wait_ge(s("o_squared"), h + 1)
                dve.wait_ge(s("o_rnorm"), h + 1)
                v.tensor_tensor(score[:, :], score[:, :], rnorm[:, :], ALU.mult).then_inc(s("o_normed"), 1)
                dve.wait_ge(s("o_normed"), h + 1)
                v.scalar_tensor_tensor(score[:, :], score[:, :], vec[:, V_NORM:V_NORM + 1], of(gate, p),
                                       ALU.mult, ALU.mult).then_inc(s("o_gated"), 1)
                dve.wait_ge(s("y_out"), h + 1)
                v.tensor_tensor(xT[:, :], xT[:, :], ps[:, 0:4, :].rearrange("p a b -> p (a b)"), ALU.add).then_inc(s("x_added"), 1)
                dve.wait_ge(s("x_added"), h + 2)

            heads(dve, head)

def rmsnorm(nc, env, dst, col):
    vec, hT, ones, eps, ps = (env[k] for k in ("vec", "hT", "ones", "eps", "ps"))
    with ExitStack() as ctx:
        s = Signals(nc, ctx, env, f"rms{col}")
        square = ctx.enter_context(nc.sbuf_tensor(f"square{col}", [P, CT * N], F32))
        rnorm = ctx.enter_context(nc.sbuf_tensor(f"rms_rnorm{col}", [P, N], F32))
        block = ctx.enter_context(nc.Block())

        @block.scalar
        def _(act):
            nc.scalar.activation(square[:, :], hT[:, :], ACT.Square).then_inc(s("square"), 1)
            act.wait_ge(s("sum"), 1)
            nc.scalar.activation(rnorm[:, :], ps[:, 0:2, :].rearrange("p a b -> p (a b)"), ACT.Ln, bias=eps[:, 1:2],
                                 scale=1.0 / C).then_inc(s("log"), 1)
            act.wait_ge(s("log"), 1)
            nc.scalar.activation(rnorm[:, :], rnorm[:, :], ACT.Exp, scale=-0.5).then_inc(s("rnorm"), 1)

        @block.tensor
        def _(pe):
            pe.wait_ge(s("square"), 1)
            for half in range(2):
                for kt in range(CT):
                    last = nc.tensor.matmul(ps[:, half, :], ones[:, :], square[:, kt * N + half * HN:kt * N + (half + 1) * HN],
                                            start=kt == 0, stop=kt == CT - 1)
            last.then_inc(s("sum"), 1)

        @block.vector
        def _(dve):
            dve.wait_ge(s("rnorm"), 1)
            for ct in range(CT):
                c = slice(ct * N, (ct + 1) * N)
                nc.vector.scalar_tensor_tensor(dst[:, c], hT[:, c], vec[:, col + ct:col + ct + 1], rnorm[:, :],
                                               ALU.mult, ALU.mult).then_inc(s("out"), 1)
            dve.wait_ge(s("out"), CT)


def moe(nc, a, env, layer):
    xT, const, vec, hT, ps = (env[k] for k in ("xT", "const", "vec", "hT", "ps"))
    packs = a[f"moe{layer}"]
    NE = 8
    NI = a[f"moe{layer}"].shape[0] // NE
    CHUNK = 3 * C
    W1, W3, W2 = 0, C, 2 * C
    UNITS = 2 * NI
    TH = NT // 2
    assert UNITS % 2 == 0 and NE % 2 == 0
    with ExitStack() as ctx:
        sb = lambda name, cols: ctx.enter_context(nc.sbuf_tensor(f"{name}_moe{layer}", [P, cols], F32))
        acc = sb("acc", NT * C)
        if layer:
            rmsnorm(nc, env, acc, V_FFLN)
            src = acc
        else:
            src = hT
        s = Signals(nc, ctx, env, f"moe{layer}")
        sbr = lambda name, cols: ctx.enter_context(nc.sbuf_tensor(f"{name}_moe{layer}", [P, cols], F32R))
        chunks = sb("chunks", 2 * CHUNK)
        w_high, w_low = (sbr(name, 2 * NI * CHUNK) for name in ("w_high", "w_low"))
        src_high, src_low = (sbr(name, CT * N) for name in ("src_high", "src_low"))
        hid_high, hid_low = (sbr(name, NI * N) for name in ("hid_high", "hid_low"))
        silu = sb("silu", 2 * HN)
        comb = sb("comb", NE * NT)
        mine = sb("mine", 2 * NT)
        rt = {k: sb("rt_" + k, NT * NE) for k in ("logits", "abs", "hot1", "hot2", "a", "b", "c")}
        st = {k: sb("st_" + k, NT) for k in ("max1", "max2", "index", "gate1", "gate2", "sum")}
        block = ctx.enter_context(nc.Block())
        gate_col = V_GATE1 if layer else V_GATE0

        def experts(engine, body):
            with engine.Fori(0, NE // 2 - 1) as i:
                body(2 * i, 0, True)
                body(2 * i + 1, 1, True)
            body(NE - 2, 0, True)
            body(NE - 1, 1, False)

        @block.sync
        def _(sp):
            for slot in range(2):
                sp.dma_start(chunks[:, slot * CHUNK:(slot + 1) * CHUNK], packs[slot]).then_inc(s(f"chunk{slot}"), 16)
            with sp.Fori(0, NE * NI // 2 - 1) as i:
                for slot in range(2):
                    sp.wait_ge(s("split"), 2 * i + slot + 1)
                    nxt = packs[bass.ds(2 * i + slot + 2, 1)].rearrange("o p n -> p (o n)")
                    sp.dma_start(chunks[:, slot * CHUNK:(slot + 1) * CHUNK], nxt).then_inc(s(f"chunk{slot}"), 16)
            if layer:
                out = a["out"].rearrange("(n p) c -> p n c", p=P)
                sp.wait_ge(s("final"), 1)
                sp.dma_start(out, acc[:, :].rearrange("p (n c) -> p n c", n=NT)).then_inc(s("stored"), 16)
                sp.wait_ge(s("stored"), 16)

        @block.tensor
        def _(pe):
            mm = nc.tensor.matmul
            for n in range(NT):
                for kt in range(CT):
                    last = mm(ps[:, 7, n * NE:(n + 1) * NE], src[:, kt * N + n * P:kt * N + (n + 1) * P],
                              vec[:, gate_col + kt * NE:gate_col + (kt + 1) * NE], start=kt == 0, stop=kt == CT - 1)
            last.then_inc(s("logits_ps"), 1)
            pe.sem_inc(s("y_ps"), 1)
            pe.wait_ge(s("src_low"), 1)
            with pe.Fori(0, NE // 2) as i:
                for slot in range(2):
                    e = 2 * i + slot
                    for u in range(UNITS):
                        half, it = divmod(u, NI)
                        if not half:
                            pe.wait_ge(s("split"), NI * e + it + 1)
                        pe.wait_ge(s("up_free"), UNITS * e + u + 1)
                        for bank, base in ((u % 2, W1), (2 + u % 2, W3)):
                            for kt in range(CT):
                                c = (slot * NI + it) * CHUNK + base + kt * P
                                r = slice(kt * N + half * HN, kt * N + (half + 1) * HN)
                                mm(ps[:, bank, :], w_high[:, c:c + P], src_high[:, r], start=kt == 0, stop=False)
                                mm(ps[:, bank, :], w_high[:, c:c + P], src_low[:, r], start=False, stop=False)
                                last = mm(ps[:, bank, :], w_low[:, c:c + P], src_high[:, r], start=False, stop=kt == CT - 1)
                            if base == W1:
                                last.then_inc(s("up1_ps"), 1)
                        last.then_inc(s("up3_ps"), 1)
                    for n in range(NT):
                        half = n // TH
                        pe.wait_ge(s("hidden"), UNITS * e + NI * (half + 1) + 2)
                        pe.wait_ge(s("y_free"), NT * e + n + 1)
                        y = ps[:, 4 + n % 4, 0:C]
                        for it in range(NI):
                            h = slice(it * N + n * P, it * N + (n + 1) * P)
                            w2 = slice((slot * NI + it) * CHUNK + W2, (slot * NI + it) * CHUNK + W2 + C)
                            mm(y, hid_high[:, h], w_high[:, w2], start=it == 0, stop=False)
                            mm(y, hid_high[:, h], w_low[:, w2], start=False, stop=False)
                            last = mm(y, hid_low[:, h], w_high[:, w2], start=False, stop=it == NI - 1)
                        last.then_inc(s("y_ps"), 1)
            ident = const[:, K_ID:K_ID + P]
            if layer:
                pe.wait_ge(s("streams"), 1)
                for n in range(NT):
                    for ct in range(CT):
                        last = nc.tensor.transpose(ps[:, n // 2, (n % 2) * C + ct * P:(n % 2) * C + (ct + 1) * P],
                                                   xT[:, ct * N + n * P:ct * N + (n + 1) * P], ident)
            else:
                pe.wait_ge(s("y_free"), NT * NE + 4)
                for n in range(NT):
                    for ct in range(CT):
                        last = nc.tensor.transpose(ps[:, 2 * ct + n // 4, (n % 4) * P:(n % 4 + 1) * P],
                                                   acc[:, n * C + ct * P:n * C + (ct + 1) * P], ident)
            last.then_inc(s("turned"), 1)

        @block.scalar
        def _(act):
            def split(e, slot, it):
                place = slot * NI + it
                act.wait_ge(s(f"chunk{place % 2}"), 8 * NI * (e - slot) + 16 * (place // 2 + 1))
                nc.scalar.activation(w_high[:, place * CHUNK:(place + 1) * CHUNK], chunks[:, place % 2 * CHUNK:(place % 2 + 1) * CHUNK],
                                     ACT.Copy).then_inc(s("w_high"), 1)

            nc.scalar.activation(src_high[:, :], src[:, :], ACT.Copy).then_inc(s("src_high"), 1)
            for it in range(NI):
                split(0, 0, it)
            act.wait_ge(s("exp_in"), 1)
            if layer:
                nc.scalar.activation(st["gate2"][:, :], st["gate2"][:, :], ACT.Exp).then_inc(s("exp"), 1)
            else:
                nc.scalar.activation(rt["b"][:, :], rt["b"][:, :], ACT.Exp).then_inc(s("exp"), 1)
                act.wait_ge(s("exp_in"), 2)
                nc.scalar.activation(rt["b"][:, :], rt["b"][:, :], ACT.Exp).then_inc(s("exp"), 1)

            def expert(e, slot, more):
                for u in range(UNITS):
                    act.wait_ge(s("up1_ps"), UNITS * e + u + 1)
                    act.wait_ge(s("hidden"), UNITS * e + u + 1)
                    nc.scalar.activation(silu[:, (u % 2) * HN:(u % 2 + 1) * HN], ps[:, u % 2, :],
                                         ACT.Silu).then_inc(s("silu"), 1)
                    if more and u % 2:
                        if u == 1:
                            act.wait_ge(s("y_ps"), NT * e + 1)
                        split(e + 1, 1 - slot, u // 2)

            experts(act, expert)

        @block.gpsimd
        def _(pool):
            def split(e, slot, it):
                place = slot * NI + it
                pool.wait_ge(s("w_high"), NI * e + it + 1)
                w = slice(place * CHUNK, (place + 1) * CHUNK)
                nc.gpsimd.tensor_tensor(w_low[:, w], chunks[:, place % 2 * CHUNK:(place % 2 + 1) * CHUNK],
                                        w_high[:, w], ALU.subtract).then_inc(s("split"), 1)

            with pool.Fori(0, NE // 2) as i:
                for slot in range(2):
                    for it in range(NI):
                        split(2 * i + slot, slot, it)

        @block.vector
        def _(dve):
            v = nc.vector
            steps = [0]

            def step(ins):
                steps[0] += 1
                ins.then_inc(s("dve_step"), 1)
                dve.wait_ge(s("dve_step"), steps[0])

            by_tile = lambda t: t[:, :].rearrange("p (n e) -> p n e", e=NE)
            each = lambda t: t[:, :].unsqueeze(2).broadcast_to([P, NT, NE])
            rank = const[:, K_RANK:K_RANK + NE].unsqueeze(1).broadcast_to([P, NT, NE])
            L, AB, H1, H2, TA, TB, TC = (by_tile(rt[k]) for k in ("logits", "abs", "hot1", "hot2", "a", "b", "c"))
            dve.sem_inc(s("up_free"), 2)
            dve.sem_inc(s("hidden"), 2)
            dve.wait_ge(s("logits_ps"), 1)
            step(v.tensor_copy(rt["logits"][:, :], ps[:, 7, 0:NT * NE]))
            dve.wait_ge(s("src_high"), 1)
            v.tensor_tensor(src_low[:, :], src[:, :], src_high[:, :], ALU.subtract).then_inc(s("src_low"), 1)
            dve.wait_ge(s("src_low"), 1)
            v.memset(acc[:, :], 0.0).then_inc(s("y_free"), 4)

            def first_max(scores, top, hot):
                step(v.tensor_reduce(st[top][:, :], scores, AX, ALU.max))
                step(v.tensor_tensor(TA, scores, each(st[top]), ALU.is_equal))
                step(v.tensor_tensor(TA, TA, rank, ALU.mult))
                step(v.tensor_reduce(st["index"][:, :], TA, AX, ALU.max))
                step(v.tensor_tensor(hot, rank, each(st["index"]), ALU.is_equal))

            def sparse_gate(scores, top, gate, n):
                step(v.tensor_tensor(TA, AB, each(st[top]), ALU.max))
                step(v.tensor_scalar(rt["a"][:, :], rt["a"][:, :], 0.02, None, ALU.mult))
                step(v.tensor_tensor(TB, scores, each(st[top]), ALU.subtract))
                step(v.tensor_scalar(rt["c"][:, :], rt["b"][:, :], -1.0, None, ALU.mult))
                step(v.tensor_tensor(TA, TC, TA, ALU.is_le))
                v.tensor_copy(st["index"][:, :], st[top][:, :]).then_inc(s("exp_in"), 1)
                dve.wait_ge(s("exp"), n)
                step(v.tensor_tensor(TB, TB, TA, ALU.mult))
                step(v.tensor_reduce(st["sum"][:, :], TB, AX, ALU.add))
                step(v.reciprocal(st[gate][:, :], st["sum"][:, :]))

            first_max(L, "max1", H1)
            if layer:
                step(v.scalar_tensor_tensor(TC, H1, -BIG, L, ALU.mult, ALU.add))
                first_max(TC, "max2", H2)
                v.tensor_tensor(st["gate2"][:, :], st["max2"][:, :], st["max1"][:, :], ALU.subtract).then_inc(s("exp_in"), 1)
                dve.wait_ge(s("exp"), 1)
                step(v.tensor_scalar(st["sum"][:, :], st["gate2"][:, :], 1.0, None, ALU.add))
                step(v.reciprocal(st["gate1"][:, :], st["sum"][:, :]))
                step(v.tensor_tensor(st["gate2"][:, :], st["gate2"][:, :], st["gate1"][:, :], ALU.mult))
            else:
                step(v.scalar_tensor_tensor(rt["abs"][:, :], rt["logits"][:, :], -1.0, rt["logits"][:, :], ALU.mult, ALU.max))
                sparse_gate(L, "max1", "gate1", 1)
                step(v.scalar_tensor_tensor(TC, H1, -BIG, L, ALU.mult, ALU.add))
                step(v.tensor_copy(rt["logits"][:, :], rt["c"][:, :]))
                first_max(L, "max2", H2)
                sparse_gate(L, "max2", "gate2", 2)
            step(v.tensor_tensor(H1, H1, each(st["gate1"]), ALU.mult))
            step(v.tensor_tensor(H2, H2, each(st["gate2"]), ALU.mult))
            step(v.tensor_tensor(comb[:, :].rearrange("p (e n) -> p n e", e=NE), H1, H2, ALU.add))
            with dve.Fori(0, NE // 2) as i:
                for slot in range(2):
                    e = 2 * i + slot
                    v.tensor_copy(mine[:, slot * NT:(slot + 1) * NT], comb[:, bass.ds(e * NT, NT)]).then_inc(s("mine"), 1)
                    for u in range(UNITS):
                        half, it = divmod(u, NI)
                        dve.wait_ge(s("silu"), UNITS * e + u + 1)
                        dve.wait_ge(s("up3_ps"), UNITS * e + u + 1)
                        c = slice(it * N + half * HN, it * N + (half + 1) * HN)
                        full = silu[:, (u % 2) * HN:(u % 2 + 1) * HN]
                        v.tensor_tensor(full, full, ps[:, 2 + u % 2, :], ALU.mult).then_inc(s("up_free"), 1)
                        if u == 0:
                            dve.wait_ge(s("y_ps"), NT * e + 1)
                        dve.wait_ge(s("up_free"), UNITS * e + u + 3)
                        v.tensor_copy(hid_high[:, c], full).then_inc(s("hid_high"), 1)
                        dve.wait_ge(s("hid_high"), UNITS * e + u + 1)
                        v.tensor_tensor(hid_low[:, c], full, hid_high[:, c], ALU.subtract).then_inc(s("hidden"), 1)
                    dve.wait_ge(s("mine"), e + 1)
                    for n in range(NT):
                        dve.wait_ge(s("y_ps"), NT * e + n + 2)
                        dve.wait_ge(s("y_free"), NT * e + n + 4)
                        tile = acc[:, n * C:(n + 1) * C]
                        c = slot * NT + n
                        v.scalar_tensor_tensor(tile, ps[:, 4 + n % 4, 0:C], mine[:, c:c + 1], tile, ALU.mult,
                                               ALU.add).then_inc(s("y_free"), 1)
            if layer:
                dve.wait_ge(s("y_ps"), NT * NE + 1)
                v.tensor_tensor(xT[:, :], xT[:, :], hT[:, :], ALU.add).then_inc(s("streams"), 1)
                dve.wait_ge(s("turned"), 1)
                dve.wait_ge(s("y_free"), NT * NE + 4)
                v.tensor_tensor(acc[:, :], acc[:, :], ps[:, 0:4, :].rearrange("p a b -> p (a b)"), ALU.add).then_inc(s("final"), 1)
                dve.wait_ge(s("final"), 1)
            else:
                dve.wait_ge(s("turned"), 1)
                v.tensor_tensor(xT[:, :], xT[:, :], ps[:, 0:4, :].rearrange("p a b -> p (a b)"), ALU.add).then_inc(s("final"), 1)
                dve.wait_ge(s("final"), 1)


SEG = 3 * P


def softmax_group(nc, dve, s, g, buf, env, probs, stat, scale):
    const, ps = env["const"], env["ps"]
    v = nc.vector
    p = probs[:, buf * 4 * SEG:(buf + 1) * 4 * SEG].rearrange("p (u k) -> p u k", u=4)
    first, second = p[:, :, 0:P], p[:, :, P:SEG]
    top, total, inverse = (stat[:, (buf * 3 + i) * 8:(buf * 3 + i + 1) * 8] for i in range(3))
    each = lambda ap, part: ap[:, 4 * part:4 * part + 4].unsqueeze(2).broadcast_to([P, 4, P * (part + 1)])
    mask = const[:, K_CAUSAL:K_CAUSAL + SEG].unsqueeze(1).broadcast_to([P, 4, SEG])
    dve.wait_ge(s("scores_ps"), g + 1)
    v.scalar_tensor_tensor(p, ps[:, 0:4, 0:SEG], scale, mask, ALU.mult, ALU.add).then_inc(s("masked"), 1)
    dve.wait_ge(s("masked"), g + 2)
    v.tensor_reduce(top[:, 0:4], first, AX, ALU.max)
    v.tensor_reduce(top[:, 4:8], second, AX, ALU.max).then_inc(s("max"), 1)
    dve.wait_ge(s("max"), g + 1)
    v.tensor_tensor(first, first, each(top, 0), ALU.subtract)
    v.tensor_tensor(second, second, each(top, 1), ALU.subtract).then_inc(s("centred"), 1)
    dve.wait_ge(s("exp"), g + 1)
    v.tensor_reduce(total[:, 0:4], first, AX, ALU.add)
    v.tensor_reduce(total[:, 4:8], second, AX, ALU.add).then_inc(s("sum"), 1)
    dve.wait_ge(s("sum"), g + 1)
    v.reciprocal(inverse, total).then_inc(s("inverse"), 1)
    dve.wait_ge(s("inverse"), g + 1)
    v.tensor_tensor(first, first, each(inverse, 0), ALU.mult)
    v.tensor_tensor(second, second, each(inverse, 1), ALU.mult).then_inc(s("probs"), 1)


def turn_probs(nc, pe, s, g, buf, env, probs):
    ps, ident = env["ps"], env["const"][:, K_ID:K_ID + P]
    pe.wait_ge(s("probs"), g + 1)
    for piece in range(3):
        for u in range(4):
            c = (buf * 4 + u) * SEG + piece * P
            last = nc.tensor.transpose(ps[:, 4 + piece, u * P:(u + 1) * P], probs[:, c:c + P], ident)
    last.then_inc(s("turned"), 1)


def attention1(nc, a, env):
    xT, const, hT, ps = (env[k] for k in ("xT", "const", "hT", "ps"))
    HD = 16
    with ExitStack() as ctx:
        s = Signals(nc, ctx, env, "a1")
        sb = lambda name, cols: ctx.enter_context(nc.sbuf_tensor(name, [P, cols], F32))
        wkv = sb("wkv", 4 * P)
        wq = sb("wq", 2 * P)
        wo = sb("wo1", C)
        kT = sb("kT", N)
        qT = sb("qT", N)
        plain = sb("plain", N)
        spin = sb("spin", N)
        values = sb("values", N)
        probs = sb("probs", 2 * 4 * SEG)
        probs_t = sb("probs_t", 2 * 4 * SEG)
        stat = sb("stat1", 48)
        oT = sb("oT", N)
        block = ctx.enter_context(nc.Block())
        flat = lambda ap: ap.rearrange("p a b -> p (a b)")
        by_batch = lambda ap: ap.rearrange("p (b t) -> p b t", b=B)
        packs = a["att1"]

        @block.sync
        def _(sp):
            sp.dma_start(wkv[:, :], a["att1_kv"]).then_inc(s("kv_weights"), 16)
            sp.dma_start(wq[:, :], packs[0, :, 0:2 * P]).then_inc(s("q_weights"), 16)
            sp.dma_start(wo[:, :], packs[0, :, 2 * P:2 * P + C]).then_inc(s("o_weights"), 16)
            with sp.Fori(0, 3) as t:
                nxt = packs[bass.ds(t + 1, 1)].rearrange("o p n -> p (o n)")
                sp.wait_ge(s("plain_ps"), t + 2)
                sp.dma_start(wq[:, :], nxt[:, 0:2 * P]).then_inc(s("q_weights"), 16)
                sp.wait_ge(s("y_ps"), t + 1)
                sp.dma_start(wo[:, :], nxt[:, 2 * P:2 * P + C]).then_inc(s("o_weights"), 16)

        @block.tensor
        def _(pe):
            mm = nc.tensor.matmul

            def rope(w, n):
                for half in range(2):
                    for kt in range(CT):
                        last = mm(ps[:, half, :], w[:, kt * P:(kt + 1) * P], hT[:, kt * N + half * HN:kt * N + (half + 1) * HN],
                                  start=kt == 0, stop=kt == CT - 1)
                last.then_inc(s("plain_ps"), 1)
                pe.wait_ge(s("plain"), n + 1)
                for half in range(2):
                    last = mm(ps[:, 2 + half, :], const[:, K_ROT1:K_ROT1 + P], plain[:, half * HN:(half + 1) * HN], start=True, stop=True)
                last.then_inc(s("rotated_ps"), 1)

            pe.wait_ge(s("kv_weights"), 16)
            for n in range(NT):
                for kt in range(CT):
                    last = mm(ps[:, 4 + n // 4, (n % 4) * P:(n % 4 + 1) * P], hT[:, kt * N + n * P:kt * N + (n + 1) * P],
                              wkv[:, (2 + kt) * P:(3 + kt) * P], start=kt == 0, stop=kt == CT - 1)
            last.then_inc(s("values_ps"), 1)
            rope(wkv, 0)
            pe.wait_ge(s("roped"), 1)
            pe.wait_ge(s("values"), 1)

            def scores(t, b):
                g = B * t + b
                pe.wait_ge(s("masked"), g + 1)
                if b == 0:
                    pe.wait_ge(s("roped"), t + 2)
                for u in range(4):
                    rows = slice(32 * u, 32 * u + HD)
                    for q, (c, k) in enumerate(((0, P), (P, 2 * P))):
                        last = mm(ps[:, u, c:c + k], qT[rows, b * T + q * P:b * T + (q + 1) * P], kT[rows, b * T:b * T + k],
                                  start=True, stop=True)
                last.then_inc(s("scores_ps"), 1)

            def weigh(t, b):
                g = B * t + b
                pe.wait_ge(s("probs_t"), g + 1)
                pe.wait_ge(s("o"), g + 1)
                for u in range(4):
                    rows = slice(32 * u, 32 * (u + 1))
                    for piece, (tile, q) in enumerate(((0, 0), (0, 1), (1, 1))):
                        c = (b % 2) * 4 * SEG + (piece * 4 + u) * P
                        last = mm(ps[rows, 7, q * P:(q + 1) * P], values[:, (2 * b + tile) * P + 32 * u:(2 * b + tile) * P + 32 * (u + 1)],
                                  probs_t[:, c:c + P], start=piece < 2, stop=piece != 1, skip_group_check=True)
                last.then_inc(s("o_ps"), 1)

            with pe.Fori(0, 4) as t:
                pe.wait_ge(s("q_weights"), 16 * t + 16)
                rope(wq, t + 1)
                for b in range(B + 1):
                    if b < B:
                        scores(t, b)
                    if b:
                        if b == 1:
                            pe.wait_ge(s("x_added"), t + 1)
                        turn_probs(nc, pe, s, B * t + b - 1, (b - 1) % 2, env, probs)
                        weigh(t, b - 1)
                pe.wait_ge(s("o"), B * t + B + 1)
                pe.wait_ge(s("o_weights"), 16 * t + 16)
                for ct in range(CT):
                    for half in range(2):
                        last = mm(ps[:, 4 + 2 * ct + half, :], wo[:, ct * P:(ct + 1) * P], oT[:, half * HN:(half + 1) * HN],
                                  start=True, stop=True)
                last.then_inc(s("y_ps"), 1)

        @block.scalar
        def _(act):
            A = nc.scalar.activation
            act.sem_inc(s("o"), 1)
            act.wait_ge(s("values_ps"), 1)
            A(values[:, :], flat(ps[:, 4:6, :]), ACT.Copy).then_inc(s("values"), 1)
            act.wait_ge(s("plain_ps"), 1)
            A(plain[:, :], flat(ps[:, 0:2, :]), ACT.Copy).then_inc(s("plain"), 1)
            with act.Fori(0, 4) as t:
                act.wait_ge(s("plain_ps"), t + 2)
                act.wait_ge(s("roped"), t + 1)
                A(plain[:, :], flat(ps[:, 0:2, :]), ACT.Copy).then_inc(s("plain"), 1)
                for b in range(B + 1):
                    if b < B:
                        act.wait_ge(s("centred"), B * t + b + 1)
                        p = probs[:, (b % 2) * 4 * SEG:(b % 2 + 1) * 4 * SEG]
                        A(p, p, ACT.Exp).then_inc(s("exp"), 1)
                    if b:
                        g = B * t + b - 1
                        act.wait_ge(s("turned"), g + 1)
                        p = probs_t[:, ((b - 1) % 2) * 4 * SEG:((b - 1) % 2 + 1) * 4 * SEG]
                        A(p, flat(ps[:, 4:7, :]), ACT.Copy).then_inc(s("probs_t"), 1)
                        act.wait_ge(s("o_ps"), g + 1)
                        A(oT[:, (b - 1) * T:b * T], ps[:, 7, 0:T], ACT.Copy).then_inc(s("o"), 1)

        @block.vector
        def _(dve):
            v = nc.vector

            def rope(dst, n):
                cos, sin = (over_batches(const[:, k:k + T]) for k in (K_COS1, K_SIN1))
                dve.wait_ge(s("plain"), n + 1)
                v.tensor_tensor(by_batch(dst[:, :]), by_batch(plain[:, :]), cos, ALU.mult).then_inc(s("cos"), 1)
                dve.wait_ge(s("rotated_ps"), n + 1)
                v.tensor_tensor(by_batch(spin[:, :]), by_batch(flat(ps[:, 2:4, :])), sin, ALU.mult).then_inc(s("sin"), 1)
                dve.wait_ge(s("cos"), n + 1)
                dve.wait_ge(s("sin"), n + 1)
                v.tensor_tensor(dst[:, :], dst[:, :], spin[:, :], ALU.add).then_inc(s("roped"), 1)

            rope(kT, 0)
            dve.sem_inc(s("masked"), 1)
            dve.sem_inc(s("x_added"), 1)
            with dve.Fori(0, 4) as t:
                rope(qT, t + 1)
                for b in range(B):
                    softmax_group(nc, dve, s, B * t + b, b % 2, env, probs, stat, float(HD) ** -0.5)
                dve.wait_ge(s("y_ps"), t + 1)
                v.tensor_tensor(xT[:, :], xT[:, :], flat(ps[:, 4:8, :]), ALU.add).then_inc(s("x_added"), 1)
                dve.wait_ge(s("x_added"), t + 2)


def attention2(nc, a, env):
    const, hT, ps = (env[k] for k in ("const", "hT", "ps"))
    KV, REP = 4, 4
    with ExitStack() as ctx:
        sb = lambda name, cols: ctx.enter_context(nc.sbuf_tensor(name, [P, cols], F32))
        nT = sb("nT", CT * N)
        rmsnorm(nc, env, nT, V_LN)
        s = Signals(nc, ctx, env, "a2")
        wp = sb("wp", (2 + REP) * C)
        wo = sb("wo2", REP * C)
        kT = sb("kT2", N)
        qT = sb("qT2", REP * N)
        plain = sb("plain2", N)
        spin = sb("spin2", N)
        values = sb("values2", N)
        probs = sb("probs2", 2 * 4 * SEG)
        probs_t = sb("probs_t2", 4 * SEG)
        stat = sb("stat2", 48)
        oT = sb("oT2", REP * N)
        block = ctx.enter_context(nc.Block())
        flat = lambda ap: ap.rearrange("p a b -> p (a b)")
        by_batch = lambda ap: ap.rearrange("p (b t) -> p b t", b=B)
        packs = a["att2"]
        WP = (2 + REP) * C
        ROPES = 1 + REP

        @block.sync
        def _(sp):
            sp.dma_start(wp[:, :], packs[0, :, 0:WP]).then_inc(s("p_weights"), 16)
            sp.dma_start(wo[:, :], packs[0, :, WP:WP + REP * C]).then_inc(s("o_weights"), 16)
            with sp.Fori(0, KV - 1) as kv:
                nxt = packs[bass.ds(kv + 1, 1)].rearrange("o p n -> p (o n)")
                sp.wait_ge(s("plain_ps"), ROPES * kv + ROPES)
                sp.dma_start(wp[:, :], nxt[:, 0:WP]).then_inc(s("p_weights"), 16)
                sp.wait_ge(s("y_ps"), 2 * kv + 2)
                sp.dma_start(wo[:, :], nxt[:, WP:WP + REP * C]).then_inc(s("o_weights"), 16)

        @block.tensor
        def _(pe):
            mm = nc.tensor.matmul
            with pe.Fori(0, KV) as kv:
                pe.wait_ge(s("p_weights"), 16 * kv + 16)
                pe.wait_ge(s("h_added"), 2 * kv + 1)
                for n in range(NT):
                    for kt in range(CT):
                        last = mm(ps[:, 6 + n // 4, (n % 4) * P:(n % 4 + 1) * P], nT[:, kt * N + n * P:kt * N + (n + 1) * P],
                                  wp[:, C + kt * P:C + (kt + 1) * P], start=kt == 0, stop=kt == CT - 1)
                last.then_inc(s("values_ps"), 1)
                for r in range(ROPES):
                    n = ROPES * kv + r
                    w = wp[:, (0 if r == 0 else (1 + r) * C):]
                    for half in range(2):
                        for kt in range(CT):
                            last = mm(ps[:, half, :], w[:, kt * P:(kt + 1) * P], nT[:, kt * N + half * HN:kt * N + (half + 1) * HN],
                                      start=kt == 0, stop=kt == CT - 1)
                    last.then_inc(s("plain_ps"), 1)
                    pe.wait_ge(s("plain"), n + 1)
                    pe.wait_ge(s("roped"), n + 1)
                    for half in range(2):
                        last = mm(ps[:, 2 + half, :], const[:, K_ROT2:K_ROT2 + P], plain[:, half * HN:(half + 1) * HN],
                                  start=True, stop=True)
                    last.then_inc(s("rotated_ps"), 1)
                pe.wait_ge(s("values"), kv + 1)

                def scores(j):
                    pe.wait_ge(s("masked"), REP * kv + j + 1)
                    if j == 0:
                        pe.wait_ge(s("roped"), ROPES * kv + ROPES + 1)
                    for u in range(B):
                        for q, (c, k) in enumerate(((0, P), (P, 2 * P))):
                            last = mm(ps[:, u, c:c + k], qT[:, j * N + u * T + q * P:j * N + u * T + (q + 1) * P],
                                      kT[:, u * T:u * T + k], start=True, stop=True)
                    last.then_inc(s("scores_ps"), 1)

                def weigh(j):
                    g = REP * kv + j
                    pe.wait_ge(s("probs_t"), g + 1)
                    for u in range(B):
                        for piece, (tile, q) in enumerate(((0, 0), (0, 1), (1, 1))):
                            c = (piece * 4 + u) * P
                            col = (u % 2) * T + q * P
                            last = mm(ps[:, 4 + u // 2, col:col + P], values[:, (2 * u + tile) * P:(2 * u + tile + 1) * P],
                                      probs_t[:, c:c + P], start=piece < 2, stop=piece != 1, skip_group_check=True)
                    last.then_inc(s("o_ps"), 1)

                for j in range(REP + 1):
                    if j < REP:
                        scores(j)
                    if j:
                        g = REP * kv + j - 1
                        pe.wait_ge(s("o"), g + 1)
                        turn_probs(nc, pe, s, g, (j - 1) % 2, env, probs)
                        weigh(j - 1)
                pe.wait_ge(s("o"), REP * kv + REP + 1)
                pe.wait_ge(s("o_weights"), 16 * kv + 16)
                for ct in range(CT):
                    pe.wait_ge(s("h_added"), 2 * kv + ct + 1)
                    for half in range(2):
                        for j in range(REP):
                            last = mm(ps[:, 6 + half, :], wo[:, j * C + ct * P:j * C + (ct + 1) * P],
                                      oT[:, j * N + half * HN:j * N + (half + 1) * HN], start=j == 0, stop=j == REP - 1)
                    last.then_inc(s("y_ps"), 1)

        @block.scalar
        def _(act):
            A = nc.scalar.activation
            act.sem_inc(s("o"), 1)
            with act.Fori(0, KV) as kv:
                act.wait_ge(s("values_ps"), kv + 1)
                A(values[:, :], flat(ps[:, 6:8, :]), ACT.Copy).then_inc(s("values"), 1)
                for r in range(ROPES):
                    n = ROPES * kv + r
                    act.wait_ge(s("plain_ps"), n + 1)
                    act.wait_ge(s("roped"), n + 1)
                    A(plain[:, :], flat(ps[:, 0:2, :]), ACT.Copy).then_inc(s("plain"), 1)
                for j in range(REP + 1):
                    if j < REP:
                        act.wait_ge(s("centred"), REP * kv + j + 1)
                        p = probs[:, (j % 2) * 4 * SEG:(j % 2 + 1) * 4 * SEG]
                        A(p, p, ACT.Exp).then_inc(s("exp"), 1)
                    if j:
                        g = REP * kv + j - 1
                        act.wait_ge(s("turned"), g + 1)
                        A(probs_t[:, :], flat(ps[:, 4:7, :]), ACT.Copy).then_inc(s("probs_t"), 1)
                        act.wait_ge(s("o_ps"), g + 1)
                        A(oT[:, (j - 1) * N:j * N], flat(ps[:, 4:6, :]), ACT.Copy).then_inc(s("o"), 1)

        @block.vector
        def _(dve):
            v = nc.vector
            cos, sin = (over_batches(const[:, k:k + T]) for k in (K_COS2, K_SIN2))
            for free in ("masked", "roped", "h_added"):
                dve.sem_inc(s(free), 1)
            with dve.Fori(0, KV) as kv:
                for r in range(ROPES):
                    n = ROPES * kv + r
                    dst = kT[:, :] if r == 0 else qT[:, (r - 1) * N:r * N]
                    dve.wait_ge(s("plain"), n + 1)
                    v.tensor_tensor(by_batch(dst), by_batch(plain[:, :]), cos, ALU.mult).then_inc(s("cos"), 1)
                    dve.wait_ge(s("rotated_ps"), n + 1)
                    v.tensor_tensor(by_batch(spin[:, :]), by_batch(flat(ps[:, 2:4, :])), sin, ALU.mult).then_inc(s("sin"), 1)
                    dve.wait_ge(s("cos"), n + 1)
                    dve.wait_ge(s("sin"), n + 1)
                    v.tensor_tensor(dst, dst, spin[:, :], ALU.add).then_inc(s("roped"), 1)
                for j in range(REP):
                    softmax_group(nc, dve, s, REP * kv + j, j % 2, env, probs, stat, float(P) ** -0.5)
                for ct in range(CT):
                    dve.wait_ge(s("y_ps"), 2 * kv + ct + 1)
                    c = slice(ct * N, (ct + 1) * N)
                    v.tensor_tensor(hT[:, c], hT[:, c], flat(ps[:, 6:8, :]), ALU.add).then_inc(s("h_added"), 1)
                dve.wait_ge(s("h_added"), 2 * kv + 3)



def constants():
    k = np.zeros((P, K_COLS), np.float32)
    k[:, K_ID:K_ID + P] = np.eye(P)
    i = np.arange(P)
    for l in range(LEVELS):
        k[:, K_MASK + l * P:K_MASK + (l + 1) * P] = ((i[:, None] >> (l + 1)) == (i[None] >> (l + 1))) & ((i[:, None] >> l) % 2 == 0) & ((i[None] >> l) % 2 == 1)
    k[:, K_RANK:K_RANK + 8] = np.arange(8, 0, -1)
    later = (i[None] > i[:, None]) * -BIG
    k[:, K_CAUSAL:K_CAUSAL + P] = later
    k[:, K_CAUSAL + 2 * P:K_CAUSAL + 3 * P] = later
    t = np.arange(T, dtype=np.float32)
    hd = 16
    f = (np.float32(1.0) / np.float32(10000.0) ** (np.arange(0, hd, 2, dtype=np.float32) / np.float32(hd))).astype(np.float32)
    ang = np.tile((t[:, None] * f[None]).astype(np.float32), (1, 2)).T
    for g in range(4):
        k[32 * g:32 * g + hd, K_COS1:K_COS1 + T] = np.cos(ang)
        k[32 * g:32 * g + hd, K_SIN1:K_SIN1 + T] = np.sin(ang)
        for d in range(hd):
            src, sign = (d + 8, -1) if d < 8 else (d - 8, 1)
            k[32 * g + src, K_ROT1 + 32 * g + d] = sign
    f = (np.float32(1000000.0) ** (-np.arange(0, P, 2, dtype=np.float32) / np.float32(P))).astype(np.float32)
    ang = np.repeat((t[:, None] * f[None]).astype(np.float32), 2, axis=1).T
    k[:, K_COS2:K_COS2 + T] = np.cos(ang)
    k[:, K_SIN2:K_SIN2 + T] = np.sin(ang)
    for d in range(0, P, 2):
        k[d + 1, K_ROT2 + d] = -1
        k[d, K_ROT2 + d + 1] = 1
    return k


def rows(w):
    return w.reshape(-1, P, w.shape[-1]).transpose(1, 0, 2)


def flat_rows(w):
    return rows(w).reshape(P, -1)


def layout(inp):
    g = lambda name: np.asarray(inp[name])
    out = {}
    out["xT"] = flat_rows(g("x").reshape(N, C).T)
    out["fT"] = flat_rows(g("fside_BxSxS_0").reshape(N, C).T)
    out["emb"] = g("cond_512").reshape(-1)
    out["const"] = constants()
    vec = np.zeros((P, V_COLS), np.float32)
    for i, name in enumerate(("L0_cond", "L0_cond2", "L1_cond", "L1_cond2")):
        vec[:, V_W + 2 * i:V_W + 2 * i + 2] = g(name + "_w").reshape(CT, P).T
        vec[:, V_U + 2 * i:V_U + 2 * i + 2] = g(name + "_u").reshape(CT, P).T
    vec[:, V_NORM] = g("L0_attn_norm_w")
    vec[:, V_LN:V_LN + 2] = g("L1_ffn_ln_w").reshape(CT, P).T
    vec[:, V_FFLN:V_FFLN + 2] = g("L1_ffn_ff_ln_w").reshape(CT, P).T
    vec[:, V_GATE0:V_GATE0 + 16] = flat_rows(g("L0_ffn_gate_w").T)
    vec[:, V_GATE1:V_GATE1 + 16] = flat_rows(g("L1_ffn_gate_w"))
    out["vec"] = vec
    out["low_w"] = np.concatenate([flat_rows(g("L0_attn_" + name)) for name in ("Wf1", "Wg1", "Wb")], axis=1)
    gsa = np.zeros((GH, P, G_COLS), np.float32)
    for h in range(GH):
        c = slice(h * P, (h + 1) * P)
        for key, name in (("q", "Wq"), ("k", "Wk"), ("v", "Wv"), ("w", "Ww")):
            gsa[h, :, G_W[key]:G_W[key] + 2 * P] = flat_rows(g("L0_attn_" + name)[:, c])
        gsa[h, :, G_W["f"]:G_W["f"] + P] = g("L0_attn_Wf2")[:, c]
        gsa[h, :, G_W["g"]:G_W["g"] + P] = g("L0_attn_Wg2")[:, c]
        gsa[h, :, G_W["o"]:G_W["o"] + C] = g("L0_attn_Wo")[c]
        for j, name in enumerate(("cq", "ck", "cv")):
            gsa[h, :, G_W["conv"] + 4 * j:G_W["conv"] + 4 * j + 4] = g("L0_attn_" + name)[c]
        gsa[h, :, G_W["bg"]] = g("L0_attn_bg2")[c]
    out["gsa"] = gsa
    layout_rest(g, out)
    return out

def layout_rest(g, out):
    kv = np.zeros((P, 4 * P), np.float32)
    for kt in range(CT):
        for h in range(4):
            c = kt * P + 32 * h
            kv[:, c:c + 16] = g("L1_attn_wk")[kt * P:(kt + 1) * P, 16 * h:16 * h + 16]
            kv[:, 2 * P + c:2 * P + c + 16] = g("L1_attn_wv")[kt * P:(kt + 1) * P, 16 * h:16 * h + 16]
    out["att1_kv"] = kv
    att1 = np.zeros((4, P, 2 * P + C), np.float32)
    for t in range(4):
        for u in range(4):
            h = 4 * u + t
            for kt in range(CT):
                att1[t, :, kt * P + 32 * u:kt * P + 32 * u + 16] = g("L1_attn_wq")[kt * P:(kt + 1) * P, 16 * h:16 * h + 16]
            att1[t, 32 * u:32 * u + 16, 2 * P:] = g("L1_attn_wo")[16 * h:16 * h + 16]
    out["att1"] = att1
    att2 = []
    for kv in range(4):
        c = slice(kv * P, (kv + 1) * P)
        heads = [slice(h * P, (h + 1) * P) for h in range(4 * kv, 4 * kv + 4)]
        att2.append(np.concatenate([flat_rows(g("L1_ffn_wk")[:, c]), flat_rows(g("L1_ffn_wv")[:, c])]
                                   + [flat_rows(g("L1_ffn_wq")[:, h]) for h in heads]
                                   + [g("L1_ffn_wo")[h] for h in heads], axis=1))
    out["att2"] = np.stack(att2)
    tiles = lambda w: [slice(i, i + P) for i in range(0, w.shape[1], P)]
    chunk = lambda w1, w3, w2, t: np.concatenate([flat_rows(w1[:, t]), flat_rows(w3[:, t]), w2[t]], axis=1)
    out["moe0"] = np.stack([chunk(w1.T, w3.T, w2.T, t) for w1, w3, w2 in zip(g("L0_ffn_w1"), g("L0_ffn_w3"), g("L0_ffn_w2"))
                            for t in tiles(w1.T)])
    out["moe1"] = np.stack([chunk(w1, w3, w2, t) for w1, w3, w2 in zip(g("L1_ffn_w1"), g("L1_ffn_w3"), g("L1_ffn_w2"))
                            for t in tiles(w1)])



def kernel(**inputs):
    import concourse.bacc as bacc
    from concourse.bass_utils import run_bass_kernel_spmd

    nc = bacc.Bacc("TRN2", target_bir_lowering=False, num_devices=1)
    arrays = {f"in_{n}": np.ascontiguousarray(v) for n, v in layout(inputs).items()}
    args = {n[3:]: nc.dram_tensor(n, v.shape, mybir.dt.from_np(v.dtype), kind="ExternalInput").ap() for n, v in arrays.items()}
    args["out"] = nc.dram_tensor("out", (N, C), F32, kind="ExternalOutput").ap()
    build(nc, args)
    r = run_bass_kernel_spmd(nc, [arrays], core_ids=[0])
    return r.results[0]["out"].reshape(B, T, C)
```

```python
from contextlib import ExitStack

import numpy as np

import concourse.bass as bass
from concourse import mybir

F32 = mybir.dt.float32
F32R = mybir.dt.float32r
ALU = mybir.AluOpType
ACT = mybir.ActivationFunctionType
AX = mybir.AxisListType.X

P = 128
B, T, C, TD = 4, 256, 256, 64
N = B * T
CT = C // P
NT = N // P
HN = N // 2
NCOND = 4

GH, GK, LEVELS, KW = 16, 2, 8, 4
G_W = dict(q=0, k=256, v=512, w=768, f=1024, g=1152, o=1280, conv=1536, bg=1548)
G_COLS = 1552
BIG = 1e30

K_ID, K_MASK, K_CAUSAL = 0, 128, 128 + LEVELS * 128
K_COS1 = K_CAUSAL + 384
K_SIN1, K_COS2, K_SIN2 = K_COS1 + T, K_COS1 + 2 * T, K_COS1 + 3 * T
K_ROT1 = K_COS1 + 4 * T
K_ROT2 = K_ROT1 + P
K_RANK = K_ROT2 + P
K_COLS = K_RANK + 8

V_W, V_U, V_NORM, V_LN, V_FFLN = 0, 8, 16, 17, 19
V_GATE0, V_GATE1 = 21, 37
V_COLS = 53

A_Q, A_K, A_V, A_O = 0, 1024, 1280, 1408
A_COLS = A_O + 4 * C
F_K, F_V, F_COLS = 0, 1024, 2048


class Signals:

    def __init__(self, nc, ctx, env, stage):
        self.nc, self.ctx, self.stage, self.known = nc, ctx, stage, {}
        env["signals"].append(self)

    def __call__(self, name):
        if name not in self.known:
            self.known[name] = self.ctx.enter_context(self.nc.semaphore(f"{self.stage}_{name}"))
        return self.known[name]


def clear_signals(nc, env):
    with nc.Block() as block:
        @block.gpsimd
        def _(pool):
            for signals in env["signals"]:
                for semaphore in signals.known.values():
                    nc.gpsimd.sem_clear(semaphore)
    env["signals"].clear()


def halves(ap, level):
    h = 1 << level
    v = ap.rearrange("p (n two h) -> p n two h", two=2, h=h)
    return v[:, :, 0, :], v[:, :, 1, :]


def packed(ap, level):
    return ap.rearrange("p (n h) -> p n h", h=1 << level)


def over_batches(ap, n=B):
    return ap.unsqueeze(1).broadcast_to([ap.shape[0], n, ap.shape[1]])


def build(nc, a):
    with ExitStack() as ctx:
        env = shared(nc, ctx)
        condition(nc, a, env, 0)
        slot_attention(nc, a, env)
        clear_signals(nc, env)
        condition(nc, a, env, 1)
        moe(nc, a, env, 0)
        condition(nc, a, env, 2)
        attention1(nc, a, env)
        clear_signals(nc, env)
        condition(nc, a, env, 3)
        attention2(nc, a, env)
        moe(nc, a, env, 1)


def shared(nc, ctx):
    keep = lambda name, cols: ctx.enter_context(nc.sbuf_tensor(name, [P, cols], F32))
    return dict(
        xT=keep("xT", CT * N),
        hT=keep("hT", CT * N),
        const=keep("const", K_COLS),
        vec=keep("vec", V_COLS),
        tf=keep("tf", 3 * B),
        dec=keep("dec", 8 * B),
        ones=keep("ones", P),
        eps=keep("eps", 4),
        ps=ctx.enter_context(nc.psum_tensor("ps", [P, 8, 512], F32)),
        signals=[],
    )


def condition(nc, a, env, i):
    xT, const, vec, hT, ones, eps, tf, dec = (env[k] for k in ("xT", "const", "vec", "hT", "ones", "eps", "tf", "dec"))
    with ExitStack() as ctx:
        s = Signals(nc, ctx, env, f"cond{i}")
        sb = lambda name, cols: ctx.enter_context(nc.sbuf_tensor(f"{name}_c{i}", [P, cols], F32))
        fT = sb("fT", CT * N)
        emb = sb("emb", B * TD)
        dw = sb("dw", 2 * 8)
        ek = sb("ek", CT * N)
        ekv = sb("ekv", CT * N)
        bonus = sb("bonus", CT * N)
        bonus_v = sb("bonus_v", CT * N)
        gate = sb("r_gate", CT * N)
        sc = sb("sc", CT * 4 * N)
        block = ctx.enter_context(nc.Block())
        tile = lambda t, ct: t[:, ct * N:(ct + 1) * N]
        scan = lambda ct, n: sc[:, (ct * 4 + n) * N:(ct * 4 + n + 1) * N]
        by_batch = lambda ap: ap.rearrange("p (c b t) -> p c b t", c=CT, b=B)
        first = i == 0

        @block.sync
        def _(sp):
            sp.dma_start(fT[:, :], a["fT"]).then_inc(s("f_loaded"), 16)
            if first:
                sp.dma_start(vec[:, :], a["vec"]).then_inc(s("vec_loaded"), 16)
                sp.dma_start(emb[:, :], a["emb"].partition_broadcast(P)).then_inc(s("vec_loaded"), 16)
                sp.dma_start(xT[:, :], a["xT"]).then_inc(s("x_loaded"), 16)
                sp.dma_start(const[:, :], a["const"]).then_inc(s("const_loaded"), 16)
                sp.wait_ge(s("const_loaded"), 16)

        @block.scalar
        def _(act):
            A = nc.scalar.activation
            if first:
                act.wait_ge(s("emb_sum"), 1)
                A(tf[:, 0:B], tf[:, 0:B], ACT.Sigmoid).then_inc(s("tf"), 1)
                act.wait_ge(s("x_loaded"), 16)
            A(gate[:, :], xT[:, :], ACT.Sigmoid).then_inc(s("r_sigmoid"), 1)
            if first:
                act.wait_ge(s("vec_loaded"), 32)
                A(dw[:, 0:8], vec[:, V_W:V_W + 8], ACT.Exp).then_inc(s("exp_w"), 1)
                act.wait_ge(s("exp_w"), 1)
                A(dw[:, 8:16], dw[:, 0:8], ACT.Exp, scale=-1.0).then_inc(s("decay_w"), 1)
            act.wait_ge(s("k_min"), 1)
            A(ek[:, :], ek[:, :], ACT.Exp).then_inc(s("ek"), 1)
            act.wait_ge(s("uk_min"), CT)
            A(bonus[:, :], bonus[:, :], ACT.Exp).then_inc(s("euk"), 1)
            for ct in range(CT):
                act.wait_ge(s("den"), ct + 1)
                A(scan(ct, 3), scan(ct, 2), ACT.Ln).then_inc(s("log"), 1)
            for ct in range(CT):
                act.wait_ge(s("log"), ct + 1)
                A(scan(ct, 3), scan(ct, 3), ACT.Exp, scale=-1.0).then_inc(s("near"), 1)

        @block.gpsimd
        def _(pool):
            g = nc.gpsimd
            if first:
                g.memset(ones[:, :], 1.0).then_inc(s("ones"), 1)
                g.memset(eps[:, 0:1], 1e-6).then_inc(s("ones"), 1)
                g.memset(eps[:, 1:2], 1e-5).then_inc(s("ones"), 1)
                pool.wait_ge(s("ones"), 3)
            pool.wait_ge(s("f_loaded"), 16)
            pool.wait_ge(s("ek"), 1)
            pool.wait_ge(s("euk"), 1)
            g.tensor_tensor(bonus[:, :], bonus[:, :], ek[:, :], ALU.subtract).then_inc(s("bonus"), 1)
            pool.wait_ge(s("bonus"), 1)
            g.tensor_tensor(bonus_v[:, :], bonus[:, :], fT[:, :], ALU.mult).then_inc(s("bonus_v"), 1)
            pool.wait_ge(s("r_sigmoid"), 1)
            if first:
                pool.wait_ge(s("tf_parts"), 2)
            w = tf[:, 2 * B:3 * B].unsqueeze(1).unsqueeze(3).broadcast_to([P, CT, B, T])
            g.tensor_tensor(by_batch(gate[:, :]), by_batch(gate[:, :]), w, ALU.mult).then_inc(s("r_gate"), 1)
            pool.wait_ge(s("r_gate"), 1)
            for ct in range(CT):
                pool.wait_ge(s("num_step"), 2 * ct + 2)
                g.tensor_tensor(scan(ct, 0), scan(ct, 0), tile(gate, ct), ALU.mult).then_inc(s("num"), 1)

        @block.vector
        def _(dve):
            v = nc.vector
            if first:
                dve.wait_ge(s("vec_loaded"), 32)
                v.tensor_reduce(tf[:, 0:B], emb[:, :].rearrange("p (b d) -> p b d", b=B), AX, ALU.add).then_inc(s("emb_sum"), 1)
            dve.wait_ge(s("f_loaded"), 16)
            v.tensor_scalar(ek[:, :], fT[:, :], 30.0, None, ALU.min).then_inc(s("k_min"), 1)
            for ct in range(CT):
                u = vec[:, V_U + 2 * i + ct:V_U + 2 * i + ct + 1]
                v.tensor_scalar(tile(bonus, ct), tile(fT, ct), u, 30.0, ALU.add, ALU.min).then_inc(s("uk_min"), 1)
            if first:
                dve.wait_ge(s("tf"), 1)
                v.tensor_scalar(tf[:, B:2 * B], tf[:, 0:B], 0.5, 0.5, ALU.mult, ALU.add).then_inc(s("tf_parts"), 1)
                v.tensor_scalar(tf[:, 2 * B:3 * B], tf[:, 0:B], 0.2, 0.8, ALU.mult, ALU.add).then_inc(s("tf_parts"), 1)
                dve.wait_ge(s("tf_parts"), 2)
                dve.wait_ge(s("decay_w"), 1)
                for b in range(B):
                    v.tensor_scalar(dec[:, b * 8:(b + 1) * 8], dw[:, 8:16], tf[:, B + b:B + b + 1], None,
                                    ALU.mult).then_inc(s("decay"), 1)
                dve.wait_ge(s("decay"), B)
            dve.wait_ge(s("ek"), 1)
            v.tensor_tensor(ekv[:, :], ek[:, :], fT[:, :], ALU.mult).then_inc(s("ekv"), 1)

            def scans(ct, n, src):
                for b in range(B):
                    d = dec[:, b * 8 + 2 * i + ct:b * 8 + 2 * i + ct + 1].broadcast_to([P, T])
                    k = tile(src, ct)[:, b * T:(b + 1) * T]
                    fwd, bwd = (scan(ct, n + m)[:, b * T:(b + 1) * T] for m in range(2))
                    v.tensor_tensor_scan(fwd, d, k, 0.0, ALU.mult, ALU.add)
                    last = v.tensor_tensor_scan(bwd[:, ::-1], d, k[:, ::-1], 0.0, ALU.mult, ALU.add)
                return last

            for ct in range(CT):
                scans(ct, 2, ek).then_inc(s("den_scans"), 1)
            for ct in range(CT):
                dve.wait_ge(s("den_scans"), ct + 1)
                v.tensor_tensor(scan(ct, 2), scan(ct, 2), scan(ct, 3), ALU.add).then_inc(s("den_step"), 1)
                dve.wait_ge(s("bonus"), 1)
                dve.wait_ge(s("den_step"), 2 * ct + 1)
                v.tensor_tensor(scan(ct, 2), scan(ct, 2), tile(bonus, ct), ALU.add).then_inc(s("den_step"), 1)
                dve.wait_ge(s("den_step"), 2 * ct + 2)
                v.tensor_scalar(scan(ct, 2), scan(ct, 2), 1e-8, None, ALU.max).then_inc(s("den"), 1)
            dve.wait_ge(s("ekv"), 1)
            for ct in range(CT):
                scans(ct, 0, ekv).then_inc(s("num_scans"), 1)
            for ct in range(CT):
                dve.wait_ge(s("num_scans"), ct + 1)
                v.tensor_tensor(scan(ct, 0), scan(ct, 0), scan(ct, 1), ALU.add).then_inc(s("num_step"), 1)
                dve.wait_ge(s("num_step"), 2 * ct + 1)
                dve.wait_ge(s("bonus_v"), 1)
                v.tensor_tensor(scan(ct, 0), scan(ct, 0), tile(bonus_v, ct), ALU.add).then_inc(s("num_step"), 1)
            for ct in range(CT):
                dve.wait_ge(s("den"), ct + 1)
                dve.wait_ge(s("near"), ct + 1)
                v.tensor_tensor(scan(ct, 2), scan(ct, 2), scan(ct, 3), ALU.mult).then_inc(s("newton"), 1)
                dve.wait_ge(s("newton"), 2 * ct + 1)
                v.scalar_tensor_tensor(scan(ct, 2), scan(ct, 2), 2.0, scan(ct, 3), ALU.subtract, ALU.mult).then_inc(s("newton"), 1)
                dve.wait_ge(s("newton"), 2 * ct + 2)
                dve.wait_ge(s("num"), ct + 1)
                v.scalar_tensor_tensor(tile(hT, ct), scan(ct, 0), -1.0, scan(ct, 2), ALU.mult, ALU.mult).then_inc(s("h"), 1)
            dve.wait_ge(s("h"), CT)


def slot_attention(nc, a, env):
    xT, const, vec, hT, ones, eps, ps = (env[k] for k in ("xT", "const", "vec", "hT", "ones", "eps", "ps"))
    SCALE = float(P) ** -0.5
    ident = const[:, K_ID:K_ID + P]
    PROJ = ("w", "k", "q", "v", "f", "g")
    CONV = ("w", "k", "q", "v")
    TAPS = dict(q=0, k=4, v=8, w=8)
    NPROJ, NCONV = len(PROJ), len(CONV)
    with ExitStack() as ctx:
        s = Signals(nc, ctx, env, "gsa")
        sb = lambda name, cols, dt=F32: ctx.enter_context(nc.sbuf_tensor(name, [P, cols], dt))
        wt = sb("wt", G_W["o"])
        wo = sb("wo", C)
        small = sb("small", G_COLS - G_W["conv"])
        low_w = sb("low_w", 2 * CT * P + CT * GH)
        low = sb("low", 2 * N)
        raw = sb("raw", 2 * B * (T + KW - 1))
        y = sb("y", 2 * NCONV * N)
        prefix = sb("prefix", 2 * N)
        gate = sb("gate", 2 * N)
        beta = sb("beta", N)
        front_sum = sb("front_sum", N)
        suffix = sb("suffix", N)
        rnorm = sb("rnorm", N)
        writes = sb("writes", LEVELS * N)
        pre = sb("pre", LEVELS * HN)
        kq = sb("kq", N + HN)
        pairs = sb("pairs", 2 * HN)
        wt_t = sb("wt_t", 2 * N)
        v_t = sb("v_t", N)
        score = sb("score", N)
        sm = sb("sm", N)
        o = sb("o", N)
        tmp = sb("tmp", N)
        stat = sb("stat", 3 * NT)
        zero = sb("zero", P + 512, mybir.dt.bfloat16)
        beta_dram = nc.dram_tensor("beta_all", (GH, N), F32).ap()
        block = ctx.enter_context(nc.Block())

        own = kq[:, 0:N]
        Y = lambda p, name: y[:, (p * NCONV + CONV.index(name)) * N:(p * NCONV + CONV.index(name) + 1) * N]
        raws = raw[:, :].rearrange("p (j b t) -> p j b t", j=2, b=B)
        of = lambda buf, p: buf[:, p * N:(p + 1) * N]
        pair = lambda j: ps[:, 2 * j:2 * j + 2, :].rearrange("p a b -> p (a b)")
        by_batch = lambda ap: ap.rearrange("p (b t) -> p b t", b=B)
        packs = a["gsa"]

        def heads(engine, body):
            body(0, 0, False, True)
            with engine.Fori(0, GH // 2 - 1) as i:
                body(2 * i + 1, 1, True, True)
                body(2 * i + 2, 0, True, True)
            body(GH - 1, 1, True, False)

        O_NORM, V_TURN, OUT, PROJECT = 1, 2, (4, 5), {6: 0, 7: 1, 8: 2}
        PROJ_PAIR = dict(w=3, k=3, q=3, v=1, f=3, g=1)

        @block.sync
        def _(sp):
            sp.dma_start(low_w[:, :], a["low_w"]).then_inc(s("low_weights"), 16)
            sp.dma_start(wt[:, :], packs[0, :, 0:G_W["o"]]).then_inc(s("proj_weights"), 16)
            sp.dma_start(small[:, :], packs[0, :, G_W["conv"]:G_COLS]).then_inc(s("small_weights"), 16)
            sp.dma_start(wo[:, :], packs[0, :, G_W["o"]:G_W["conv"]]).then_inc(s("out_weights"), 16)
            sp.wait_ge(s("beta_all"), 1)
            sp.dma_start(beta_dram, tmp[0:GH, :]).then_inc(s("beta_stored"), 16)
            sp.wait_ge(s("beta_stored"), 16)
            sp.dma_start(beta[:, :], beta_dram[0].partition_broadcast(P)).then_inc(s("beta"), 16)

            def load(f):
                nxt = packs[bass.ds(f + 1, 1)].rearrange("o p n -> p (o n)")
                sp.wait_ge(s("proj"), NPROJ * f + NPROJ)
                sp.dma_start(wt[:, :], nxt[:, 0:G_W["o"]]).then_inc(s("proj_weights"), 16)
                sp.wait_ge(s("conv"), NCONV * f + NCONV)
                sp.wait_ge(s("proj_out"), NPROJ * f + NPROJ)
                sp.dma_start(small[:, :], nxt[:, G_W["conv"]:G_COLS]).then_inc(s("small_weights"), 16)
                sp.wait_ge(s("w_beta"), f + 1)
                row = beta_dram[bass.ds(f + 1, 1)].rearrange("o n -> (o n)")
                sp.dma_start(beta[:, :], row.partition_broadcast(P)).then_inc(s("beta"), 16)

            def load_out(h):
                own_out = packs[bass.ds(h, 1)].rearrange("o p n -> p (o n)")
                sp.wait_ge(s("y_out"), CT * h)
                sp.dma_start(wo[:, :], own_out[:, G_W["o"]:G_W["conv"]]).then_inc(s("out_weights"), 16)

            load(0)
            with sp.Fori(1, GH - 1) as f:
                load(f)
                load_out(f)
            load_out(GH - 1)

        @block.tensor
        def _(pe):
            mm = nc.tensor.matmul

            def ones_sum(banks, src):
                for half in range(2):
                    last = mm(ps[:, banks + half, :], ones[:, :], src[:, half * HN:(half + 1) * HN], start=True, stop=True)
                return last

            def project(f, j):
                name = PROJ[j]
                bank = 2 * PROJ_PAIR[name]
                if j == 0:
                    pe.wait_ge(s("proj_weights"), 16 * f + 16)
                else:
                    pe.wait_ge(s("proj_out"), NPROJ * f + min(j, {"v": 1, "f": 3, "g": 4}.get(name, j)))
                for half in range(2):
                    if name in "fg":
                        base = (name == "g") * N
                        last = mm(ps[:, bank + half, :], wt[:, G_W[name]:G_W[name] + P],
                                  low[:, base + half * HN:base + (half + 1) * HN], start=True, stop=True)
                    else:
                        for kt in range(CT):
                            last = mm(ps[:, bank + half, :], wt[:, G_W[name] + kt * P:G_W[name] + (kt + 1) * P],
                                      hT[:, kt * N + half * HN:kt * N + (half + 1) * HN], start=kt == 0, stop=kt == CT - 1)
                last.then_inc(s("proj"), 1)

            def w_norm(f):
                pe.wait_ge(s("proj_out"), NPROJ * f + NPROJ)
                pe.wait_ge(s("w_squared"), f + 1)
                ones_sum(2, front_sum).then_inc(s("w_norm_ps"), 1)

            def o_norm(h):
                pe.wait_ge(s("o_squared"), h + 1)
                ones_sum(6, sm).then_inc(s("o_norm_ps"), 1)

            def out(h, ct):
                if ct:
                    pe.wait_ge(s("x_added"), CT * h + ct)
                else:
                    pe.wait_ge(s("o_gated"), h + 1)
                    pe.wait_ge(s("out_weights"), 16 * h + 16)
                for half in range(2):
                    last = mm(ps[:, 6 + half, :], wo[:, ct * P:(ct + 1) * P], o[:, half * HN:(half + 1) * HN],
                              start=True, stop=True)
                last.then_inc(s("y_out"), 1)

            pe.wait_ge(s("low_weights"), 16)
            for half in range(2):
                for kt in range(CT):
                    last = mm(ps[0:GH, 4 + half, :], low_w[:, 2 * CT * P + kt * GH:2 * CT * P + (kt + 1) * GH],
                              hT[:, kt * N + half * HN:kt * N + (half + 1) * HN], start=kt == 0, stop=kt == CT - 1)
            last.then_inc(s("beta_ps"), 1)
            for j in range(2):
                for half in range(2):
                    for kt in range(CT):
                        last = mm(ps[:, 2 * j + half, :], low_w[:, (j * CT + kt) * P:(j * CT + kt + 1) * P],
                                  hT[:, kt * N + half * HN:kt * N + (half + 1) * HN], start=kt == 0, stop=kt == CT - 1)
                last.then_inc(s("low_ps"), 1)
            pe.wait_ge(s("low"), 2)
            pe.wait_ge(s("zero"), 1)
            for j in range(NPROJ):
                project(0, j)
            w_norm(0)

            def head(h, p, before, more):
                pe.wait_ge(s("silu"), NCONV * h + NCONV)
                pe.wait_ge(s("w_log"), h + 1)
                if before:
                    pe.wait_ge(s("aw_pairs"), LEVELS * h)
                for n in range(NT):
                    mm(ps[:, n // 4, (n % 4) * P:(n % 4 + 1) * P], Y(p, "k")[:, n * P:(n + 1) * P],
                       Y(p, "q")[:, n * P:(n + 1) * P], start=True, stop=True)
                for b in range(B):
                    last = mm(ps[:, 2, b * P:(b + 1) * P], Y(p, "k")[:, b * T:b * T + P],
                              Y(p, "q")[:, b * T + P:(b + 1) * T], start=True, stop=True)
                last.then_inc(s("kq_ps"), 1)
                if before:
                    pe.wait_ge(s("own"), h)
                pe.wait_ge(s("qk"), h + 1)
                ones_sum(4, front_sum).then_inc(s("qk_ps"), 1)

                def turn(l):
                    n = LEVELS * h + l
                    pe.wait_ge(s("writes"), n + 1)
                    if l >= 2:
                        pe.wait_ge(s("writes_t"), n - 1)
                    else:
                        pe.wait_ge(s("kq"), h + 1)
                    for i, tile in enumerate(range(NT) if l < LEVELS - 1 else range(0, NT, 2)):
                        c = l * N + tile * P
                        last = nc.tensor.transpose(ps[:, 2 * (l % 2) + i // 4, (i % 4) * P:(i % 4 + 1) * P], writes[:, c:c + P], ident)
                    last.then_inc(s("writes_t_ps"), 1)

                def read(l):
                    n = LEVELS * h + l
                    pe.wait_ge(s("writes_t"), n + 1)
                    if l < 2:
                        pe.wait_ge(s("score_diag"), h + 1)
                    else:
                        pe.wait_ge(s("score_level"), n - 1)
                    wt_l = wt_t[:, (l % 2) * N:(l % 2 + 1) * N]
                    if l < LEVELS - 1:
                        pe.wait_ge(s("kq_pairs"), (LEVELS - 1) * h + l + 1)
                        for i in range(NT):
                            c = (l % 2) * HN + i * (P // 2)
                            last = mm(ps[:, 4 + l % 2, i * (P // 2):(i + 1) * (P // 2)], wt_l[:, i * P:(i + 1) * P],
                                      pairs[:, c:c + P // 2], start=True, stop=True)
                    else:
                        for b in range(B):
                            last = mm(ps[:, 4 + l % 2, b * P:(b + 1) * P], wt_l[:, b * P:(b + 1) * P],
                                      kq[:, N + b * P:N + (b + 1) * P], start=True, stop=True)
                    last.then_inc(s("level_ps"), 1)

                for l in range(LEVELS + 1):
                    if l < LEVELS:
                        turn(l)
                    if l >= 1:
                        read(l - 1)
                    if l == O_NORM and before:
                        o_norm(h - 1)
                    if l == V_TURN:
                        if before:
                            pe.wait_ge(s("o_log"), h)
                        for n in range(NT):
                            last = nc.tensor.transpose(ps[:, 6 + n // 4, (n % 4) * P:(n % 4 + 1) * P],
                                                       Y(p, "v")[:, n * P:(n + 1) * P], ident)
                        last.then_inc(s("v_t_ps"), 1)
                    if l in OUT and before:
                        if l == OUT[0]:
                            pe.wait_ge(s("v_t"), h + 1)
                        out(h - 1, OUT.index(l))
                    if l in PROJECT and more:
                        if PROJECT[l] == 0:
                            pe.wait_ge(s("v_t"), h + 1)
                            if before:
                                pe.wait_ge(s("x_added"), CT * h)
                        project(h + 1, PROJECT[l])

                pe.wait_ge(s("score_level"), LEVELS * h + LEVELS)
                for n in range(NT):
                    last = nc.tensor.transpose(ps[:, n // 4, (n % 4) * P:(n % 4 + 1) * P], score[:, n * P:(n + 1) * P], ident)
                last.then_inc(s("score_t"), 1)
                if more:
                    pe.wait_ge(s("writes_t"), LEVELS * h + LEVELS)
                    project(h + 1, PROJ.index("v"))
                    project(h + 1, PROJ.index("f"))
                pe.wait_ge(s("softmax"), h + 1)
                for n in range(NT):
                    last = nc.tensor.transpose(ps[:, 4 + n // 4, (n % 4) * P:(n % 4 + 1) * P], sm[:, n * P:(n + 1) * P], ident)
                last.then_inc(s("slots_ps"), 1)
                if more:
                    project(h + 1, PROJ.index("g"))
                    pe.wait_ge(s("proj_out"), NPROJ * h + NPROJ + PROJ.index("f") + 1)
                else:
                    pe.wait_ge(s("v_t"), h + 1)
                    pe.wait_ge(s("x_added"), CT * h)
                for half in range(2):
                    mm(ps[:, 6 + half, :], zero[0:1, 0:P], zero[0:1, P:P + 512], start=True, stop=False, skip_group_check=True)

                def products(l):
                    n = LEVELS * h + l
                    pe.wait_ge(s("reads"), n + 1)
                    if l >= 2:
                        pe.wait_ge(s("aw_pairs"), n - 1)
                    w = P // 2 if l < LEVELS - 1 else P
                    for i, tile in enumerate(range(NT) if l < LEVELS - 1 else range(0, NT, 2)):
                        last = mm(ps[:, l % 2, i * w:(i + 1) * w], writes[:, l * N + tile * P:l * N + (tile + 1) * P],
                                  sm[:, (l % 2) * HN + i * w:(l % 2) * HN + (i + 1) * w], start=True, stop=True)
                    last.then_inc(s("aw_pairs_ps"), 1)

                def collect(l):
                    pe.wait_ge(s("aw_pairs"), LEVELS * h + l + 1)
                    c = (l % 2) * HN
                    if l < LEVELS - 1:
                        for i in range(NT):
                            dst = halves(ps[:, 6 + i // 4, (i % 4) * P:(i % 4 + 1) * P], l)[1]
                            last = mm(dst, v_t[:, i * P:(i + 1) * P], packed(pairs[:, c + i * (P // 2):c + (i + 1) * (P // 2)], l),
                                      start=False, stop=False, skip_group_check=True)
                    else:
                        for b in range(B):
                            i = 2 * b + 1
                            last = mm(ps[:, 6 + i // 4, (i % 4) * P:(i % 4 + 1) * P], v_t[:, 2 * b * P:(2 * b + 1) * P],
                                      pairs[:, c + b * P:c + (b + 1) * P], start=False, stop=True, skip_group_check=True)
                    last.then_inc(s("level_out"), 1)

                for l in range(LEVELS + 1):
                    if l < LEVELS:
                        products(l)
                    if l == 1:
                        pe.wait_ge(s("slot_write"), h + 1)
                        ones_sum(4, tmp).then_inc(s("slot_write_ps"), 1)
                    if l >= 1:
                        collect(l - 1)
                    if l == 3 and more:
                        w_norm(h + 1)

            heads(pe, head)
            o_norm(GH - 1)
            pe.wait_ge(s("o_log"), GH)
            for ct in range(CT):
                out(GH - 1, ct)

        @block.scalar
        def _(act):
            A = nc.scalar.activation
            act.wait_ge(s("beta_ps"), 1)
            A(tmp[0:GH, :], ps[0:GH, 4:6, :].rearrange("p a b -> p (a b)"), ACT.Sigmoid).then_inc(s("beta_all"), 1)
            for j in range(2):
                act.wait_ge(s("low_ps"), j + 1)
                A(low[:, j * N:(j + 1) * N], pair(j), ACT.Copy).then_inc(s("low"), 1)
            act.wait_ge(s("zero"), 1)

            def take(f, p, name):
                j = PROJ.index(name)
                src = pair(PROJ_PAIR[name])
                if j == 0:
                    act.wait_ge(s("small_weights"), 16 * f + 16)
                act.wait_ge(s("proj"), NPROJ * f + j + 1)
                if name == "f":
                    A(of(prefix, p), src, ACT.Sigmoid).then_inc(s("proj_out"), 1)
                elif name == "g":
                    c = G_W["bg"] - G_W["conv"]
                    A(of(gate, p), src, ACT.Sigmoid, bias=small[:, c:c + 1]).then_inc(s("proj_out"), 1)
                else:
                    if j >= 2:
                        act.wait_ge(s("conv"), NCONV * f + j - 1)
                    A(raws[:, j % 2, :, KW - 1:], by_batch(src), ACT.Copy)
                    c = TAPS[name] + KW - 1
                    A(Y(p, name), src, ACT.Copy, scale=small[:, c:c + 1]).then_inc(s("proj_out"), 1)

            def silus(f, p, later):
                for i, name in enumerate(CONV):
                    act.wait_ge(s("conv"), NCONV * f + i + 1)
                    A(Y(p, name), Y(p, name), ACT.Silu).then_inc(s("silu"), 1)
                    if i == 1:
                        act.wait_ge(s("silu"), NCONV * f + 1)
                        if later:
                            act.wait_ge(s("qk_ps"), f)
                        A(front_sum[:, :], Y(p, "w"), ACT.Square).then_inc(s("w_squared"), 1)

            def w_rnorm(f, used):
                act.wait_ge(s("w_norm_ps"), f + 1)
                if used is not None:
                    act.wait_ge(s("o_normed"), used)
                A(rnorm[:, :], pair(1), ACT.Ln, bias=eps[:, 0:1]).then_inc(s("w_log"), 1)
                act.wait_ge(s("w_log"), f + 1)
                A(rnorm[:, :], rnorm[:, :], ACT.Exp, scale=-0.5).then_inc(s("w_rnorm"), 1)

            def take_prefix(h, p, l):
                A(packed(pre[:, l * HN:(l + 1) * HN], l), halves(of(prefix, p), l)[1], ACT.Copy).then_inc(s("pre"), 1)

            def o_log(h):
                act.wait_ge(s("o_norm_ps"), h + 1)
                A(rnorm[:, :], pair(3), ACT.Ln, bias=eps[:, 1:2], scale=1.0 / P).then_inc(s("o_log"), 1)

            def o_rnorm(h):
                act.wait_ge(s("o_log"), h + 1)
                A(rnorm[:, :], rnorm[:, :], ACT.Exp, scale=-0.5).then_inc(s("o_rnorm"), 1)

            def o_square(h):
                act.wait_ge(s("o"), h + 1)
                A(sm[:, :], o[:, :], ACT.Square).then_inc(s("o_squared"), 1)

            for name in PROJ:
                take(0, 0, name)
            silus(0, 0, False)
            w_rnorm(0, None)

            def head(h, p, before, more):
                if before:
                    act.wait_ge(s("reads"), LEVELS * (h - 1) + 1)
                take_prefix(h, p, 0)
                if before:
                    act.wait_ge(s("o"), h)
                act.wait_ge(s("kq_ps"), h + 1)
                A(kq[:, 0:N], pair(0), ACT.Copy, scale=SCALE)
                A(kq[:, N:], ps[:, 2, :], ACT.Copy, scale=SCALE).then_inc(s("kq"), 1)
                for l in range(LEVELS + 2):
                    n = LEVELS * h + l
                    if 0 < l < LEVELS:
                        act.wait_ge(s("prefix"), (LEVELS - 1) * h + l)
                        take_prefix(h, p, l)
                    if l - 1 == O_NORM and before:
                        if more:
                            act.wait_ge(s("bw"), h + 1)
                        o_log(h - 1)
                    if l - 2 == O_NORM and before:
                        o_rnorm(h - 1)
                    if l - 1 == V_TURN:
                        act.wait_ge(s("v_t_ps"), h + 1)
                        A(v_t[:, :], pair(3), ACT.Copy).then_inc(s("v_t"), 1)
                    if l - 1 in PROJECT and more:
                        take(h + 1, 1 - p, PROJ[PROJECT[l - 1]])
                    if l < LEVELS:
                        act.wait_ge(s("writes_t_ps"), n + 1)
                        if l >= 2:
                            act.wait_ge(s("level_ps"), n - 1)
                        w = N if l < LEVELS - 1 else HN
                        A(wt_t[:, (l % 2) * N:(l % 2) * N + w], pair(l % 2)[:, 0:w], ACT.Copy).then_inc(s("writes_t"), 1)
                    if l == 0 and before:
                        o_square(h - 1)
                act.wait_ge(s("centred"), h + 1)
                A(sm[:, :], sm[:, :], ACT.Exp).then_inc(s("exp"), 1)
                if more:
                    take(h + 1, 1 - p, "v")
                    take(h + 1, 1 - p, "f")
                act.wait_ge(s("slots_ps"), h + 1)
                A(score[:, :], pair(2), ACT.Copy).then_inc(s("slots"), 1)
                if more:
                    take(h + 1, 1 - p, "g")
                    silus(h + 1, 1 - p, True)
                    w_rnorm(h + 1, h if before else None)

            heads(act, head)
            o_square(GH - 1)
            o_log(GH - 1)
            o_rnorm(GH - 1)

        @block.gpsimd
        def _(pool):
            g = nc.gpsimd
            g.memset(zero[:, :], 0.0)
            g.memset(raw[:, :], 0.0)
            g.memset(writes[:, :], 0.0).then_inc(s("zero"), 1)
            pool.wait_ge(s("zero"), 1)

            def head(h, p, before, more):
                pool.wait_ge(s("bw"), h + 1)
                for l in range(LEVELS):
                    left, right = halves(of(prefix, p), l)
                    half = [P, N >> (l + 1), 1 << l]
                    sl = halves(suffix[:, :], l)[0]
                    pool.wait_ge(s("suffix"), LEVELS * h + l + 1)
                    g.tensor_tensor(halves(writes[:, l * N:(l + 1) * N], l)[0], halves(Y(p, "w"), l)[0], sl,
                                    ALU.mult).then_inc(s("writes"), 1)
                    if l == LEVELS - 1:
                        break
                    if l:
                        pool.wait_ge(s("prefix"), (LEVELS - 1) * h + l)
                    else:
                        pool.wait_ge(s("proj_out"), NPROJ * h + NPROJ)
                    end = right[:, :, (1 << l) - 1:1 << l].broadcast_to(half)
                    g.tensor_tensor(sl, sl, end, ALU.mult).then_inc(s("suffix"), 1)
                    pool.wait_ge(s("suffix"), LEVELS * h + l + 2)
                    pool.wait_ge(s("pre"), LEVELS * h + l + 1)
                    end = left[:, :, (1 << l) - 1:1 << l].broadcast_to(half)
                    g.tensor_tensor(right, right, end, ALU.mult).then_inc(s("prefix"), 1)
                pool.wait_ge(s("slots"), h + 1)
                for l in range(LEVELS):
                    if l >= 2:
                        pool.wait_ge(s("aw_pairs_ps"), LEVELS * h + l - 1)
                    g.tensor_tensor(packed(sm[:, (l % 2) * HN:(l % 2 + 1) * HN], l), halves(score[:, :], l)[1],
                                    packed(pre[:, l * HN:(l + 1) * HN], l), ALU.mult).then_inc(s("reads"), 1)

            heads(pool, head)

        @block.vector
        def _(dve):
            v = nc.vector
            dve.wait_ge(s("zero"), 1)

            def conv(f, p, j):
                name = CONV[j]
                dve.wait_ge(s("proj_out"), NPROJ * f + j + 1)
                for tap in range(KW - 1):
                    c = TAPS[name] + tap
                    ins = v.scalar_tensor_tensor(by_batch(Y(p, name)), raws[:, j % 2, :, tap:tap + T], small[:, c:c + 1],
                                                 by_batch(Y(p, name)), ALU.mult, ALU.add)
                    if tap < KW - 2:
                        ins.then_inc(s("tap"), 1)
                        dve.wait_ge(s("tap"), (KW - 2) * (NCONV * f + j) + tap + 1)
                ins.then_inc(s("conv"), 1)

            def times_beta(f, p):
                dve.wait_ge(s("w_squared"), f + 1)
                dve.wait_ge(s("beta"), 16 * f + 16)
                v.tensor_tensor(Y(p, "w"), Y(p, "w"), beta[:, :], ALU.mult).then_inc(s("w_beta"), 1)

            def times_norm(f, p):
                dve.wait_ge(s("w_beta"), f + 1)
                dve.wait_ge(s("w_rnorm"), f + 1)
                v.tensor_tensor(Y(p, "w"), Y(p, "w"), rnorm[:, :], ALU.mult).then_inc(s("bw"), 1)

            def q_times_k(f, p):
                dve.wait_ge(s("silu"), NCONV * f + NCONV)
                dve.wait_ge(s("w_norm_ps"), f + 1)
                v.tensor_tensor(front_sum[:, :], Y(p, "q"), Y(p, "k"), ALU.mult).then_inc(s("qk"), 1)

            def gate_o(h, p):
                dve.wait_ge(s("o_squared"), h + 1)
                dve.wait_ge(s("o_rnorm"), h + 1)
                v.tensor_tensor(o[:, :], o[:, :], rnorm[:, :], ALU.mult).then_inc(s("o_normed"), 1)
                dve.wait_ge(s("o_normed"), h + 1)
                v.scalar_tensor_tensor(o[:, :], o[:, :], vec[:, V_NORM:V_NORM + 1], of(gate, p),
                                       ALU.mult, ALU.mult).then_inc(s("o_gated"), 1)

            def add_out(h, ct):
                dve.wait_ge(s("y_out"), CT * h + ct + 1)
                x = xT[:, ct * N:(ct + 1) * N]
                v.tensor_tensor(x, x, pair(3), ALU.add).then_inc(s("x_added"), 1)

            dve.wait_ge(s("small_weights"), 16)
            for j in range(NCONV):
                conv(0, 0, j)
            times_beta(0, 0)
            times_norm(0, 0)
            q_times_k(0, 0)
            v.memset(suffix[:, :], 1.0).then_inc(s("suffix"), 1)

            def head(h, p, before, more):
                def masked(l, products):
                    m = halves(const[:, K_MASK + l * P:K_MASK + (l + 1) * P], l)[1]
                    m = m.unsqueeze(1).broadcast_to([P, NT, m.shape[1], m.shape[2]])
                    split = dict(i=NT, h=1 << l)
                    return v.tensor_tensor(pairs[:, (l % 2) * HN:(l % 2 + 1) * HN].rearrange("p (i n h) -> p i n h", **split),
                                           products, m, ALU.mult)

                dve.wait_ge(s("kq"), h + 1)
                for l in range(LEVELS + 1):
                    if l < LEVELS - 1:
                        if l >= 2:
                            dve.wait_ge(s("level_ps"), LEVELS * h + l - 1)
                        kq_l = kq[:, 0:N].rearrange("p (i n two h) -> p i n two h", i=NT, two=2, h=1 << l)[:, :, :, 1, :]
                        masked(l, kq_l).then_inc(s("kq_pairs"), 1)
                    if before and l - 1 in OUT:
                        add_out(h - 1, OUT.index(l - 1))
                    if l == 0:
                        dve.wait_ge(s("bw"), h + 1)
                        dve.wait_ge(s("qk_ps"), h + 1)
                        v.scalar_tensor_tensor(score[:, :], pair(2), SCALE, Y(p, "w"), ALU.mult, ALU.mult).then_inc(s("score_diag"), 1)
                    if l >= 1:
                        k = l - 1
                        n = LEVELS * h + k
                        dve.wait_ge(s("level_ps"), n + 1)
                        dve.wait_ge(s("pre"), n + 1)
                        t = tmp[:, (k % 2) * HN:(k % 2 + 1) * HN]
                        v.tensor_tensor(t, ps[:, 4 + k % 2, :], pre[:, k * HN:(k + 1) * HN], ALU.mult).then_inc(s("level_read"), 1)
                        dve.wait_ge(s("level_read"), n + 1)
                        if k:
                            dve.wait_ge(s("score_level"), n)
                        else:
                            dve.wait_ge(s("score_diag"), h + 1)
                        right = halves(score[:, :], k)[1]
                        v.tensor_tensor(right, right, packed(t, k), ALU.add).then_inc(s("score_level"), 1)
                    if before and l == 3:
                        gate_o(h - 1, 1 - p)
                    if more and l - 1 in PROJECT:
                        conv(h + 1, 1 - p, PROJECT[l - 1])

                sv = sm[:, :].rearrange("p (n m) -> p n m", n=NT)
                across = lambda ap: ap.unsqueeze(2).broadcast_to([P, NT, P])
                pv = pair(0).rearrange("p (n m) -> p n m", n=NT)
                dve.wait_ge(s("score_t"), h + 1)
                v.tensor_reduce(stat[:, 0:NT], pv, AX, ALU.max).then_inc(s("max"), 1)
                dve.wait_ge(s("max"), h + 1)
                v.tensor_tensor(sv, pv, across(stat[:, 0:NT]), ALU.subtract).then_inc(s("centred"), 1)
                dve.wait_ge(s("exp"), h + 1)
                v.tensor_reduce(stat[:, NT:2 * NT], sv, AX, ALU.add).then_inc(s("sum"), 1)
                dve.wait_ge(s("sum"), h + 1)
                v.reciprocal(stat[:, 2 * NT:3 * NT], stat[:, NT:2 * NT]).then_inc(s("inverse"), 1)
                dve.wait_ge(s("inverse"), h + 1)
                v.tensor_tensor(sv, sv, across(stat[:, 2 * NT:3 * NT]), ALU.mult).then_inc(s("softmax"), 1)
                if more:
                    conv(h + 1, 1 - p, CONV.index("q"))

                dve.wait_ge(s("slots"), h + 1)
                v.tensor_tensor(tmp[:, :], score[:, :], Y(p, "w"), ALU.mult).then_inc(s("slot_write"), 1)
                for l in range(LEVELS):
                    dve.wait_ge(s("aw_pairs_ps"), LEVELS * h + l + 1)
                    if l >= 2:
                        dve.wait_ge(s("level_out"), LEVELS * h + l - 1)
                    if l < LEVELS - 1:
                        aw = ps[:, l % 2, :].rearrange("p (i n h) -> p i n h", i=NT, h=1 << l)
                        masked(l, aw).then_inc(s("aw_pairs"), 1)
                    else:
                        v.tensor_copy(pairs[:, (l % 2) * HN:(l % 2 + 1) * HN], ps[:, l % 2, :]).then_inc(s("aw_pairs"), 1)
                    if more and l == 1:
                        conv(h + 1, 1 - p, CONV.index("v"))
                    if l == 2:
                        dve.wait_ge(s("slot_write_ps"), h + 1)
                        v.tensor_tensor(own, pair(2), Y(p, "v"), ALU.mult).then_inc(s("own"), 1)
                    if more and l == 3:
                        v.memset(suffix[:, :], 1.0).then_inc(s("suffix"), 1)
                    if more and l == 2:
                        times_beta(h + 1, 1 - p)
                    if more and l == 5:
                        q_times_k(h + 1, 1 - p)
                    if more and l == 6:
                        times_norm(h + 1, 1 - p)
                dve.wait_ge(s("own"), h + 1)
                dve.wait_ge(s("level_out"), LEVELS * h + LEVELS)
                v.tensor_tensor(o[:, :], pair(3), own, ALU.add).then_inc(s("o"), 1)

            heads(dve, head)
            gate_o(GH - 1, 1)
            for ct in range(CT):
                add_out(GH - 1, ct)
            dve.wait_ge(s("x_added"), CT * GH)

def rmsnorm(nc, env, dst, col):
    vec, hT, ones, eps, ps = (env[k] for k in ("vec", "hT", "ones", "eps", "ps"))
    with ExitStack() as ctx:
        s = Signals(nc, ctx, env, f"rms{col}")
        square = ctx.enter_context(nc.sbuf_tensor(f"square{col}", [P, CT * N], F32))
        rnorm = ctx.enter_context(nc.sbuf_tensor(f"rms_rnorm{col}", [P, N], F32))
        block = ctx.enter_context(nc.Block())

        @block.scalar
        def _(act):
            nc.scalar.activation(square[:, :], hT[:, :], ACT.Square).then_inc(s("square"), 1)
            act.wait_ge(s("sum"), 1)
            nc.scalar.activation(rnorm[:, :], ps[:, 0:2, :].rearrange("p a b -> p (a b)"), ACT.Ln, bias=eps[:, 1:2],
                                 scale=1.0 / C).then_inc(s("log"), 1)
            act.wait_ge(s("log"), 1)
            nc.scalar.activation(rnorm[:, :], rnorm[:, :], ACT.Exp, scale=-0.5).then_inc(s("rnorm"), 1)

        @block.tensor
        def _(pe):
            pe.wait_ge(s("square"), 1)
            for half in range(2):
                for kt in range(CT):
                    last = nc.tensor.matmul(ps[:, half, :], ones[:, :], square[:, kt * N + half * HN:kt * N + (half + 1) * HN],
                                            start=kt == 0, stop=kt == CT - 1)
            last.then_inc(s("sum"), 1)

        @block.vector
        def _(dve):
            dve.wait_ge(s("rnorm"), 1)
            for ct in range(CT):
                c = slice(ct * N, (ct + 1) * N)
                nc.vector.scalar_tensor_tensor(dst[:, c], hT[:, c], vec[:, col + ct:col + ct + 1], rnorm[:, :],
                                               ALU.mult, ALU.mult).then_inc(s("out"), 1)
            dve.wait_ge(s("out"), CT)


def moe(nc, a, env, layer):
    xT, const, vec, hT, ps = (env[k] for k in ("xT", "const", "vec", "hT", "ps"))
    packs = a[f"moe{layer}"]
    NE = 8
    NI = a[f"moe{layer}"].shape[0] // NE
    CHUNK = 3 * C
    W1, W3, W2 = 0, C, 2 * C
    UNITS = 2 * NI
    TH = NT // 2
    assert UNITS % 2 == 0 and NE % 2 == 0
    with ExitStack() as ctx:
        sb = lambda name, cols: ctx.enter_context(nc.sbuf_tensor(f"{name}_moe{layer}", [P, cols], F32))
        acc = sb("acc", NT * C)
        if layer:
            rmsnorm(nc, env, acc, V_FFLN)
            src = acc
        else:
            src = hT
        s = Signals(nc, ctx, env, f"moe{layer}")
        sbr = lambda name, cols: ctx.enter_context(nc.sbuf_tensor(f"{name}_moe{layer}", [P, cols], F32R))
        chunks = sb("chunks", 2 * CHUNK)
        w_high, w_low = (sbr(name, 2 * NI * CHUNK) for name in ("w_high", "w_low"))
        src_high, src_low = (sbr(name, CT * N) for name in ("src_high", "src_low"))
        hid_high, hid_low = (sbr(name, NI * N) for name in ("hid_high", "hid_low"))
        silu = sb("silu", 2 * HN)
        comb = sb("comb", NE * NT)
        mine = sb("mine", 2 * NT)
        rt = {k: sb("rt_" + k, NT * NE) for k in ("logits", "abs", "hot1", "hot2", "a", "b", "c")}
        st = {k: sb("st_" + k, NT) for k in ("max1", "max2", "index", "gate1", "gate2", "sum")}
        block = ctx.enter_context(nc.Block())
        gate_col = V_GATE1 if layer else V_GATE0

        def experts(engine, body):
            with engine.Fori(0, NE // 2 - 1) as i:
                body(2 * i, 0, True)
                body(2 * i + 1, 1, True)
            body(NE - 2, 0, True)
            body(NE - 1, 1, False)

        @block.sync
        def _(sp):
            for slot in range(2):
                sp.dma_start(chunks[:, slot * CHUNK:(slot + 1) * CHUNK], packs[slot]).then_inc(s(f"chunk{slot}"), 16)
            with sp.Fori(0, NE * NI // 2 - 1) as i:
                for slot in range(2):
                    sp.wait_ge(s("split"), 2 * i + slot + 1)
                    nxt = packs[bass.ds(2 * i + slot + 2, 1)].rearrange("o p n -> p (o n)")
                    sp.dma_start(chunks[:, slot * CHUNK:(slot + 1) * CHUNK], nxt).then_inc(s(f"chunk{slot}"), 16)
            if layer:
                out = a["out"].rearrange("(n p) c -> p n c", p=P)
                sp.wait_ge(s("final"), 1)
                sp.dma_start(out, acc[:, :].rearrange("p (n c) -> p n c", n=NT)).then_inc(s("stored"), 16)
                sp.wait_ge(s("stored"), 16)

        @block.tensor
        def _(pe):
            mm = nc.tensor.matmul
            for n in range(NT):
                for kt in range(CT):
                    last = mm(ps[:, 7, n * NE:(n + 1) * NE], src[:, kt * N + n * P:kt * N + (n + 1) * P],
                              vec[:, gate_col + kt * NE:gate_col + (kt + 1) * NE], start=kt == 0, stop=kt == CT - 1)
            last.then_inc(s("logits_ps"), 1)
            pe.sem_inc(s("y_ps"), 1)
            pe.wait_ge(s("src_low"), 1)
            with pe.Fori(0, NE // 2) as i:
                for slot in range(2):
                    e = 2 * i + slot
                    for u in range(UNITS):
                        half, it = divmod(u, NI)
                        if not half:
                            pe.wait_ge(s("split"), NI * e + it + 1)
                        pe.wait_ge(s("up_free"), UNITS * e + u + 1)
                        for bank, base in ((u % 2, W1), (2 + u % 2, W3)):
                            for kt in range(CT):
                                c = (slot * NI + it) * CHUNK + base + kt * P
                                r = slice(kt * N + half * HN, kt * N + (half + 1) * HN)
                                mm(ps[:, bank, :], w_high[:, c:c + P], src_high[:, r], start=kt == 0, stop=False)
                                mm(ps[:, bank, :], w_high[:, c:c + P], src_low[:, r], start=False, stop=False)
                                last = mm(ps[:, bank, :], w_low[:, c:c + P], src_high[:, r], start=False, stop=kt == CT - 1)
                            if base == W1:
                                last.then_inc(s("up1_ps"), 1)
                        last.then_inc(s("up3_ps"), 1)
                    for n in range(NT):
                        half = n // TH
                        pe.wait_ge(s("hidden"), UNITS * e + NI * (half + 1) + 2)
                        pe.wait_ge(s("y_free"), NT * e + n + 1)
                        y = ps[:, 4 + n % 4, 0:C]
                        for it in range(NI):
                            h = slice(it * N + n * P, it * N + (n + 1) * P)
                            w2 = slice((slot * NI + it) * CHUNK + W2, (slot * NI + it) * CHUNK + W2 + C)
                            mm(y, hid_high[:, h], w_high[:, w2], start=it == 0, stop=False)
                            mm(y, hid_high[:, h], w_low[:, w2], start=False, stop=False)
                            last = mm(y, hid_low[:, h], w_high[:, w2], start=False, stop=it == NI - 1)
                        last.then_inc(s("y_ps"), 1)
            ident = const[:, K_ID:K_ID + P]
            if layer:
                pe.wait_ge(s("streams"), 1)
                for n in range(NT):
                    for ct in range(CT):
                        last = nc.tensor.transpose(ps[:, n // 2, (n % 2) * C + ct * P:(n % 2) * C + (ct + 1) * P],
                                                   xT[:, ct * N + n * P:ct * N + (n + 1) * P], ident)
            else:
                pe.wait_ge(s("y_free"), NT * NE + 4)
                for n in range(NT):
                    for ct in range(CT):
                        last = nc.tensor.transpose(ps[:, 2 * ct + n // 4, (n % 4) * P:(n % 4 + 1) * P],
                                                   acc[:, n * C + ct * P:n * C + (ct + 1) * P], ident)
            last.then_inc(s("turned"), 1)

        @block.scalar
        def _(act):
            def split(e, slot, it):
                place = slot * NI + it
                act.wait_ge(s(f"chunk{place % 2}"), 8 * NI * (e - slot) + 16 * (place // 2 + 1))
                nc.scalar.activation(w_high[:, place * CHUNK:(place + 1) * CHUNK], chunks[:, place % 2 * CHUNK:(place % 2 + 1) * CHUNK],
                                     ACT.Copy).then_inc(s("w_high"), 1)

            nc.scalar.activation(src_high[:, :], src[:, :], ACT.Copy).then_inc(s("src_high"), 1)
            for it in range(NI):
                split(0, 0, it)
            act.wait_ge(s("exp_in"), 1)
            if layer:
                nc.scalar.activation(st["gate2"][:, :], st["gate2"][:, :], ACT.Exp).then_inc(s("exp"), 1)
            else:
                nc.scalar.activation(rt["b"][:, :], rt["b"][:, :], ACT.Exp).then_inc(s("exp"), 1)
                act.wait_ge(s("exp_in"), 2)
                nc.scalar.activation(rt["b"][:, :], rt["b"][:, :], ACT.Exp).then_inc(s("exp"), 1)

            def expert(e, slot, more):
                for u in range(UNITS):
                    act.wait_ge(s("up1_ps"), UNITS * e + u + 1)
                    act.wait_ge(s("hidden"), UNITS * e + u + 1)
                    nc.scalar.activation(silu[:, (u % 2) * HN:(u % 2 + 1) * HN], ps[:, u % 2, :],
                                         ACT.Silu).then_inc(s("silu"), 1)
                    if more and u % 2:
                        if u == 1:
                            act.wait_ge(s("y_ps"), NT * e + 1)
                        split(e + 1, 1 - slot, u // 2)

            experts(act, expert)

        @block.gpsimd
        def _(pool):
            def split(e, slot, it):
                place = slot * NI + it
                pool.wait_ge(s("w_high"), NI * e + it + 1)
                w = slice(place * CHUNK, (place + 1) * CHUNK)
                nc.gpsimd.tensor_tensor(w_low[:, w], chunks[:, place % 2 * CHUNK:(place % 2 + 1) * CHUNK],
                                        w_high[:, w], ALU.subtract).then_inc(s("split"), 1)

            with pool.Fori(0, NE // 2) as i:
                for slot in range(2):
                    for it in range(NI):
                        split(2 * i + slot, slot, it)

        @block.vector
        def _(dve):
            v = nc.vector
            steps = [0]

            def step(ins):
                steps[0] += 1
                ins.then_inc(s("dve_step"), 1)
                dve.wait_ge(s("dve_step"), steps[0])

            by_tile = lambda t: t[:, :].rearrange("p (n e) -> p n e", e=NE)
            each = lambda t: t[:, :].unsqueeze(2).broadcast_to([P, NT, NE])
            rank = const[:, K_RANK:K_RANK + NE].unsqueeze(1).broadcast_to([P, NT, NE])
            L, AB, H1, H2, TA, TB, TC = (by_tile(rt[k]) for k in ("logits", "abs", "hot1", "hot2", "a", "b", "c"))
            dve.sem_inc(s("up_free"), 2)
            dve.sem_inc(s("hidden"), 2)
            dve.wait_ge(s("logits_ps"), 1)
            step(v.tensor_copy(rt["logits"][:, :], ps[:, 7, 0:NT * NE]))
            dve.wait_ge(s("src_high"), 1)
            v.tensor_tensor(src_low[:, :], src[:, :], src_high[:, :], ALU.subtract).then_inc(s("src_low"), 1)
            dve.wait_ge(s("src_low"), 1)
            v.memset(acc[:, :], 0.0).then_inc(s("y_free"), 4)

            def first_max(scores, top, hot):
                step(v.tensor_reduce(st[top][:, :], scores, AX, ALU.max))
                step(v.tensor_tensor(TA, scores, each(st[top]), ALU.is_equal))
                step(v.tensor_tensor(TA, TA, rank, ALU.mult))
                step(v.tensor_reduce(st["index"][:, :], TA, AX, ALU.max))
                step(v.tensor_tensor(hot, rank, each(st["index"]), ALU.is_equal))

            def sparse_gate(scores, top, gate, n):
                step(v.tensor_tensor(TA, AB, each(st[top]), ALU.max))
                step(v.tensor_scalar(rt["a"][:, :], rt["a"][:, :], 0.02, None, ALU.mult))
                step(v.tensor_tensor(TB, scores, each(st[top]), ALU.subtract))
                step(v.tensor_scalar(rt["c"][:, :], rt["b"][:, :], -1.0, None, ALU.mult))
                step(v.tensor_tensor(TA, TC, TA, ALU.is_le))
                v.tensor_copy(st["index"][:, :], st[top][:, :]).then_inc(s("exp_in"), 1)
                dve.wait_ge(s("exp"), n)
                step(v.tensor_tensor(TB, TB, TA, ALU.mult))
                step(v.tensor_reduce(st["sum"][:, :], TB, AX, ALU.add))
                step(v.reciprocal(st[gate][:, :], st["sum"][:, :]))

            first_max(L, "max1", H1)
            if layer:
                step(v.scalar_tensor_tensor(TC, H1, -BIG, L, ALU.mult, ALU.add))
                first_max(TC, "max2", H2)
                v.tensor_tensor(st["gate2"][:, :], st["max2"][:, :], st["max1"][:, :], ALU.subtract).then_inc(s("exp_in"), 1)
                dve.wait_ge(s("exp"), 1)
                step(v.tensor_scalar(st["sum"][:, :], st["gate2"][:, :], 1.0, None, ALU.add))
                step(v.reciprocal(st["gate1"][:, :], st["sum"][:, :]))
                step(v.tensor_tensor(st["gate2"][:, :], st["gate2"][:, :], st["gate1"][:, :], ALU.mult))
            else:
                step(v.scalar_tensor_tensor(rt["abs"][:, :], rt["logits"][:, :], -1.0, rt["logits"][:, :], ALU.mult, ALU.max))
                sparse_gate(L, "max1", "gate1", 1)
                step(v.scalar_tensor_tensor(TC, H1, -BIG, L, ALU.mult, ALU.add))
                step(v.tensor_copy(rt["logits"][:, :], rt["c"][:, :]))
                first_max(L, "max2", H2)
                sparse_gate(L, "max2", "gate2", 2)
            step(v.tensor_tensor(H1, H1, each(st["gate1"]), ALU.mult))
            step(v.tensor_tensor(H2, H2, each(st["gate2"]), ALU.mult))
            step(v.tensor_tensor(comb[:, :].rearrange("p (e n) -> p n e", e=NE), H1, H2, ALU.add))
            with dve.Fori(0, NE // 2) as i:
                for slot in range(2):
                    e = 2 * i + slot
                    v.tensor_copy(mine[:, slot * NT:(slot + 1) * NT], comb[:, bass.ds(e * NT, NT)]).then_inc(s("mine"), 1)
                    for u in range(UNITS):
                        half, it = divmod(u, NI)
                        dve.wait_ge(s("silu"), UNITS * e + u + 1)
                        dve.wait_ge(s("up3_ps"), UNITS * e + u + 1)
                        c = slice(it * N + half * HN, it * N + (half + 1) * HN)
                        full = silu[:, (u % 2) * HN:(u % 2 + 1) * HN]
                        v.tensor_tensor(full, full, ps[:, 2 + u % 2, :], ALU.mult).then_inc(s("up_free"), 1)
                        if u == 0:
                            dve.wait_ge(s("y_ps"), NT * e + 1)
                        dve.wait_ge(s("up_free"), UNITS * e + u + 3)
                        v.tensor_copy(hid_high[:, c], full).then_inc(s("hid_high"), 1)
                        dve.wait_ge(s("hid_high"), UNITS * e + u + 1)
                        v.tensor_tensor(hid_low[:, c], full, hid_high[:, c], ALU.subtract).then_inc(s("hidden"), 1)
                    dve.wait_ge(s("mine"), e + 1)
                    for n in range(NT):
                        dve.wait_ge(s("y_ps"), NT * e + n + 2)
                        dve.wait_ge(s("y_free"), NT * e + n + 4)
                        tile = acc[:, n * C:(n + 1) * C]
                        c = slot * NT + n
                        v.scalar_tensor_tensor(tile, ps[:, 4 + n % 4, 0:C], mine[:, c:c + 1], tile, ALU.mult,
                                               ALU.add).then_inc(s("y_free"), 1)
            if layer:
                dve.wait_ge(s("y_ps"), NT * NE + 1)
                v.tensor_tensor(xT[:, :], xT[:, :], hT[:, :], ALU.add).then_inc(s("streams"), 1)
                dve.wait_ge(s("turned"), 1)
                dve.wait_ge(s("y_free"), NT * NE + 4)
                v.tensor_tensor(acc[:, :], acc[:, :], ps[:, 0:4, :].rearrange("p a b -> p (a b)"), ALU.add).then_inc(s("final"), 1)
                dve.wait_ge(s("final"), 1)
            else:
                dve.wait_ge(s("turned"), 1)
                v.tensor_tensor(xT[:, :], xT[:, :], ps[:, 0:4, :].rearrange("p a b -> p (a b)"), ALU.add).then_inc(s("final"), 1)
                dve.wait_ge(s("final"), 1)


SEG = 3 * P


def softmax_groups(nc, dve, s, first_group, count, env, probs, stat, scale):
    const, ps = env["const"], env["ps"]
    v = nc.vector
    mask = const[:, K_CAUSAL:K_CAUSAL + SEG].unsqueeze(1).broadcast_to([P, 4, SEG])
    each = lambda ap, part: ap[:, 4 * part:4 * part + 4].unsqueeze(2).broadcast_to([P, 4, P * (part + 1)])
    for n in range(count + 1):
        if n < count:
            g = first_group + n
            p, parts, top, total, inverse = softmax_buffers(probs, stat, n % 2)
            dve.wait_ge(s("scores_ps"), g + 1)
            v.scalar_tensor_tensor(p, ps[:, 0:4, 0:SEG], scale, mask, ALU.mult, ALU.add).then_inc(s("masked"), 1)
            dve.wait_ge(s("masked"), g + 2)
            v.tensor_reduce(top[:, 0:4], parts[0], AX, ALU.max)
            v.tensor_reduce(top[:, 4:8], parts[1], AX, ALU.max).then_inc(s("max"), 1)
            dve.wait_ge(s("max"), g + 1)
            v.tensor_scalar(top, top, -1.0, None, ALU.mult).then_inc(s("minus_max"), 1)
        if n:
            g = first_group + n - 1
            p, parts, top, total, inverse = softmax_buffers(probs, stat, (n - 1) % 2)
            dve.wait_ge(s("exp"), g + 1)
            v.reciprocal(inverse, total).then_inc(s("inverse"), 1)
            dve.wait_ge(s("inverse"), g + 1)
            v.tensor_tensor(parts[0], parts[0], each(inverse, 0), ALU.mult)
            v.tensor_tensor(parts[1], parts[1], each(inverse, 1), ALU.mult).then_inc(s("probs"), 1)


def softmax_buffers(probs, stat, buf):
    p = probs[:, buf * 4 * SEG:(buf + 1) * 4 * SEG].rearrange("p (u k) -> p u k", u=4)
    stats = [stat[:, (buf * 3 + i) * 8:(buf * 3 + i + 1) * 8] for i in range(3)]
    return p, (p[:, :, 0:P], p[:, :, P:SEG]), *stats


def softmax_exp(nc, act, s, g, buf, probs, stat):
    p, parts, top, total, inverse = softmax_buffers(probs, stat, buf)
    act.wait_ge(s("minus_max"), g + 1)
    for part in range(2):
        for u in range(4):
            c = 4 * part + u
            last = nc.scalar.activation(parts[part][:, u, :], parts[part][:, u, :], ACT.Exp, bias=top[:, c:c + 1],
                                        accum_out=total[:, c:c + 1])
    last.then_inc(s("exp"), 1)


def turn_probs(nc, pe, s, g, buf, env, probs):
    ps, ident = env["ps"], env["const"][:, K_ID:K_ID + P]
    pe.wait_ge(s("probs"), g + 1)
    for piece in range(3):
        for u in range(4):
            c = (buf * 4 + u) * SEG + piece * P
            last = nc.tensor.transpose(ps[:, 4 + piece, u * P:(u + 1) * P], probs[:, c:c + P], ident)
    last.then_inc(s("turned"), 1)


def attention1(nc, a, env):
    xT, const, hT, ps = (env[k] for k in ("xT", "const", "hT", "ps"))
    HD = 16
    with ExitStack() as ctx:
        s = Signals(nc, ctx, env, "a1")
        sb = lambda name, cols: ctx.enter_context(nc.sbuf_tensor(name, [P, cols], F32))
        wkv = sb("wkv", 4 * P)
        wq = sb("wq", 2 * P)
        wo = sb("wo1", C)
        kT = sb("kT", N)
        qT = sb("qT", N)
        plain = sb("plain", N)
        spin = sb("spin", N)
        values = sb("values", N)
        probs = sb("probs", 2 * 4 * SEG)
        probs_t = sb("probs_t", 2 * 4 * SEG)
        stat = sb("stat1", 48)
        oT = sb("oT", N)
        block = ctx.enter_context(nc.Block())
        flat = lambda ap: ap.rearrange("p a b -> p (a b)")
        by_batch = lambda ap: ap.rearrange("p (b t) -> p b t", b=B)
        packs = a["att1"]

        @block.sync
        def _(sp):
            sp.dma_start(wkv[:, :], a["att1_kv"]).then_inc(s("kv_weights"), 16)
            sp.dma_start(wq[:, :], packs[0, :, 0:2 * P]).then_inc(s("q_weights"), 16)
            sp.dma_start(wo[:, :], packs[0, :, 2 * P:2 * P + C]).then_inc(s("o_weights"), 16)
            with sp.Fori(0, 3) as t:
                nxt = packs[bass.ds(t + 1, 1)].rearrange("o p n -> p (o n)")
                sp.wait_ge(s("plain_ps"), t + 2)
                sp.dma_start(wq[:, :], nxt[:, 0:2 * P]).then_inc(s("q_weights"), 16)
                sp.wait_ge(s("y_ps"), t + 1)
                sp.dma_start(wo[:, :], nxt[:, 2 * P:2 * P + C]).then_inc(s("o_weights"), 16)

        @block.tensor
        def _(pe):
            mm = nc.tensor.matmul

            def rope(w, n):
                for half in range(2):
                    for kt in range(CT):
                        last = mm(ps[:, half, :], w[:, kt * P:(kt + 1) * P], hT[:, kt * N + half * HN:kt * N + (half + 1) * HN],
                                  start=kt == 0, stop=kt == CT - 1)
                last.then_inc(s("plain_ps"), 1)
                pe.wait_ge(s("plain"), n + 1)
                for half in range(2):
                    last = mm(ps[:, 2 + half, :], const[:, K_ROT1:K_ROT1 + P], plain[:, half * HN:(half + 1) * HN], start=True, stop=True)
                last.then_inc(s("rotated_ps"), 1)

            pe.wait_ge(s("kv_weights"), 16)
            for n in range(NT):
                for kt in range(CT):
                    last = mm(ps[:, 4 + n // 4, (n % 4) * P:(n % 4 + 1) * P], hT[:, kt * N + n * P:kt * N + (n + 1) * P],
                              wkv[:, (2 + kt) * P:(3 + kt) * P], start=kt == 0, stop=kt == CT - 1)
            last.then_inc(s("values_ps"), 1)
            rope(wkv, 0)
            pe.wait_ge(s("roped"), 1)
            pe.wait_ge(s("values"), 1)

            def scores(t, b):
                g = B * t + b
                pe.wait_ge(s("masked"), g + 1)
                if b == 0:
                    pe.wait_ge(s("roped"), t + 2)
                for u in range(4):
                    rows = slice(32 * u, 32 * u + HD)
                    for q, (c, k) in enumerate(((0, P), (P, 2 * P))):
                        last = mm(ps[:, u, c:c + k], qT[rows, b * T + q * P:b * T + (q + 1) * P], kT[rows, b * T:b * T + k],
                                  start=True, stop=True)
                last.then_inc(s("scores_ps"), 1)

            def weigh(t, b):
                g = B * t + b
                pe.wait_ge(s("probs_t"), g + 1)
                pe.wait_ge(s("o"), g + 1)
                for u in range(4):
                    rows = slice(32 * u, 32 * (u + 1))
                    for piece, (tile, q) in enumerate(((0, 0), (0, 1), (1, 1))):
                        c = (b % 2) * 4 * SEG + (piece * 4 + u) * P
                        last = mm(ps[rows, 7, q * P:(q + 1) * P], values[:, (2 * b + tile) * P + 32 * u:(2 * b + tile) * P + 32 * (u + 1)],
                                  probs_t[:, c:c + P], start=piece < 2, stop=piece != 1, skip_group_check=True)
                last.then_inc(s("o_ps"), 1)

            with pe.Fori(0, 4) as t:
                pe.wait_ge(s("q_weights"), 16 * t + 16)
                rope(wq, t + 1)
                scores(t, 0)
                scores(t, 1)
                pe.wait_ge(s("x_added"), t + 1)
                for b in range(B):
                    turn_probs(nc, pe, s, B * t + b, b % 2, env, probs)
                    if b + 2 < B:
                        scores(t, b + 2)
                    weigh(t, b)
                pe.wait_ge(s("o"), B * t + B + 1)
                pe.wait_ge(s("o_weights"), 16 * t + 16)
                for ct in range(CT):
                    for half in range(2):
                        last = mm(ps[:, 4 + 2 * ct + half, :], wo[:, ct * P:(ct + 1) * P], oT[:, half * HN:(half + 1) * HN],
                                  start=True, stop=True)
                last.then_inc(s("y_ps"), 1)

        @block.scalar
        def _(act):
            A = nc.scalar.activation
            act.sem_inc(s("o"), 1)
            act.wait_ge(s("values_ps"), 1)
            A(values[:, :], flat(ps[:, 4:6, :]), ACT.Copy).then_inc(s("values"), 1)
            act.wait_ge(s("plain_ps"), 1)
            A(plain[:, :], flat(ps[:, 0:2, :]), ACT.Copy).then_inc(s("plain"), 1)
            with act.Fori(0, 4) as t:
                act.wait_ge(s("plain_ps"), t + 2)
                act.wait_ge(s("roped"), t + 1)
                A(plain[:, :], flat(ps[:, 0:2, :]), ACT.Copy).then_inc(s("plain"), 1)
                for b in range(B + 1):
                    if b < B:
                        softmax_exp(nc, act, s, B * t + b, b % 2, probs, stat)
                    if b:
                        g = B * t + b - 1
                        act.wait_ge(s("turned"), g + 1)
                        p = probs_t[:, ((b - 1) % 2) * 4 * SEG:((b - 1) % 2 + 1) * 4 * SEG]
                        A(p, flat(ps[:, 4:7, :]), ACT.Copy).then_inc(s("probs_t"), 1)
                        act.wait_ge(s("o_ps"), g + 1)
                        A(oT[:, (b - 1) * T:b * T], ps[:, 7, 0:T], ACT.Copy).then_inc(s("o"), 1)

        @block.vector
        def _(dve):
            v = nc.vector

            def rope(dst, n):
                cos, sin = (over_batches(const[:, k:k + T]) for k in (K_COS1, K_SIN1))
                dve.wait_ge(s("plain"), n + 1)
                v.tensor_tensor(by_batch(dst[:, :]), by_batch(plain[:, :]), cos, ALU.mult).then_inc(s("cos"), 1)
                dve.wait_ge(s("rotated_ps"), n + 1)
                v.tensor_tensor(by_batch(spin[:, :]), by_batch(flat(ps[:, 2:4, :])), sin, ALU.mult).then_inc(s("sin"), 1)
                dve.wait_ge(s("cos"), n + 1)
                dve.wait_ge(s("sin"), n + 1)
                v.tensor_tensor(dst[:, :], dst[:, :], spin[:, :], ALU.add).then_inc(s("roped"), 1)

            rope(kT, 0)
            dve.sem_inc(s("masked"), 1)
            dve.sem_inc(s("x_added"), 1)
            with dve.Fori(0, 4) as t:
                rope(qT, t + 1)
                softmax_groups(nc, dve, s, B * t, B, env, probs, stat, float(HD) ** -0.5)
                dve.wait_ge(s("y_ps"), t + 1)
                v.tensor_tensor(xT[:, :], xT[:, :], flat(ps[:, 4:8, :]), ALU.add).then_inc(s("x_added"), 1)
                dve.wait_ge(s("x_added"), t + 2)


def attention2(nc, a, env):
    const, hT, ps = (env[k] for k in ("const", "hT", "ps"))
    KV, REP = 4, 4
    with ExitStack() as ctx:
        sb = lambda name, cols: ctx.enter_context(nc.sbuf_tensor(name, [P, cols], F32))
        nT = sb("nT", CT * N)
        rmsnorm(nc, env, nT, V_LN)
        s = Signals(nc, ctx, env, "a2")
        wp = sb("wp", (2 + REP) * C)
        wo = sb("wo2", REP * C)
        kT = sb("kT2", N)
        qT = sb("qT2", REP * N)
        plain = sb("plain2", 2 * N)
        spin = sb("spin2", N)
        values = sb("values2", N)
        probs = sb("probs2", 2 * 4 * SEG)
        probs_t = sb("probs_t2", 4 * SEG)
        stat = sb("stat2", 48)
        oT = sb("oT2", REP * N)
        block = ctx.enter_context(nc.Block())
        flat = lambda ap: ap.rearrange("p a b -> p (a b)")
        by_batch = lambda ap: ap.rearrange("p (b t) -> p b t", b=B)
        packs = a["att2"]
        WP = (2 + REP) * C
        ROPES = 1 + REP

        @block.sync
        def _(sp):
            sp.dma_start(wp[:, :], packs[0, :, 0:WP]).then_inc(s("p_weights"), 16)
            sp.dma_start(wo[:, :], packs[0, :, WP:WP + REP * C]).then_inc(s("o_weights"), 16)
            with sp.Fori(0, KV - 1) as kv:
                nxt = packs[bass.ds(kv + 1, 1)].rearrange("o p n -> p (o n)")
                sp.wait_ge(s("plain_ps"), ROPES * kv + ROPES)
                sp.dma_start(wp[:, :], nxt[:, 0:WP]).then_inc(s("p_weights"), 16)
                sp.wait_ge(s("y_ps"), 2 * kv + 2)
                sp.dma_start(wo[:, :], nxt[:, WP:WP + REP * C]).then_inc(s("o_weights"), 16)

        @block.tensor
        def _(pe):
            mm = nc.tensor.matmul
            with pe.Fori(0, KV) as kv:
                def project(r):
                    w = wp[:, (0 if r == 0 else (1 + r) * C):]
                    if r >= 2:
                        pe.wait_ge(s("plain"), ROPES * kv + r - 1)
                    for half in range(2):
                        for kt in range(CT):
                            last = mm(ps[:, 4 * (r % 2) + half, :], w[:, kt * P:(kt + 1) * P],
                                      nT[:, kt * N + half * HN:kt * N + (half + 1) * HN], start=kt == 0, stop=kt == CT - 1)
                    last.then_inc(s("plain_ps"), 1)

                pe.wait_ge(s("p_weights"), 16 * kv + 16)
                pe.wait_ge(s("masked"), REP * kv + 1)
                project(0)
                pe.wait_ge(s("h_added"), 2 * kv + 1)
                for n in range(NT):
                    for kt in range(CT):
                        last = mm(ps[:, 6 + n // 4, (n % 4) * P:(n % 4 + 1) * P], nT[:, kt * N + n * P:kt * N + (n + 1) * P],
                                  wp[:, C + kt * P:C + (kt + 1) * P], start=kt == 0, stop=kt == CT - 1)
                last.then_inc(s("values_ps"), 1)
                for r in range(ROPES):
                    if r + 1 < ROPES:
                        project(r + 1)
                    if r == 1:
                        pe.wait_ge(s("values"), kv + 1)
                    pe.wait_ge(s("plain"), ROPES * kv + r + 1)
                    if r >= 2:
                        pe.wait_ge(s("roped"), ROPES * kv + r)
                    for half in range(2):
                        last = mm(ps[:, 4 * (r % 2) + 2 + half, :], const[:, K_ROT2:K_ROT2 + P],
                                  plain[:, (r % 2) * N + half * HN:(r % 2) * N + (half + 1) * HN], start=True, stop=True)
                    last.then_inc(s("rotated_ps"), 1)

                def scores(j):
                    pe.wait_ge(s("masked"), REP * kv + j + 1)
                    if j == 0:
                        pe.wait_ge(s("roped"), ROPES * kv + ROPES + 1)
                    for u in range(B):
                        for q, (c, k) in enumerate(((0, P), (P, 2 * P))):
                            last = mm(ps[:, u, c:c + k], qT[:, j * N + u * T + q * P:j * N + u * T + (q + 1) * P],
                                      kT[:, u * T:u * T + k], start=True, stop=True)
                    last.then_inc(s("scores_ps"), 1)

                def weigh(j):
                    g = REP * kv + j
                    pe.wait_ge(s("probs_t"), g + 1)
                    for u in range(B):
                        for piece, (tile, q) in enumerate(((0, 0), (0, 1), (1, 1))):
                            c = (piece * 4 + u) * P
                            col = (u % 2) * T + q * P
                            last = mm(ps[:, 4 + u // 2, col:col + P], values[:, (2 * u + tile) * P:(2 * u + tile + 1) * P],
                                      probs_t[:, c:c + P], start=piece < 2, stop=piece != 1, skip_group_check=True)
                    last.then_inc(s("o_ps"), 1)

                scores(0)
                scores(1)
                for j in range(REP):
                    g = REP * kv + j
                    pe.wait_ge(s("o"), g + 1)
                    turn_probs(nc, pe, s, g, j % 2, env, probs)
                    if j + 2 < REP:
                        scores(j + 2)
                    weigh(j)
                pe.wait_ge(s("o"), REP * kv + REP + 1)
                pe.wait_ge(s("o_weights"), 16 * kv + 16)
                for ct in range(CT):
                    for half in range(2):
                        for j in range(REP):
                            last = mm(ps[:, 6 - 2 * ct + half, :], wo[:, j * C + ct * P:j * C + (ct + 1) * P],
                                      oT[:, j * N + half * HN:j * N + (half + 1) * HN], start=j == 0, stop=j == REP - 1)
                    last.then_inc(s("y_ps"), 1)

        @block.scalar
        def _(act):
            A = nc.scalar.activation
            act.sem_inc(s("o"), 1)
            with act.Fori(0, KV) as kv:
                act.wait_ge(s("values_ps"), kv + 1)
                A(values[:, :], flat(ps[:, 6:8, :]), ACT.Copy).then_inc(s("values"), 1)
                for r in range(ROPES):
                    n = ROPES * kv + r
                    act.wait_ge(s("plain_ps"), n + 1)
                    act.wait_ge(s("roped"), ROPES * kv + max(r - 1, 0) + 1)
                    A(plain[:, (r % 2) * N:(r % 2 + 1) * N], flat(ps[:, 4 * (r % 2):4 * (r % 2) + 2, :]), ACT.Copy).then_inc(s("plain"), 1)
                for j in range(REP + 1):
                    if j < REP:
                        softmax_exp(nc, act, s, REP * kv + j, j % 2, probs, stat)
                    if j:
                        g = REP * kv + j - 1
                        act.wait_ge(s("turned"), g + 1)
                        A(probs_t[:, :], flat(ps[:, 4:7, :]), ACT.Copy).then_inc(s("probs_t"), 1)
                        act.wait_ge(s("o_ps"), g + 1)
                        A(oT[:, (j - 1) * N:j * N], flat(ps[:, 4:6, :]), ACT.Copy).then_inc(s("o"), 1)

        @block.vector
        def _(dve):
            v = nc.vector
            cos, sin = (over_batches(const[:, k:k + T]) for k in (K_COS2, K_SIN2))
            for free in ("masked", "roped", "h_added"):
                dve.sem_inc(s(free), 1)
            with dve.Fori(0, KV) as kv:
                for r in range(ROPES):
                    n = ROPES * kv + r
                    dst = kT[:, :] if r == 0 else qT[:, (r - 1) * N:r * N]
                    dve.wait_ge(s("plain"), n + 1)
                    v.tensor_tensor(by_batch(dst), by_batch(plain[:, (r % 2) * N:(r % 2 + 1) * N]), cos, ALU.mult).then_inc(s("cos"), 1)
                    dve.wait_ge(s("rotated_ps"), n + 1)
                    dve.wait_ge(s("roped"), n + 1)
                    rotated = flat(ps[:, 4 * (r % 2) + 2:4 * (r % 2) + 4, :])
                    v.tensor_tensor(by_batch(spin[:, :]), by_batch(rotated), sin, ALU.mult).then_inc(s("sin"), 1)
                    dve.wait_ge(s("cos"), n + 1)
                    dve.wait_ge(s("sin"), n + 1)
                    v.tensor_tensor(dst, dst, spin[:, :], ALU.add).then_inc(s("roped"), 1)
                softmax_groups(nc, dve, s, REP * kv, REP, env, probs, stat, float(P) ** -0.5)
                for ct in range(CT):
                    dve.wait_ge(s("y_ps"), 2 * kv + ct + 1)
                    c = slice(ct * N, (ct + 1) * N)
                    v.tensor_tensor(hT[:, c], hT[:, c], flat(ps[:, 6 - 2 * ct:8 - 2 * ct, :]), ALU.add).then_inc(s("h_added"), 1)
                dve.wait_ge(s("h_added"), 2 * kv + 3)



def constants():
    k = np.zeros((P, K_COLS), np.float32)
    k[:, K_ID:K_ID + P] = np.eye(P)
    i = np.arange(P)
    for l in range(LEVELS):
        k[:, K_MASK + l * P:K_MASK + (l + 1) * P] = ((i[:, None] >> (l + 1)) == (i[None] >> (l + 1))) & ((i[:, None] >> l) % 2 == 0) & ((i[None] >> l) % 2 == 1)
    k[:, K_RANK:K_RANK + 8] = np.arange(8, 0, -1)
    later = (i[None] > i[:, None]) * -BIG
    k[:, K_CAUSAL:K_CAUSAL + P] = later
    k[:, K_CAUSAL + 2 * P:K_CAUSAL + 3 * P] = later
    t = np.arange(T, dtype=np.float32)
    hd = 16
    f = (np.float32(1.0) / np.float32(10000.0) ** (np.arange(0, hd, 2, dtype=np.float32) / np.float32(hd))).astype(np.float32)
    ang = np.tile((t[:, None] * f[None]).astype(np.float32), (1, 2)).T
    for g in range(4):
        k[32 * g:32 * g + hd, K_COS1:K_COS1 + T] = np.cos(ang)
        k[32 * g:32 * g + hd, K_SIN1:K_SIN1 + T] = np.sin(ang)
        for d in range(hd):
            src, sign = (d + 8, -1) if d < 8 else (d - 8, 1)
            k[32 * g + src, K_ROT1 + 32 * g + d] = sign
    f = (np.float32(1000000.0) ** (-np.arange(0, P, 2, dtype=np.float32) / np.float32(P))).astype(np.float32)
    ang = np.repeat((t[:, None] * f[None]).astype(np.float32), 2, axis=1).T
    k[:, K_COS2:K_COS2 + T] = np.cos(ang)
    k[:, K_SIN2:K_SIN2 + T] = np.sin(ang)
    for d in range(0, P, 2):
        k[d + 1, K_ROT2 + d] = -1
        k[d, K_ROT2 + d + 1] = 1
    return k


def rows(w):
    return w.reshape(-1, P, w.shape[-1]).transpose(1, 0, 2)


def flat_rows(w):
    return rows(w).reshape(P, -1)


def layout(inp):
    g = lambda name: np.asarray(inp[name])
    out = {}
    out["xT"] = flat_rows(g("x").reshape(N, C).T)
    out["fT"] = flat_rows(g("fside_BxSxS_0").reshape(N, C).T)
    out["emb"] = g("cond_512").reshape(-1)
    out["const"] = constants()
    vec = np.zeros((P, V_COLS), np.float32)
    for i, name in enumerate(("L0_cond", "L0_cond2", "L1_cond", "L1_cond2")):
        vec[:, V_W + 2 * i:V_W + 2 * i + 2] = g(name + "_w").reshape(CT, P).T
        vec[:, V_U + 2 * i:V_U + 2 * i + 2] = g(name + "_u").reshape(CT, P).T
    vec[:, V_NORM] = g("L0_attn_norm_w")
    vec[:, V_LN:V_LN + 2] = g("L1_ffn_ln_w").reshape(CT, P).T
    vec[:, V_FFLN:V_FFLN + 2] = g("L1_ffn_ff_ln_w").reshape(CT, P).T
    vec[:, V_GATE0:V_GATE0 + 16] = flat_rows(g("L0_ffn_gate_w").T)
    vec[:, V_GATE1:V_GATE1 + 16] = flat_rows(g("L1_ffn_gate_w"))
    out["vec"] = vec
    out["low_w"] = np.concatenate([flat_rows(g("L0_attn_" + name)) for name in ("Wf1", "Wg1", "Wb")], axis=1)
    gsa = np.zeros((GH, P, G_COLS), np.float32)
    for h in range(GH):
        c = slice(h * P, (h + 1) * P)
        for key, name in (("q", "Wq"), ("k", "Wk"), ("v", "Wv"), ("w", "Ww")):
            gsa[h, :, G_W[key]:G_W[key] + 2 * P] = flat_rows(g("L0_attn_" + name)[:, c])
        gsa[h, :, G_W["f"]:G_W["f"] + P] = g("L0_attn_Wf2")[:, c]
        gsa[h, :, G_W["g"]:G_W["g"] + P] = g("L0_attn_Wg2")[:, c]
        gsa[h, :, G_W["o"]:G_W["o"] + C] = g("L0_attn_Wo")[c]
        for j, name in enumerate(("cq", "ck", "cv")):
            gsa[h, :, G_W["conv"] + 4 * j:G_W["conv"] + 4 * j + 4] = g("L0_attn_" + name)[c]
        gsa[h, :, G_W["bg"]] = g("L0_attn_bg2")[c]
    out["gsa"] = gsa
    layout_rest(g, out)
    return out

def layout_rest(g, out):
    kv = np.zeros((P, 4 * P), np.float32)
    for kt in range(CT):
        for h in range(4):
            c = kt * P + 32 * h
            kv[:, c:c + 16] = g("L1_attn_wk")[kt * P:(kt + 1) * P, 16 * h:16 * h + 16]
            kv[:, 2 * P + c:2 * P + c + 16] = g("L1_attn_wv")[kt * P:(kt + 1) * P, 16 * h:16 * h + 16]
    out["att1_kv"] = kv
    att1 = np.zeros((4, P, 2 * P + C), np.float32)
    for t in range(4):
        for u in range(4):
            h = 4 * u + t
            for kt in range(CT):
                att1[t, :, kt * P + 32 * u:kt * P + 32 * u + 16] = g("L1_attn_wq")[kt * P:(kt + 1) * P, 16 * h:16 * h + 16]
            att1[t, 32 * u:32 * u + 16, 2 * P:] = g("L1_attn_wo")[16 * h:16 * h + 16]
    out["att1"] = att1
    att2 = []
    for kv in range(4):
        c = slice(kv * P, (kv + 1) * P)
        heads = [slice(h * P, (h + 1) * P) for h in range(4 * kv, 4 * kv + 4)]
        att2.append(np.concatenate([flat_rows(g("L1_ffn_wk")[:, c]), flat_rows(g("L1_ffn_wv")[:, c])]
                                   + [flat_rows(g("L1_ffn_wq")[:, h]) for h in heads]
                                   + [g("L1_ffn_wo")[h] for h in heads], axis=1))
    out["att2"] = np.stack(att2)
    tiles = lambda w: [slice(i, i + P) for i in range(0, w.shape[1], P)]
    chunk = lambda w1, w3, w2, t: np.concatenate([flat_rows(w1[:, t]), flat_rows(w3[:, t]), w2[t]], axis=1)
    out["moe0"] = np.stack([chunk(w1.T, w3.T, w2.T, t) for w1, w3, w2 in zip(g("L0_ffn_w1"), g("L0_ffn_w3"), g("L0_ffn_w2"))
                            for t in tiles(w1.T)])
    out["moe1"] = np.stack([chunk(w1, w3, w2, t) for w1, w3, w2 in zip(g("L1_ffn_w1"), g("L1_ffn_w3"), g("L1_ffn_w2"))
                            for t in tiles(w1)])



def kernel(**inputs):
    import concourse.bacc as bacc
    from concourse.bass_utils import run_bass_kernel_spmd

    nc = bacc.Bacc("TRN2", target_bir_lowering=False, num_devices=1)
    arrays = {f"in_{n}": np.ascontiguousarray(v) for n, v in layout(inputs).items()}
    args = {n[3:]: nc.dram_tensor(n, v.shape, mybir.dt.from_np(v.dtype), kind="ExternalInput").ap() for n, v in arrays.items()}
    args["out"] = nc.dram_tensor("out", (N, C), F32, kind="ExternalOutput").ap()
    build(nc, args)
    r = run_bass_kernel_spmd(nc, [arrays], core_ids=[0])
    return r.results[0]["out"].reshape(B, T, C)
```
